# Optimizing a Trainium2 kernel written in Bass

```python
import numpy as np
import jax
import jax.numpy as jnp

def _softmax(x, axis=-1):
    return jax.nn.softmax(x, axis=axis)

def _gelu(x):
    return jax.nn.gelu(x, approximate=True)

def _silu(x):
    return jax.nn.silu(x)

def _sigmoid(x):
    return jax.nn.sigmoid(x)

def _layernorm(x, axis=-1, eps=1e-05):
    m = jnp.mean(x, axis=axis, keepdims=True)
    v = jnp.var(x, axis=axis, keepdims=True)
    return (x - m) / jnp.sqrt(v + eps)

def _scatter_add(tgt, idx, src, axis=0):
    return tgt.at[idx].add(src)

def _segment_sum(src, seg, n):
    return jax.ops.segment_sum(src, seg, n)
kernel_name = 'mk_decoder_postln_d1_seqx_r4_fc492c'

def setup_inputs(seed: int=0):
    np.random.seed(seed)
    _w = jnp.asarray

    def _rec_inputs():
        import jax
        import jax.numpy as jnp
        _rk = jax.random.key(seed)
        x = -0.0002928 + 1 * jax.random.normal(jax.random.fold_in(_rk, 1), (1, 2048, 256), jnp.float32)
        _lenS = 2048 - jax.random.randint(jax.random.fold_in(_rk, 7), (1,), 0, max(1, 2048 // 4) + 1, jnp.int32)
        _lenS2 = 1601 - jax.random.randint(jax.random.fold_in(_rk, 8), (1,), 0, max(1, 1601 // 4) + 1, jnp.int32)
        _ctx_1024P = jax.random.normal(jax.random.fold_in(_rk, 11), (1, 16, 256), jnp.float32)
        _ctx_1024c = jax.random.dirichlet(jax.random.fold_in(_rk, 511), 0.3 * jnp.ones((16,), jnp.float32), (1, 1601))
        _ctx_1024t = jnp.einsum('bsk,bkd->bsd', _ctx_1024c, _ctx_1024P)
        _ctx_1024t = _ctx_1024t * jax.lax.rsqrt(jnp.mean(jnp.square(_ctx_1024t)) + 1e-12) * 0.953939
        ctx_1024 = -1.39393e-06 + 0.999914 * (_ctx_1024t + 0.3 * jax.random.normal(jax.random.fold_in(_rk, 611), (1, 1601, 256), jnp.float32))
        _validS = jnp.arange(2048)[None, :] < _lenS[:, None]
        _validS2 = jnp.arange(1601)[None, :] < _lenS2[:, None]
        _causal = jnp.tril(jnp.ones((2048, 2048), dtype=bool))
        mask_BxS2_if1 = jnp.where(jnp.ones((1, 1601), dtype=bool), 1, 0).astype(jnp.int32)
        return (x, ctx_1024, mask_BxS2_if1)
    x, ctx_1024, mask_BxS2_if1 = _rec_inputs()

    def _L0_attn_setup():
        import jax, jax.numpy as jnp
        import numpy as np
        BASE_THETA = 0.5
        K_DOP = 0.2
        K_NOR = 0.15
        K_SERO = 0.1
        DIM = 256
        key = jax.random.key(seed)
        ks = jax.random.split(key, 9)
        scale = 1.0 / np.sqrt(DIM)
        x = jax.random.normal(ks[0], (2, 512, DIM), dtype=jnp.float32)
        Wq = jax.random.normal(ks[1], (DIM, DIM), dtype=jnp.float32) * scale
        bq = jnp.zeros((DIM,), dtype=jnp.float32)
        Wk = jax.random.normal(ks[2], (DIM, DIM), dtype=jnp.float32) * scale
        bk = jnp.zeros((DIM,), dtype=jnp.float32)
        Wv = jax.random.normal(ks[3], (DIM, DIM), dtype=jnp.float32) * scale
        bv = jnp.zeros((DIM,), dtype=jnp.float32)
        Wo = jax.random.normal(ks[4], (DIM, DIM), dtype=jnp.float32) * scale
        bo = jnp.zeros((DIM,), dtype=jnp.float32)
        return {'x': x, 'Wq': Wq, 'bq': bq, 'Wk': Wk, 'bk': bk, 'Wv': Wv, 'bv': bv, 'Wo': Wo, 'bo': bo}
    _L0_attn_all = _L0_attn_setup()
    _L0_attn_in = {k: v for k, v in _L0_attn_all.items() if k in ('Wq', 'bq', 'Wk', 'bk', 'Wv', 'bv', 'Wo', 'bo')}
    del _L0_attn_all

    def _L0_xattn_setup():
        import jax, jax.numpy as jnp
        import numpy as np
        D_MODEL = 256
        NUM_HEADS = 16
        D_K = D_MODEL // NUM_HEADS
        NEG_INF = -1000000000.0
        key = jax.random.key(seed)
        ks = jax.random.split(key, 12)
        B, S = (2, 512)
        scale = 1.0 / np.sqrt(D_MODEL)
        inp = {'q': jax.random.normal(ks[0], (B, S, D_MODEL), jnp.float32), 'k': jax.random.normal(ks[1], (B, S, D_MODEL), jnp.float32), 'v': jax.random.normal(ks[2], (B, S, D_MODEL), jnp.float32), 'mask': jnp.ones((B, S), jnp.int32), 'W_q': jax.random.normal(ks[3], (D_MODEL, D_MODEL), jnp.float32) * scale, 'b_q': jnp.zeros((D_MODEL,), jnp.float32), 'W_k': jax.random.normal(ks[4], (D_MODEL, D_MODEL), jnp.float32) * scale, 'b_k': jnp.zeros((D_MODEL,), jnp.float32), 'W_v': jax.random.normal(ks[5], (D_MODEL, D_MODEL), jnp.float32) * scale, 'b_v': jnp.zeros((D_MODEL,), jnp.float32), 'W_o': jax.random.normal(ks[6], (D_MODEL, D_MODEL), jnp.float32) * scale, 'b_o': jnp.zeros((D_MODEL,), jnp.float32)}
        return inp
    _L0_xattn_all = _L0_xattn_setup()
    _L0_xattn_in = {k: v for k, v in _L0_xattn_all.items() if k in ('W_q', 'b_q', 'W_k', 'b_k', 'W_v', 'b_v', 'W_o', 'b_o')}
    del _L0_xattn_all

    def _L0_ffn_setup():
        import jax, jax.numpy as jnp
        import numpy as np
        E = 16
        F_C = 2.0
        D = 256
        I = 4 * D
        IS = 2 * D
        B, S = (4, 256)
        key = jax.random.key(seed)
        ks = jax.random.split(key, 8)
        w = 0.02
        return {'hidden_states': jax.random.normal(ks[0], (B, S, D), dtype=jnp.float32), 'gate_w': jax.random.normal(ks[1], (E, D), dtype=jnp.float32) * w, 'Wg': jax.random.normal(ks[2], (E, I, D), dtype=jnp.float32) * w, 'Wu': jax.random.normal(ks[3], (E, I, D), dtype=jnp.float32) * w, 'Wd': jax.random.normal(ks[4], (E, D, I), dtype=jnp.float32) * w, 'Sg': jax.random.normal(ks[5], (IS, D), dtype=jnp.float32) * w, 'Su': jax.random.normal(ks[6], (IS, D), dtype=jnp.float32) * w, 'Sd': jax.random.normal(ks[7], (D, IS), dtype=jnp.float32) * w}
    _L0_ffn_all = _L0_ffn_setup()
    _L0_ffn_in = {k: v for k, v in _L0_ffn_all.items() if k in ('gate_w', 'Wg', 'Wu', 'Wd', 'Sg', 'Su', 'Sd')}
    del _L0_ffn_all
    return {'x': x, 'ctx_1024': ctx_1024, 'mask_BxS2_if1': mask_BxS2_if1, 'L0_attn_Wq': _L0_attn_in['Wq'], 'L0_attn_bq': _L0_attn_in['bq'], 'L0_attn_Wk': _L0_attn_in['Wk'], 'L0_attn_bk': _L0_attn_in['bk'], 'L0_attn_Wv': _L0_attn_in['Wv'], 'L0_attn_bv': _L0_attn_in['bv'], 'L0_attn_Wo': _L0_attn_in['Wo'], 'L0_attn_bo': _L0_attn_in['bo'], 'L0_xattn_W_q': _L0_xattn_in['W_q'], 'L0_xattn_b_q': _L0_xattn_in['b_q'], 'L0_xattn_W_k': _L0_xattn_in['W_k'], 'L0_xattn_b_k': _L0_xattn_in['b_k'], 'L0_xattn_W_v': _L0_xattn_in['W_v'], 'L0_xattn_b_v': _L0_xattn_in['b_v'], 'L0_xattn_W_o': _L0_xattn_in['W_o'], 'L0_xattn_b_o': _L0_xattn_in['b_o'], 'L0_ffn_gate_w': _L0_ffn_in['gate_w'], 'L0_ffn_Wg': _L0_ffn_in['Wg'], 'L0_ffn_Wu': _L0_ffn_in['Wu'], 'L0_ffn_Wd': _L0_ffn_in['Wd'], 'L0_ffn_Sg': _L0_ffn_in['Sg'], 'L0_ffn_Su': _L0_ffn_in['Su'], 'L0_ffn_Sd': _L0_ffn_in['Sd']}

def reference(x, ctx_1024, mask_BxS2_if1, L0_attn_Wq, L0_attn_bq, L0_attn_Wk, L0_attn_bk, L0_attn_Wv, L0_attn_bv, L0_attn_Wo, L0_attn_bo, L0_xattn_W_q, L0_xattn_b_q, L0_xattn_W_k, L0_xattn_b_k, L0_xattn_W_v, L0_xattn_b_v, L0_xattn_W_o, L0_xattn_b_o, L0_ffn_gate_w, L0_ffn_Wg, L0_ffn_Wu, L0_ffn_Wd, L0_ffn_Sg, L0_ffn_Su, L0_ffn_Sd):
    import jax
    import jax.numpy as jnp

    def _L0_attn_ref(x, Wq, bq, Wk, bk, Wv, bv, Wo, bo):
        import jax, jax.numpy as jnp
        import numpy as np
        BASE_THETA = 0.5
        K_DOP = 0.2
        K_NOR = 0.15
        K_SERO = 0.1
        DIM = 256
        q = jnp.einsum('bsd,ed->bse', x, Wq) + bq
        k = jnp.einsum('bsd,ed->bse', x, Wk) + bk
        v = jnp.einsum('bsd,ed->bse', x, Wv) + bv
        qk = jnp.einsum('bsd,btd->bst', q, k)
        theta = BASE_THETA + K_DOP * jax.nn.sigmoid(qk) + K_NOR * jnp.tanh(qk) + K_SERO * jax.nn.relu(qk)
        attn = jax.nn.softmax(theta, axis=-1)
        out = jnp.einsum('bst,btd->bsd', attn, v)
        return jnp.einsum('bsd,ed->bse', out, Wo) + bo

    def _L0_xattn_ref(q, k, v, mask, W_q, b_q, W_k, b_k, W_v, b_v, W_o, b_o):
        import jax, jax.numpy as jnp
        import numpy as np
        D_MODEL = 256
        NUM_HEADS = 16
        D_K = D_MODEL // NUM_HEADS
        NEG_INF = -1000000000.0
        B, S, _ = q.shape

        def proj(x, W, b):
            y = x @ W.T + b
            return y.reshape(B, -1, NUM_HEADS, D_K).transpose(0, 2, 1, 3)
        qh = proj(q, W_q, b_q)
        kh = proj(k, W_k, b_k)
        vh = proj(v, W_v, b_v)
        scores = jnp.einsum('bhqd,bhkd->bhqk', qh, kh) / jnp.sqrt(jnp.float32(D_K))
        m = mask[:, None, None, :]
        scores = jnp.where(m == 0, jnp.float32(NEG_INF), scores)
        attn = jax.nn.softmax(scores, axis=-1)
        context = jnp.einsum('bhqk,bhkd->bhqd', attn, vh)
        context = context.transpose(0, 2, 1, 3).reshape(B, S, D_MODEL)
        return context @ W_o.T + b_o

    def _L0_ffn_ref(hidden_states, gate_w, Wg, Wu, Wd, Sg, Su, Sd):
        import jax, jax.numpy as jnp
        import numpy as np
        E = 16
        F_C = 2.0
        D = 256
        I = 4 * D
        IS = 2 * D
        B, S = (4, 256)
        b, s, d = hidden_states.shape
        T = b * s
        C = int(T * F_C / E)
        flat_x = hidden_states.reshape(T, d)
        logits = flat_x @ gate_w.T
        scores = jax.nn.softmax(logits, axis=-1).T
        topk_weight, topk_idx = jax.lax.top_k(scores, C)
        xg = flat_x[topk_idx]
        g = jnp.einsum('ecd,eid->eci', xg, Wg)
        u = jnp.einsum('ecd,eid->eci', xg, Wu)
        h = jax.nn.gelu(g, approximate=False) * u
        eo = jnp.einsum('eci,edi->ecd', h, Wd)
        eo = eo * topk_weight[..., None]
        flat_out = jnp.zeros_like(flat_x).at[topk_idx.reshape(-1)].add(eo.reshape(-1, d))
        out = flat_out.reshape(b, s, d)
        sg = hidden_states @ Sg.T
        su = hidden_states @ Su.T
        shared = jax.nn.gelu(sg, approximate=False) * su @ Sd.T
        return out + shared
    x = _layernorm(x + _L0_attn_ref(x, L0_attn_Wq, L0_attn_bq, L0_attn_Wk, L0_attn_bk, L0_attn_Wv, L0_attn_bv, L0_attn_Wo, L0_attn_bo), axis=-1)
    x = _layernorm(x + _L0_xattn_ref(x, ctx_1024, ctx_1024, mask_BxS2_if1, L0_xattn_W_q, L0_xattn_b_q, L0_xattn_W_k, L0_xattn_b_k, L0_xattn_W_v, L0_xattn_b_v, L0_xattn_W_o, L0_xattn_b_o), axis=-1)
    x = _layernorm(x + _L0_ffn_ref(x, L0_ffn_gate_w, L0_ffn_Wg, L0_ffn_Wu, L0_ffn_Wd, L0_ffn_Sg, L0_ffn_Su, L0_ffn_Sd), axis=-1)
    return x

_drawn_inputs = setup_inputs


def setup_inputs(seed=0):
    import zlib

    import numpy as np

    out = dict(_drawn_inputs(seed))
    spreads = {'L0_attn_bq': (0.0, 0.556),
     'L0_attn_bk': (0.0, 0.8),
     'L0_attn_bv': (0.0, 0.1),
     'L0_attn_bo': (0.0, 0.1),
     'L0_xattn_b_q': (0.0, 0.482),
     'L0_xattn_b_k': (0.0, 2.0),
     'L0_xattn_b_v': (0.0, 0.1),
     'L0_xattn_b_o': (0.0, 0.1)}
    factors = {'L0_ffn_gate_w': 8.0,
     'L0_ffn_Wg': 8.0,
     'L0_ffn_Wu': 8.0,
     'L0_ffn_Wd': 8.0,
     'L0_ffn_Sg': 8.0,
     'L0_ffn_Su': 8.0,
     'L0_ffn_Sd': 8.0}
    for name, (base, spread) in spreads.items():
        noise = np.random.default_rng([zlib.crc32(name.encode()), seed]).standard_normal(out[name].shape)
        drawn = base * np.exp(spread * noise) if base else spread * noise
        out[name] = jnp.asarray(drawn.astype(out[name].dtype))
    for name, factor in factors.items():
        out[name] = (out[name] * factor).astype(out[name].dtype)
    return out
```

```python
from contextlib import ExitStack

import concourse.bass as bass
from concourse import mybir

F32 = mybir.dt.float32
BF16 = mybir.dt.bfloat16
I32 = mybir.dt.int32
U32 = mybir.dt.uint32
ACT = mybir.ActivationFunctionType
ALU = mybir.AluOpType
AX = mybir.AxisListType
ds = bass.ds

P = 128
T = 2048
D = 256
KD = D // P
NT = T // P
S2 = 1601
H = 16
HD = D // H
NKT = -(-S2 // P)
LASTK = S2 - (NKT - 1) * P
E = 16
CAP = T * 2 // E
CT = CAP // P
FI = 1024
FT = FI // P
FS = 512
ST = FS // P
EPS = 1e-5
BLK = 512
NB = T // BLK
QT = BLK // P
G = 4
NG = H // G
VW = 32
NEG = 1.0e9

Q_PARTS = (0, 0, 1, 1, 0, 2)
K_PARTS = (0, 1, 0, 1, 2, 0)
R_MASK = HD * len(Q_PARTS)
R_MAX = R_MASK + 3
R_ALL = R_MAX + 3


class Shared:
    pass


def chain(engine, sem, before=0):
    done = [0]

    def link(ins):
        done[0] += 1
        ins.then_inc(sem, 1)
        engine.wait_ge(sem, before + done[0])

    link.done = done
    return link


def identity(nc, pool, tile, sem, before):
    pool.memset(tile[:, :], 0.0).then_inc(sem, 1)
    pool.wait_ge(sem, before + 1)
    pool.affine_select(out=tile[:, :], in_=tile[:, :], compare_op=ALU.not_equal, fill=1.0, base=0,
                       pattern=[[-1, P]], channel_multiplier=1).then_inc(sem, 1)


def project_inputs(nc, s):
    with ExitStack() as ctx:
        def sb(name, shape, dt=F32):
            return ctx.enter_context(nc.sbuf_tensor(name, shape, dt))

        def sem(name):
            return ctx.enter_context(nc.semaphore(name))

        xT = sb("xT", [P, KD, T])
        ctxT = sb("ctxT", [P, KD, S2])
        w = {n: sb(f"w_{n}", [P, KD, D]) for n in ("q", "k", "v", "ck", "cv")}
        b_col = {n: sb(f"bcol_{n}", [P, KD]) for n in ("q", "k", "ck")}
        b_row = {n: sb(f"brow_{n}", [P, D]) for n in ("v", "cv", "o")}
        mask_i = sb("mask_i", [P, S2], I32)
        keep_key = sb("keep_key", [P, S2])
        ck = sb("ck", [P, S2])
        space = s.k_stack_space

        def scratch(at, words):
            return space[:, 2 * at:2 * (at + words)]

        W3 = (3 * S2 + 1) // 2
        part = scratch(0, W3)[:, 0:3 * S2].rearrange("p (c n) -> p c n", c=3)
        mask_part = scratch(W3, 2 * W3)[0:1, 0:6 * S2].rearrange("p (c n) -> p c n", c=6)
        rest = scratch(3 * W3, S2).bitcast(F32)
        mask_bias = scratch(3 * W3 + S2, S2).bitcast(F32)[0:1, :]
        pj = [ctx.enter_context(nc.psum_tensor(f"pj{i}", [P, BLK], F32)) for i in range(4)]

        loaded = {n: sem(f"loaded_{n}") for n in ("x", "ctx", "wq", "wk", "wv", "wck", "wcv", "b", "mask", "xn")}
        ready = sem("product_ready")
        taken = sem("product_taken")
        ck_ready = sem("ck_ready")
        parts_ready = sem("parts_ready")
        parts_out = sem("parts_out")
        mask_ready = sem("mask_ready")
        mask_out = sem("mask_out")
        ones_set = sem("ones_set")
        dve_step = sem("dve_step")
        block = ctx.enter_context(nc.Block())

        keys = [(a, min(BLK, S2 - a)) for a in range(0, S2, BLK)]
        groups = [("ck", h, a, n) for h in range(KD) for a, n in keys]
        groups += [("cv", j, j * P, D) for j in range(NKT)]
        groups += [(n, h, a * BLK, BLK) for n in ("q", "k") for h in range(KD) for a in range(NB)]
        groups += [("v", j, j * P, D) for j in range(NT)]

        @block.sync
        def _(sp):
            sp.dma_start(w["ck"][:, :, :], s.w_ck).then_inc(loaded["wck"], 16)
            sp.dma_start(ctxT[:, :, :], s.ctxT).then_inc(loaded["ctx"], 16)
            for n in ("q", "k", "ck"):
                sp.dma_start(b_col[n][:, :], s.b[n]).then_inc(loaded["b"], 16)
            for n in ("v", "cv", "o"):
                sp.dma_start(b_row[n][:, :], s.b[n].partition_broadcast(P)).then_inc(loaded["b"], 16)
            sp.dma_start(mask_i[:, :], s.mask.partition_broadcast(P)).then_inc(loaded["mask"], 16)
            sp.dma_start(w["cv"][:, :, :], s.w_cv).then_inc(loaded["wcv"], 16)
            sp.dma_start(w["q"][:, :, :], s.w_q).then_inc(loaded["wq"], 16)
            sp.dma_start(xT[:, :, :], s.xT).then_inc(loaded["x"], 16)
            sp.dma_start(w["k"][:, :, :], s.w_k).then_inc(loaded["wk"], 16)
            sp.dma_start(w["v"][:, :, :], s.w_v).then_inc(loaded["wv"], 16)
            sp.dma_start(s.act[:, :, :], s.x).then_inc(loaded["xn"], 16)
            sp.dma_start(s.wo[:, :, :], s.w_o).then_inc(loaded["xn"], 16)
            sp.wait_ge(mask_ready, 1)
            sp.wait_ge(ones_set, 3)
            sp.dma_start(s.mask_parts, mask_part[:, :, :]).then_inc(mask_out, 16)
            for h in range(KD):
                sp.wait_ge(parts_ready, h + 1)
                sp.dma_start(s.k_parts[:, h * P:(h + 1) * P, :].rearrange("c p n -> p c n"),
                             part[:, :, :]).then_inc(parts_out, 16)
            sp.wait_ge(parts_out, 16 * KD)
            sp.wait_ge(mask_out, 16)

        @block.gpsimd
        def _(pool):
            identity(nc, pool, s.ident, s.consts, 0)
            identity(nc, pool, s.ident_b, s.consts, 2)
            pool.memset(s.cv[:, :, :, HD:HD + 1], 1.0).then_inc(ones_set, 1)
            pool.memset(s.cv[:, :, :, HD + 1:VW], 0.0).then_inc(ones_set, 1)
            pool.memset(mask_part[:, 3:6, :], 1.0).then_inc(ones_set, 1)
            pool.wait_ge(ones_set, 3)

        @block.tensor
        def _(pe):
            seen = set()
            for n, (kind, i, a, cols) in enumerate(groups):
                for need in {"ck": ("wck", "ctx"), "cv": ("wcv",), "q": ("wq", "x"), "k": ("wk",), "v": ("wv",)}[kind]:
                    if need not in seen:
                        pe.wait_ge(loaded[need], 16)
                        seen.add(need)
                if n >= 4:
                    pe.wait_ge(taken, n - 3)
                src = ctxT if kind in ("ck", "cv") else xT
                for k in range(KD):
                    if kind in ("cv", "v"):
                        rows = min(P, src.shape[2] - a)
                        out, lhsT, rhs = pj[n % 4][0:rows, 0:D], src[:, k, a:a + rows], w[kind][:, k, :]
                    else:
                        out, lhsT, rhs = pj[n % 4][:, 0:cols], w[kind][:, k, i * P:(i + 1) * P], src[:, k, a:a + cols]
                    mm = pe.matmul(out, lhsT, rhs, start=(k == 0), stop=(k == KD - 1))
                mm.then_inc(ready, 1)

        @block.scalar
        def _(act):
            act.wait_ge(loaded["b"], 16 * 6)
            for n, (kind, i, a, cols) in enumerate(groups):
                if kind not in ("ck", "q", "k"):
                    continue
                act.wait_ge(ready, n + 1)
                if n:
                    act.wait_ge(taken, n)
                if kind == "ck":
                    if i and a == 0:
                        act.wait_ge(parts_ready, i)
                    out = ck[:, a:a + cols]
                else:
                    out = (s.qT if kind == "q" else s.kT)[:, i, a:a + cols]
                act.activation(out, pj[n % 4][:, 0:cols], ACT.Identity,
                               bias=b_col[kind][:, i:i + 1]).then_inc(taken, 1)

        @block.vector
        def _(dve):
            link = chain(dve, dve_step)
            dve.wait_ge(loaded["mask"], 16)
            link(dve.tensor_scalar(keep_key[:, :], mask_i[:, :], 0.0, None, ALU.not_equal))
            link(dve.tensor_scalar(mask_bias[:, :], keep_key[0:1, :], 1.0, NEG, ALU.subtract, ALU.mult))
            for c in range(3):
                link(dve.tensor_copy(mask_part[:, c, :], mask_bias[:, :]))
                if c < 2:
                    link(dve.tensor_tensor(mask_bias[:, :], mask_bias[:, :], mask_part[:, c, :], ALU.subtract))
            dve.engine_nop().then_inc(mask_ready, 1)
            dve.wait_ge(loaded["b"], 16 * 6)
            n_keys = len(keys)
            for h in range(KD):
                dve.wait_ge(taken, (h + 1) * n_keys)
                if h:
                    dve.wait_ge(parts_out, 16 * h)
                link(dve.tensor_tensor(ck[:, :], ck[:, :], keep_key[:, :], ALU.mult))
                link(dve.tensor_copy(part[:, 0, :], ck[:, :]))
                link(dve.tensor_tensor(rest[:, :], ck[:, :], part[:, 0, :], ALU.subtract))
                link(dve.tensor_copy(part[:, 1, :], rest[:, :]))
                dve.tensor_tensor(part[:, 2, :], rest[:, :], part[:, 1, :], ALU.subtract).then_inc(parts_ready, 1)
            for n, (kind, i, a, cols) in enumerate(groups):
                if kind not in ("cv", "v"):
                    continue
                dve.wait_ge(ready, n + 1)
                dve.wait_ge(taken, n)
                rows = min(P, (S2 if kind == "cv" else T) - a)
                if kind == "cv":
                    out = s.cv[0:rows, i, :, 0:HD]
                    dve.tensor_tensor(out, pj[n % 4][0:rows, 0:D].rearrange("p (h d) -> p h d", h=H),
                                      b_row["cv"][0:rows, :].rearrange("p (h d) -> p h d", h=H), ALU.add).then_inc(taken, 1)
                else:
                    dve.tensor_tensor(s.v[:, i, :], pj[n % 4][:, 0:D], b_row["v"][:, :], ALU.add).then_inc(taken, 1)
            dve.wait_ge(loaded["xn"], 32)
            dve.tensor_tensor(s.act[:, :, :], s.act[:, :, :],
                              b_row["o"][:, :].unsqueeze(1).broadcast_to([P, NT, D]), ALU.add)


def row(tile, t):
    return tile[:, ds(t, 1), :].rearrange("p o d -> p (o d)")


def norm_scale(dve, link, var, scratch, root_ready, var_ready, out):
    a, b = scratch
    link(dve.tensor_scalar(a, var, EPS, None, ALU.add))
    dve.engine_nop().then_inc(var_ready, 1)
    dve.wait_ge(root_ready, 1)
    link(dve.reciprocal(out, b))
    link(dve.tensor_tensor(b, out, out, ALU.mult))
    link(dve.tensor_tensor(b, b, a, ALU.mult))
    link(dve.tensor_scalar(b, b, -0.5, 1.5, ALU.mult, ALU.add))
    link(dve.tensor_tensor(out, out, b, ALU.mult))


def self_attention(nc, s):
    with ExitStack() as ctx:
        def sb(name, shape, dt=F32):
            return ctx.enter_context(nc.sbuf_tensor(name, shape, dt))

        def ps(name, shape, dt=F32):
            return ctx.enter_context(nc.psum_tensor(name, shape, dt))

        def sem(name):
            return ctx.enter_context(nc.semaphore(name))

        HALF = T // 2
        q_tile = sb("q_tile", [P, KD, P])
        th_half = sb("th_half", [P, T])
        th_full = sb("th_full", [P, T])
        w = sb("w", [P, T])
        probs = sb("probs", [P, T])
        probsT = sb("probsT", [P, NT, P])
        oT = sb("oT", [P, KD, P])
        neg_max = sb("neg_max", [P, 1])
        shift = sb("shift", [P, 1])
        row_sums = sb("row_sums", [P, NT])
        r_sum = sb("r_sum", [P, 1])
        stats = sb("stats", [P, 6])
        z = sb("z", [P, D])
        all_stats = sb("all_stats", [P, NT, 6])
        mvs = sb("mvs", [P, NT, 2])
        nrm = sb("nrm", [P, 3, NT])
        scores = ps("scores", [P, T])
        turned = [ps(f"turned{i}", [P, 4, P]) for i in range(2)]
        out_T = ps("out_T", [P, KD, P])
        y = ps("y", [P, D])

        q_ready = sem("q_ready")
        scores_ready = sem("scores_ready")
        th_ready = sem("th_ready")
        scores_free = sem("scores_free")
        shift_ready = sem("shift_ready")
        probs_ready = sem("probs_ready")
        turned_ready = sem("turned_ready")
        probsT_ready = sem("probsT_ready")
        outT_ready = sem("outT_ready")
        oT_ready = sem("oT_ready")
        y_ready = sem("y_ready")
        z_ready = sem("z_ready")
        w_step = sem("w_step")
        z_step = sem("z_step")
        n_step = sem("n_step")
        var_ready = sem("var_ready")
        root_ready = sem("root_ready")
        x1_ready = sem("x1_ready")
        x1T_ready = sem("x1T_ready")
        x1T_taken = sem("x1T_taken")
        k_stacked = sem("k_stacked")
        block = ctx.enter_context(nc.Block())

        @block.sync
        def _(sp):
            for j, c in enumerate(K_PARTS):
                sp.dma_start(s.k_stack[HD * j:HD * (j + 1), :, :],
                             s.k_parts[c].rearrange("(h d) n -> d h n", h=H)).then_inc(k_stacked, 16)
            for h in range(H):
                sp.dma_start(s.k_stack[R_MASK:R_ALL, h, :], s.mask_parts[0]).then_inc(k_stacked, 16)
            sp.wait_ge(k_stacked, 16 * (len(K_PARTS) + H))

        @block.gpsimd
        def _(pool):
            with pool.Fori(0, NT) as t:
                pool.wait_ge(scores_free, 2 * t + 2)
                pool.tensor_copy(q_tile[:, :, :], s.qT[:, :, ds(t * P, P)]).then_inc(q_ready, 1)

        @block.tensor
        def _(pe):
            def score_tile(t):
                pe.wait_ge(q_ready, t + 1)
                for c in range(2):
                    pe.wait_ge(scores_free, 2 * t + c + 1)
                    for b in range(2):
                        cols = slice(c * HALF + b * BLK, c * HALF + (b + 1) * BLK)
                        for k in range(KD):
                            mm = pe.matmul(scores[:, cols], q_tile[:, k, :], s.kT[:, k, cols],
                                           start=(k == 0), stop=(k == KD - 1))
                    mm.then_inc(scores_ready, 1)

            def value_tile(t):
                pe.wait_ge(probs_ready, t + 1)

                def products(g, half):
                    for j in range(4 * g, 4 * g + 4):
                        mm = pe.matmul(out_T[:, half, :], s.v[:, j, half * P:(half + 1) * P], probsT[:, j, :],
                                       start=(j == 0), stop=(j == NT - 1))
                    return mm

                for g in range(4):
                    pe.wait_ge(probsT_ready, 4 * t + g + 1)
                    for j in range(4):
                        c = 4 * g + j
                        mm = pe.transpose(turned[g % 2][:, j, :], probs[:, c * P:(c + 1) * P], s.ident[:, :])
                    mm.then_inc(turned_ready, 1)
                    if g == 1:
                        pe.wait_ge(oT_ready, t + 1)
                    if g >= 1:
                        pe.wait_ge(probsT_ready, 4 * t + g + 2)
                        products(g - 1, 0)
                pe.wait_ge(probsT_ready, 4 * t + 6)
                products(3, 0)
                for g in range(4):
                    mm = products(g, 1)
                mm.then_inc(outT_ready, 1)

            def project_tile(t):
                pe.wait_ge(oT_ready, t + 2)
                pe.wait_ge(z_ready, t + 1)
                for k in range(KD):
                    mm = pe.matmul(y[:, :], oT[:, k, :], s.wo[:, k, :], start=(k == 0), stop=(k == KD - 1))
                mm.then_inc(y_ready, 1)

            score_tile(0)
            score_tile(1)
            value_tile(0)
            with pe.Fori(2, NT) as t:
                score_tile(t)
                project_tile(t - 2)
                value_tile(t - 1)
            project_tile(NT - 2)
            value_tile(NT - 1)
            project_tile(NT - 1)

            transpose_tiles(pe, s.act, s.ident, turned, x1_ready, x1T_ready, x1T_taken)

        @block.scalar
        def _(act):
            act.sem_inc(probsT_ready, 2)
            act.sem_inc(oT_ready, 1)

            def tanhs(t):
                for c in range(2):
                    cols = slice(c * HALF, (c + 1) * HALF)
                    act.wait_ge(scores_ready, 2 * t + c + 1)
                    act.wait_ge(scores_free, 2 * t + c + 1)
                    act.activation(th_half[:, cols], scores[:, cols], ACT.Tanh, scale=0.5)
                    act.activation(th_full[:, cols], scores[:, cols], ACT.Tanh).then_inc(th_ready, 1)

            def exps(t, sums):
                act.wait_ge(shift_ready, t + 1)
                act.activation(probs[:, :], w[:, :], ACT.Exp, bias=shift[:, :], scale=0.1,
                               accum_out=sums).then_inc(probs_ready, 1)

            def evacuate(t):
                for g in range(4):
                    act.wait_ge(turned_ready, 4 * t + g + 1)
                    act.copy(probsT[:, 4 * g:4 * g + 4, :], turned[g % 2][:, :, :]).then_inc(probsT_ready, 1)
                act.wait_ge(outT_ready, t + 1)
                act.copy(oT[:, :, :], out_T[:, :, :]).then_inc(oT_ready, 1)

            tanhs(0)
            exps(0, row_sums[:, 0:1])
            with act.Fori(1, NT) as t:
                tanhs(t)
                evacuate(t - 1)
                exps(t, row_sums[:, ds(t, 1)])
            evacuate(NT - 1)

            act.wait_ge(var_ready, 1)
            act.activation(nrm[:, 1, :], nrm[:, 0, :], ACT.Sqrt).then_inc(root_ready, 1)
            take_tiles(act, s.actT, turned, x1T_ready, x1T_taken)

        @block.vector
        def _(dve):
            dve.sem_inc(scores_free, 2)
            dve.sem_inc(z_ready, 1)

            def w_tile(t, first=False):
                link = chain(dve, w_step, 3 * t)
                if not first:
                    dve.wait_ge(probs_ready, t)
                for c in range(2):
                    cols = slice(c * HALF, (c + 1) * HALF)
                    dve.wait_ge(th_ready, 2 * t + c + 1)
                    link(dve.scalar_tensor_tensor(out=th_half[:, cols], in0=th_full[:, cols], scalar=1.5,
                                                  in1=th_half[:, cols], op0=ALU.mult, op1=ALU.add))
                    dve.scalar_tensor_tensor(out=w[:, cols], in0=scores[:, cols], scalar=0.0,
                                             in1=th_half[:, cols], op0=ALU.max, op1=ALU.add).then_inc(scores_free, 1)
                dve.wait_ge(scores_free, 2 * t + 4)
                link(dve.tensor_reduce(neg_max[:, :], w[:, :], AX.X, ALU.max, negate=True))
                dve.tensor_scalar(shift[:, :], neg_max[:, :], 0.1, None, ALU.mult).then_inc(shift_ready, 1)

            def z_tile(t):
                link = chain(dve, z_step, 4 * t)
                dve.wait_ge(y_ready, t + 1)
                link(dve.reciprocal(r_sum[:, :], row_sums[:, ds(t, 1)]))
                dve.scalar_tensor_tensor(out=z[:, :], in0=y[:, :], scalar=r_sum[:, :], in1=row(s.act, t),
                                         op0=ALU.mult, op1=ALU.add).then_inc(z_ready, 1)
                dve.wait_ge(z_ready, t + 2)
                link(dve.bn_stats(stats[:, :], z[:, :]))
                link(dve.tensor_scalar(row(s.act, t), z[:, :], 1.0, None, ALU.mult))
                link(dve.tensor_scalar(row(all_stats, t), stats[:, :], 1.0, None, ALU.mult))

            w_tile(0, first=True)
            w_tile(1)
            with dve.Fori(2, NT) as t:
                w_tile(t)
                z_tile(t - 2)
            z_tile(NT - 2)
            z_tile(NT - 1)

            link = chain(dve, n_step)
            for t in range(NT):
                last = dve.bn_aggr(mvs[:, t, :], all_stats[:, t, :])
            link(last)
            norm_scale(dve, link, mvs[:, :, 1], (nrm[:, 0, :], nrm[:, 1, :]), root_ready, var_ready, nrm[:, 2, :])
            for t in range(NT):
                dve.tensor_scalar(s.act[:, t, :], s.act[:, t, :], mvs[:, t, 0:1], nrm[:, 2, t:t + 1],
                                  ALU.subtract, ALU.mult).then_inc(x1_ready, 1)


def transpose_tiles(pe, src, ident, banks, src_ready, ready, taken):
    for n in range(NT // 2):
        if n >= 2:
            pe.wait_ge(taken, n - 1)
        pe.wait_ge(src_ready, 2 * n + 2)
        for k in range(KD):
            for j in range(2):
                mm = pe.transpose(banks[n % 2][:, 2 * k + j, :], src[:, 2 * n + j, k * P:(k + 1) * P], ident[:, :])
        mm.then_inc(ready, 1)


def take_tiles(act, dst, banks, ready, taken):
    for n in range(NT // 2):
        act.wait_ge(ready, n + 1)
        act.copy(dst[:, :, 2 * n * P:(2 * n + 2) * P],
                 banks[n % 2][:, :, :].rearrange("p (k c) d -> p k (c d)", k=KD)).then_inc(taken, 1)


def cross_attention(nc, s):
    with ExitStack() as ctx:
        s.q_stack = ctx.enter_context(nc.sbuf_tensor("q_stack", [P, NB * NG, G, BLK], BF16))
        stack_queries(nc, s)
        s.ctx = s.actT[:, :, :].rearrange("p k t -> p (k t)").rearrange("p (t d) -> p t d", t=NT)
        attend(nc, s)
    cross_output(nc, s)


def stack_queries(nc, s):
    with ExitStack() as ctx:
        def sb(name, shape, dt=F32):
            return ctx.enter_context(nc.sbuf_tensor(name, shape, dt))

        def sem(name):
            return ctx.enter_context(nc.semaphore(name))

        QSCALE = float(HD) ** -0.5
        w = sb("w_cq", [P, KD, D])
        b = sb("b_cq", [P, KD])
        q = sb("cq", [P, 2, KD, BLK])
        rest = sb("cq_rest", [P, KD, BLK])
        part = sb("cq_part", [P, 2, 3, KD, BLK], BF16)
        pq = [ctx.enter_context(nc.psum_tensor(f"pq{i}", [P, KD, BLK], F32)) for i in range(2)]
        loaded = sem("cq_loaded")
        b_scaled = sem("cq_b_scaled")
        ready = sem("cq_product")
        scaled = sem("cq_scaled")
        split = sem("cq_split")
        parts_out = [sem(f"cq_parts_out{i}") for i in range(NB)]
        stacked = sem("cq_stacked")
        ones = sem("cq_ones")
        step = sem("cq_step")
        block = ctx.enter_context(nc.Block())

        @block.sync
        def _(sp):
            sp.dma_start(w[:, :, :], s.w_cq).then_inc(loaded, 16)
            sp.dma_start(b[:, :], s.b["cq"]).then_inc(loaded, 16)
            for n in range(NB):
                sp.wait_ge(split, n + 1)
                for c in range(3):
                    sp.dma_start(s.q_parts[c, :, n * BLK:(n + 1) * BLK].rearrange("(k p) t -> p k t", p=P),
                                 part[:, n % 2, c, :, :]).then_inc(parts_out[n], 16)
            sp.wait_ge(parts_out[NB - 1], 48)

        @block.gpsimd
        def _(pool):
            pool.memset(s.q_stack[R_MASK:R_ALL, 0:NB * NG // 2, :, :], 1.0).then_inc(ones, 1)
            pool.wait_ge(ones, 1)
            for n in range(NB):
                pool.wait_ge(parts_out[n], 48)
                for j, c in enumerate(Q_PARTS):
                    pool.dma_start(s.q_stack[HD * j:HD * (j + 1), NG * n:NG * (n + 1), :, :].rearrange("p g h t -> p (g h) t"),
                                   s.q_parts[c, :, n * BLK:(n + 1) * BLK].rearrange("(h d) t -> d h t", h=H)).then_inc(stacked, 16)
            pool.wait_ge(stacked, 16 * NB * len(Q_PARTS))

        @block.tensor
        def _(pe):
            pe.wait_ge(loaded, 32)
            for n in range(NB):
                if n >= 2:
                    pe.wait_ge(scaled, n - 1)
                for half in range(KD):
                    for k in range(KD):
                        mm = pe.matmul(pq[n % 2][:, half, :], w[:, k, half * P:(half + 1) * P],
                                       s.actT[:, k, n * BLK:(n + 1) * BLK], start=(k == 0), stop=(k == KD - 1))
                mm.then_inc(ready, 1)

        @block.scalar
        def _(act):
            act.wait_ge(b_scaled, 1)
            for n in range(NB):
                act.wait_ge(ready, n + 1)
                if n >= 2:
                    act.wait_ge(split, n - 1)
                for half in range(KD):
                    ins = act.activation(q[:, n % 2, half, :], pq[n % 2][:, half, :], ACT.Identity,
                                         bias=b[:, half:half + 1], scale=QSCALE)
                ins.then_inc(scaled, 1)

        @block.vector
        def _(dve):
            dve.memset(s.q_stack[R_MASK:R_ALL, NB * NG // 2:, :, :], 1.0)
            dve.wait_ge(loaded, 32)
            dve.tensor_scalar(b[:, :], b[:, :], QSCALE, None, ALU.mult).then_inc(b_scaled, 1)
            link = chain(dve, step)
            for n in range(NB):
                dve.wait_ge(scaled, n + 1)
                if n >= 2:
                    dve.wait_ge(parts_out[n - 2], 48)
                src, out = q[:, n % 2, :, :], part[:, n % 2, :, :, :]
                link(dve.tensor_copy(out[:, 0], src))
                link(dve.tensor_tensor(rest[:, :, :], src, out[:, 0], ALU.subtract))
                link(dve.tensor_copy(out[:, 1], rest[:, :, :]))
                dve.tensor_tensor(out[:, 2], rest[:, :, :], out[:, 1], ALU.subtract).then_inc(split, 1)


def attend(nc, s):
    with ExitStack() as ctx:
        def sb(name, shape, dt=F32):
            return ctx.enter_context(nc.sbuf_tensor(name, shape, dt))

        def ps(name, shape, dt=F32):
            return ctx.enter_context(nc.psum_tensor(name, shape, dt))

        def sem(name):
            return ctx.enter_context(nc.semaphore(name))

        NIT = NB * NG
        CHUNKS = ((0, 2 * BLK), (2 * BLK, S2))
        NCH = 2 * QT * G
        STEPS = NKT
        E_IT = STEPS * G

        probs = sb("xprobs", [P, 2, G, BLK])
        out_sb = sb("xout_sb", [P, BLK])
        chunk_max = sb("chunk_max", [P, 2, QT, G])
        max_rest = sb("max_rest", [P, 2, QT, G])
        max_part = sb("max_part", [P, QT, 3 * G], BF16)
        max_rows = sb("max_rows", [3 * G, QT, P], BF16)
        r_den = sb("r_den", [P, QT, G])
        a_ps = [ps(f"a_ps{i}", [P, 2 * BLK]) for i in range(2)]
        e_ps = [ps(f"e_ps{i}", [P, BLK]) for i in range(2)]
        o_ps = ps("o_ps", [P, BLK])
        t_ps = ps("t_ps", [P, QT, P])
        t_rows = t_ps[:, :, :].bitcast(BF16)[0:3 * G, :, 0:P]

        chunk_ready = sem("chunk_ready")
        chunk_free = sem("chunk_free")
        max_split = sem("max_split")
        rows_ready = sem("rows_ready")
        rows_taken = sem("rows_taken")
        rows_in = sem("rows_in")
        s_ready = sem("s_ready")
        exp_done = sem("exp_done")
        pv_done = sem("pv_done")
        out_taken = sem("out_taken")
        ctx_turned = sem("ctx_turned")
        ctx_done = sem("ctx_done")
        m_step = sem("m_step")
        c_step = sem("c_step")
        block = ctx.enter_context(nc.Block())

        @block.sync
        def _(sp):
            def rows_to_stack(it):
                sp.wait_ge(rows_taken, it + 1)
                for c in range(3):
                    sp.dma_start(s.q_stack[R_MAX + c:R_MAX + c + 1, ds(it, 1), :, :].rearrange("p o h t -> p o (h t)"),
                                 max_rows[G * c:G * (c + 1), :, :]).then_inc(rows_in, 16)

            with sp.Fori(0, NIT) as it:
                rows_to_stack(it)
            sp.wait_ge(rows_in, 48 * NIT)

        @block.tensor
        def _(pe):
            def max_chunk(it, g, c):
                qt, h, part = c // (2 * G), c // 2 % G, c % 2
                a, b = CHUNKS[part]
                bank = a_ps[c % 2]
                pe.wait_ge(chunk_free, NCH * it + c + 1)
                for k in range(a, b, BLK):
                    n = min(BLK, b - k)
                    mm = pe.matmul(bank[:, k - a:k - a + n],
                                   s.q_stack[0:R_MAX, ds(it, 1), h, qt * P:(qt + 1) * P].rearrange("p o t -> p (o t)"),
                                   s.k_stack[0:R_MAX, G * g + h, k:k + n], start=True, stop=True)
                mm.then_inc(chunk_ready, 1)

            def turn_maxima(it, before):
                pe.wait_ge(max_split, it + 1)
                pe.wait_ge(ctx_done, before + 1)
                if not (isinstance(it, int) and it == 0):
                    pe.wait_ge(rows_taken, it)
                for qt in range(QT):
                    mm = pe.transpose(t_rows[:, qt, :], max_part[:, qt, :], s.ident_b[:, :])
                mm.then_inc(rows_ready, 1)

            def values(it, g, j):
                for h in range(G):
                    rows = P if j < NKT - 1 else LASTK
                    pe.wait_ge(exp_done, E_IT * it + G * j + h + 3)
                    if j == 0 and h == 0:
                        pe.wait_ge(out_taken, it + 1)
                    mm = pe.matmul(o_ps[VW * h:VW * (h + 1), :], s.cv[0:rows, j, G * g + h, :],
                                   probs[0:rows, (g * STEPS + j) % 2, h, :], start=(j == 0), stop=(j == NKT - 1))
                mm.then_inc(pv_done, 1)

            def iteration(it, g, with_maxima):
                ahead, ga = it + 2, (g + 2) % NG
                slots = {}
                if with_maxima:
                    for c in range(NCH):
                        slots.setdefault(c * 11 // 8, []).append(c)
                pe.wait_ge(rows_in, 48 * (it + 1))
                for j in range(STEPS):
                    rows = P if j < NKT - 1 else LASTK
                    for h in range(G):
                        pe.wait_ge(exp_done, E_IT * it + G * j + h + 1)
                        pe.matmul(e_ps[h % 2][0:rows, :], s.k_stack[0:R_ALL, G * g + h, j * P:j * P + rows],
                                  s.q_stack[0:R_ALL, ds(it, 1), h, :].rearrange("p o t -> p (o t)"),
                                  start=True, stop=True).then_inc(s_ready, 1)
                        for c in slots.get(G * j + h, []):
                            max_chunk(ahead, ga, c)
                    if j:
                        values(it, g, j - 1)
                if with_maxima:
                    turn_maxima(ahead, it)
                values(it, g, STEPS - 1)
                pe.wait_ge(out_taken, it + 2)
                pe.wait_ge(rows_taken, (it + 3) if with_maxima else NIT)
                pe.wait_ge(ctx_done, it + 1)
                for qt in range(QT):
                    mm = pe.transpose(t_ps[:, qt, :], out_sb[:, qt * P:(qt + 1) * P], s.ident[:, :])
                mm.then_inc(ctx_turned, 1)

            for it in range(2):
                for c in range(NCH):
                    max_chunk(it, it, c)
                turn_maxima(it, 0)
            with pe.Fori(0, NB - 1) as qb:
                for g in range(NG):
                    iteration(NG * qb + g, g, True)
            for g in range(NG):
                iteration(NG * (NB - 1) + g, g, g + 2 < NG)

        @block.scalar
        def _(act):
            act.sem_inc(exp_done, 2)
            act.sem_inc(out_taken, 1)

            def iteration(it, g):
                for j in range(STEPS):
                    rows = P if j < NKT - 1 else LASTK
                    for h in range(G):
                        act.wait_ge(s_ready, E_IT * it + G * j + h + 1)
                        if h == 0:
                            act.wait_ge(pv_done, STEPS * it + j + 1)
                        act.activation(probs[0:rows, (g * STEPS + j) % 2, h, :], e_ps[h % 2][0:rows, :],
                                       ACT.Exp).then_inc(exp_done, 1)
                act.wait_ge(pv_done, STEPS * it + STEPS + 2)
                act.copy(out_sb[:, :], o_ps[:, :]).then_inc(out_taken, 1)

            with act.Fori(0, NB) as qb:
                for g in range(NG):
                    iteration(NG * qb + g, g)

        @block.vector
        def _(dve):
            dve.sem_inc(chunk_free, 2)
            dve.sem_inc(pv_done, 2)
            dve.sem_inc(ctx_done, 1)

            def take_chunk(it, c):
                qt, h, part = c // (2 * G), c // 2 % G, c % 2
                a, b = CHUNKS[part]
                dve.wait_ge(chunk_ready, NCH * it + c + 1)
                dve.tensor_reduce(chunk_max[:, part, qt, h:h + 1], a_ps[c % 2][:, 0:b - a], AX.X,
                                  ALU.max).then_inc(chunk_free, 1)

            def split_maxima(it):
                link = chain(dve, m_step, 4 * it)
                dve.wait_ge(chunk_free, NCH * it + NCH + 2)
                m, rest = max_rest[:, 0, :, :], max_rest[:, 1, :, :]
                link(dve.tensor_tensor(m, chunk_max[:, 0, :, :], chunk_max[:, 1, :, :], ALU.max))
                link(dve.tensor_scalar(max_part[:, :, 0:G], m, -1.0, None, ALU.mult))
                link(dve.scalar_tensor_tensor(out=rest, in0=m, scalar=-1.0, in1=max_part[:, :, 0:G],
                                              op0=ALU.mult, op1=ALU.subtract))
                link(dve.tensor_copy(max_part[:, :, G:2 * G], rest))
                dve.tensor_tensor(max_part[:, :, 2 * G:3 * G], rest, max_part[:, :, G:2 * G],
                                  ALU.subtract).then_inc(max_split, 1)

            def take_rows(it):
                dve.wait_ge(rows_ready, it + 1)
                if not (isinstance(it, int) and it == 0):
                    dve.wait_ge(rows_in, 48 * it)
                dve.tensor_copy(max_rows[:, :, :], t_rows).then_inc(rows_taken, 1)

            def take_context(it, qb, g):
                link = chain(dve, c_step, it)
                dve.wait_ge(ctx_turned, it + 1)
                heads = t_ps[:, :, :].rearrange("p q (h v) -> p q h v", h=G)
                link(dve.reciprocal(r_den[:, :, :], heads[:, :, :, HD]))
                dve.tensor_tensor(s.ctx[:, ds(qb * QT, QT), G * HD * g:G * HD * (g + 1)].rearrange("p q (h d) -> p q h d", h=G),
                                  heads[:, :, :, 0:HD], r_den[:, :, :].unsqueeze(3).broadcast_to([P, QT, G, HD]),
                                  ALU.mult).then_inc(ctx_done, 1)

            def iteration(it, qb, g, with_maxima):
                if with_maxima:
                    for c in range(NCH):
                        take_chunk(it + 2, c)
                    split_maxima(it + 2)
                    take_rows(it + 2)
                take_context(it, qb, g)

            for it in range(2):
                for c in range(NCH):
                    take_chunk(it, c)
                split_maxima(it)
                take_rows(it)
            with dve.Fori(0, NB - 1) as qb:
                for g in range(NG):
                    iteration(NG * qb + g, qb, g, True)
            for g in range(NG):
                iteration(NG * (NB - 1) + g, NB - 1, g, g + 2 < NG)


def cross_output(nc, s):
    with ExitStack() as ctx:
        def sb(name, shape, dt=F32):
            return ctx.enter_context(nc.sbuf_tensor(name, shape, dt))

        def sem(name):
            return ctx.enter_context(nc.semaphore(name))

        w = sb("w_co", [P, KD, D])
        b = sb("b_co", [P, D])
        turned_sb = sb("ctxT_sb", [P, 2, KD, P])
        all_stats = sb("all_stats2", [P, NT, 6])
        mvs = sb("mvs2", [P, NT, 2])
        nrm = sb("nrm2", [P, 3, NT])
        turned = [ctx.enter_context(nc.psum_tensor(f"ctxT{i}", [P, KD, P], F32)) for i in range(2)]
        y = [ctx.enter_context(nc.psum_tensor(f"y2{i}", [P, D], F32)) for i in range(2)]
        banks = [ctx.enter_context(nc.psum_tensor(f"x2T{i}", [P, 4, P], F32)) for i in range(2)]
        loaded = sem("co_loaded")
        turned_ready = sem("co_turned")
        turned_taken = sem("co_taken")
        y_ready = sem("co_y")
        z_ready = sem("co_z")
        biased = sem("co_biased")
        step = sem("co_step")
        var_ready, root_ready = sem("var_ready2"), sem("root_ready2")
        x2_ready, x2T_ready, x2T_taken = sem("x2_ready"), sem("x2T_ready"), sem("x2T_taken")
        block = ctx.enter_context(nc.Block())

        @block.sync
        def _(sp):
            sp.dma_start(w[:, :, :], s.w_co).then_inc(loaded, 16)
            sp.dma_start(b[:, :], s.b["co"].partition_broadcast(P)).then_inc(loaded, 16)

        @block.tensor
        def _(pe):
            pe.wait_ge(loaded, 32)
            for t in range(NT + 1):
                if t < NT:
                    if t >= 2:
                        pe.wait_ge(turned_taken, t - 1)
                    for k in range(KD):
                        mm = pe.transpose(turned[t % 2][:, k, :], s.ctx[:, t, k * P:(k + 1) * P], s.ident[:, :])
                    mm.then_inc(turned_ready, 1)
                if t:
                    u = t - 1
                    pe.wait_ge(turned_taken, u + 1)
                    if u >= 2:
                        pe.wait_ge(z_ready, u - 1)
                    for k in range(KD):
                        mm = pe.matmul(y[u % 2][:, :], turned_sb[:, u % 2, k, :], w[:, k, :], start=(k == 0), stop=(k == KD - 1))
                    mm.then_inc(y_ready, 1)
            transpose_tiles(pe, s.act, s.ident, banks, x2_ready, x2T_ready, x2T_taken)

        @block.scalar
        def _(act):
            for t in range(NT):
                act.wait_ge(turned_ready, t + 1)
                if t >= 2:
                    act.wait_ge(y_ready, t - 1)
                act.copy(turned_sb[:, t % 2, :, :], turned[t % 2][:, :, :]).then_inc(turned_taken, 1)
            act.wait_ge(var_ready, 1)
            act.activation(nrm[:, 1, :], nrm[:, 0, :], ACT.Sqrt).then_inc(root_ready, 1)
            take_tiles(act, s.actT, banks, x2T_ready, x2T_taken)

        @block.vector
        def _(dve):
            link = chain(dve, step)
            dve.wait_ge(loaded, 32)
            link(dve.tensor_tensor(s.act[:, :, :], s.act[:, :, :],
                                   b[:, :].unsqueeze(1).broadcast_to([P, NT, D]), ALU.add))
            for t in range(NT):
                dve.wait_ge(y_ready, t + 1)
                dve.tensor_tensor(s.act[:, t, :], y[t % 2][:, :], s.act[:, t, :], ALU.add).then_inc(z_ready, 1)
                dve.wait_ge(z_ready, t + 1)
                link(dve.bn_stats(all_stats[:, t, :], s.act[:, t, :]))
            for t in range(NT):
                last = dve.bn_aggr(mvs[:, t, :], all_stats[:, t, :])
            link(last)
            norm_scale(dve, link, mvs[:, :, 1], (nrm[:, 0, :], nrm[:, 1, :]), root_ready, var_ready, nrm[:, 2, :])
            for t in range(NT):
                dve.tensor_scalar(s.act[:, t, :], s.act[:, t, :], mvs[:, t, 0:1], nrm[:, 2, t:t + 1],
                                  ALU.subtract, ALU.mult).then_inc(x2_ready, 1)


def route(nc, s):
    with ExitStack() as ctx:
        def sb(name, shape, dt=F32):
            return ctx.enter_context(nc.sbuf_tensor(name, shape, dt))

        def ps(name, shape, dt=F32):
            return ctx.enter_context(nc.psum_tensor(name, shape, dt))

        def sem(name):
            return ctx.enter_context(nc.semaphore(name))

        gate = sb("gate", [P, KD, E])
        sg, su = sb("sg", [P, KD, FS]), sb("su", [P, KD, FS])
        sd = sb("sd", [P, ST, D])
        gelu = sb("s_gelu", [P, 2, BLK])
        up = sb("s_up", [P, 2, BLK])
        hidden = sb("s_hidden", [P, 2, ST, BLK])
        down = sb("s_down", [P, 2, D])
        probs = sb("gate_probs", [P, NT, E])
        stat = sb("gate_stat", [P, 2, NT])
        by_expert = sb("by_expert", [E, T])
        best8 = sb("best8", [E, 8])
        at8 = sb("at8", [E, 8], U32)
        best = sb("best", [E, 2, CAP])
        logit_ps = ps("logit_ps", [P, NT, E])
        turn_ps = [ps(f"turn_ps{i}", [P, BLK]) for i in range(2)]
        g_ps = [ps(f"g_ps{i}", [P, BLK]) for i in range(2)]
        u_ps = [ps(f"u_ps{i}", [P, BLK]) for i in range(2)]
        y_ps = ps("y_ps", [P, D])

        loaded = sem("r_loaded")
        x2_out = sem("x2_out")
        logits_ready = sem("logits_ready")
        shifted = sem("logits_shifted")
        exp_ready = sem("gate_exp")
        probs_ready = sem("gate_probs_ready")
        turned = sem("scores_turned")
        turned_taken = sem("scores_taken")
        found = sem("found")
        best_ready = sem("best_ready")
        lists_ready = sem("lists_ready")
        lists_taken = sem("lists_taken")
        gu_ready = sem("s_gu_ready")
        gu_taken = sem("s_gu_taken")
        h_ready = sem("s_h_ready")
        y_ready = sem("s_y_ready")
        y_taken = sem("s_y_taken")
        acc_ready = sem("acc_ready")
        acc_out = sem("acc_out")
        step = sem("r_step")
        block = ctx.enter_context(nc.Block())
        rows = lambda ap: ap.rearrange("(t p) d -> p t d", p=P)

        @block.sync
        def _(sp):
            sp.dma_start(gate[:, :, :], s.gate_w).then_inc(loaded, 16)
            sp.dma_start(sg[:, :, :], s.s_gate).then_inc(loaded, 16)
            sp.dma_start(su[:, :, :], s.s_up).then_inc(loaded, 16)
            sp.dma_start(sd[:, :, :], s.s_down).then_inc(loaded, 16)
            sp.dma_start(rows(s.x2), s.act[:, :, :]).then_inc(x2_out, 16)
            for e in range(2):
                load_expert(sp, s, e, e)
            for n in range(NB):
                sp.wait_ge(acc_ready, QT * (n + 1))
                sp.dma_start(rows(s.acc)[:, QT * n:QT * (n + 1), :],
                             s.act[:, QT * n:QT * (n + 1), :]).then_inc(acc_out, 16)
            sp.wait_ge(acc_out, 16 * NB)

        @block.tensor
        def _(pe):
            pe.wait_ge(loaded, 64)
            for t in range(NT):
                for k in range(KD):
                    mm = pe.matmul(logit_ps[:, t, :], s.actT[:, k, t * P:(t + 1) * P], gate[:, k, :],
                                   start=(k == 0), stop=(k == KD - 1))
            mm.then_inc(logits_ready, 1)

            def turn_scores():
                pe.wait_ge(probs_ready, 1)
                for t in range(NT):
                    if t % QT == 0 and t // QT >= 2:
                        pe.wait_ge(turned_taken, t // QT - 1)
                    mm = pe.transpose(turn_ps[t // QT % 2][0:E, t % QT * P:(t % QT + 1) * P], probs[:, t, :], s.ident[:, :])
                    if t % QT == QT - 1:
                        mm.then_inc(turned, 1)

            def shared_rows(n):
                pe.wait_ge(h_ready, ST * (n + 1))
                for q in range(QT):
                    if QT * n + q:
                        pe.wait_ge(y_taken, QT * n + q)
                    for i in range(ST):
                        mm = pe.matmul(y_ps[:, :], hidden[:, n % 2, i, q * P:(q + 1) * P], sd[:, i, :],
                                       start=(i == 0), stop=(i == ST - 1))
                    mm.then_inc(y_ready, 1)

            for n in range(NB):
                for i in range(ST):
                    m = ST * n + i
                    if m >= 2:
                        pe.wait_ge(gu_taken, m - 1)
                    for out, weight in ((g_ps, sg), (u_ps, su)):
                        for k in range(KD):
                            mm = pe.matmul(out[m % 2][:, :], weight[:, k, i * P:(i + 1) * P],
                                           s.actT[:, k, n * BLK:(n + 1) * BLK], start=(k == 0), stop=(k == KD - 1))
                    mm.then_inc(gu_ready, 1)
                    if m == 1:
                        turn_scores()
                if n:
                    shared_rows(n - 1)
            shared_rows(NB - 1)
            pe.wait_ge(best_ready, 1)
            pe.wait_ge(turned_taken, NB)
            lists = turn_ps[0][:, 0:2 * CT * E].rearrange("p (a e) -> p a e", e=E)
            for a in range(2):
                for c in range(CT):
                    mm = pe.transpose(lists[:, CT * a + c, :], best[:, a, c * P:(c + 1) * P], s.ident[0:E, 0:E])
            mm.then_inc(lists_ready, 1)

        @block.scalar
        def _(act):
            act.wait_ge(shifted, 1)
            act.activation(probs[:, :, :], probs[:, :, :], ACT.Exp).then_inc(exp_ready, 1)

            def take_rows(n):
                for q in range(QT):
                    m = QT * n + q
                    act.wait_ge(y_ready, m + 1)
                    if m >= 2:
                        act.wait_ge(acc_ready, m - 1)
                    act.copy(down[:, m % 2, :], y_ps[:, :]).then_inc(y_taken, 1)

            for n in range(NB):
                for i in range(ST):
                    m = ST * n + i
                    act.wait_ge(gu_ready, m + 1)
                    if m >= 2:
                        act.wait_ge(h_ready, m - 1)
                    act.activation(gelu[:, m % 2, :], g_ps[m % 2][:, :], ACT.Gelu)
                    act.copy(up[:, m % 2, :], u_ps[m % 2][:, :]).then_inc(gu_taken, 1)
                    if m == 1:
                        for b in range(NB):
                            act.wait_ge(turned, b + 1)
                            act.copy(by_expert[:, b * BLK:(b + 1) * BLK], turn_ps[b % 2][0:E, :]).then_inc(turned_taken, 1)
                if n:
                    take_rows(n - 1)
            take_rows(NB - 1)

        @block.gpsimd
        def _(pool):
            def add_rows(n):
                for q in range(QT):
                    m = QT * n + q
                    pool.wait_ge(y_taken, m + 1)
                    if m == 0:
                        pool.wait_ge(x2_out, 16)
                    pool.tensor_tensor(s.act[:, m, :], s.act[:, m, :], down[:, m % 2, :], ALU.add).then_inc(acc_ready, 1)

            for n in range(NB):
                for i in range(ST):
                    m = ST * n + i
                    pool.wait_ge(gu_taken, m + 1)
                    if n >= 2 and i == 0:
                        pool.wait_ge(y_ready, QT * (n - 1))
                    pool.tensor_tensor(hidden[:, n % 2, i, :], gelu[:, m % 2, :], up[:, m % 2, :], ALU.mult).then_inc(h_ready, 1)
                if n:
                    add_rows(n - 1)
            add_rows(NB - 1)

        @block.vector
        def _(dve):
            link = chain(dve, step)
            wide = [P, NT, E]
            dve.wait_ge(logits_ready, 1)
            link(dve.tensor_reduce(stat[:, 0, :], logit_ps[:, :, :], AX.X, ALU.max))
            dve.tensor_tensor(probs[:, :, :], logit_ps[:, :, :], stat[:, 0, :].unsqueeze(2).broadcast_to(wide),
                              ALU.subtract).then_inc(shifted, 1)
            dve.wait_ge(exp_ready, 1)
            link(dve.tensor_reduce(stat[:, 0, :], probs[:, :, :], AX.X, ALU.add))
            link(dve.reciprocal(stat[:, 1, :], stat[:, 0, :]))
            dve.tensor_tensor(probs[:, :, :], probs[:, :, :], stat[:, 1, :].unsqueeze(2).broadcast_to(wide),
                              ALU.mult).then_inc(probs_ready, 1)
            dve.wait_ge(turned_taken, NB)
            with dve.Fori(0, CAP // 8) as r:
                dve.max(best8[:, :], by_expert[:, :]).then_inc(found, 1)
                dve.wait_ge(found, 4 * r + 1)
                dve.tensor_scalar(best[:, 0, ds(r * 8, 8)], best8[:, :], 1.0, None, ALU.mult).then_inc(found, 1)
                dve.max_index(at8[:, :], best8[:, :], by_expert[:, :]).then_inc(found, 1)
                dve.match_replace(out=by_expert[:, :], in_to_replace=best8[:, :], in_values=by_expert[:, :],
                                  imm_value=-1.0).then_inc(found, 1)
                dve.wait_ge(found, 4 * r + 4)
                dve.tensor_scalar(best[:, 1, ds(r * 8, 8)], at8[:, :], 1.0, None, ALU.mult)
            link(dve.engine_nop())
            dve.engine_nop().then_inc(best_ready, 1)
            dve.wait_ge(lists_ready, 1)
            lists = turn_ps[0][:, 0:2 * CT * E].rearrange("p (a c e) -> p a c e", a=2, c=CT)
            dve.tensor_copy(s.weight[:, :, :], lists[:, 0])
            dve.tensor_copy(s.token[:, :, :], lists[:, 1]).then_inc(lists_taken, 1)


def load_expert(sp, s, e, p):
    for name, dst, src in (("gate", s.wg_sb, s.w_gate), ("up", s.wu_sb, s.w_up), ("down", s.wd_sb, s.w_down)):
        sp.dma_start(dst[:, p, :, :], src[ds(e, 1)].rearrange("o p k n -> p (o k) n")).then_inc(s.w_loaded[name, p], 16)


def experts(nc, s):
    with ExitStack() as ctx:
        def sb(name, shape, dt=F32):
            return ctx.enter_context(nc.sbuf_tensor(name, shape, dt))

        def ps(name, shape, dt=F32):
            return ctx.enter_context(nc.psum_tensor(name, shape, dt))

        def sem(name):
            return ctx.enter_context(nc.semaphore(name))

        token = sb("token_e", [P, 2, CT], U32)
        xg = sb("xg", [P, 2, CT, D])
        xgT = sb("xgT", [P, 2, KD, CAP])
        gelu = sb("e_gelu", [P, 2, CAP])
        hidden = sb("e_hidden", [P, 2, FT, CAP])
        rows_out = sb("rows_out", [P, 2, CT, D])
        all_stats = sb("all_stats3", [P, NT, 6])
        mvs = sb("mvs3", [P, NT, 2])
        nrm = sb("nrm3", [P, 3, NT])
        x_ps = ps("xg_ps", [P, KD, CAP])
        gu_ps = [ps(f"gu_ps{i}", [P, 2, CAP]) for i in range(4)]
        d_ps = [ps(f"d_ps{i}", [P, CT, D]) for i in range(2)]

        token_ready = sem("token_ready")
        gathered = [sem(f"gathered{p}") for p in range(2)]
        xT_ready = sem("xgT_ready")
        xT_taken = sem("xgT_taken")
        gu_ready = sem("gu_ready")
        g_taken = sem("g_taken")
        h_ready = sem("h_ready")
        d_ready = sem("d_ready")
        out_ready = sem("out_ready")
        tick = sem("tick")
        added = sem("added")
        back = [sem(f"rows_back{i}") for i in range(NB)]
        var_ready, root_ready, step = sem("var_ready3"), sem("root_ready3"), sem("n3_step")
        normed = sem("normed")
        stored = sem("stored")
        block = ctx.enter_context(nc.Block())
        rows = lambda ap: ap.rearrange("(t p) d -> p t d", p=P)

        @block.sync
        def _(sp):
            with sp.Fori(1, E // 2) as pair:
                for p in range(2):
                    e = 2 * pair + p
                    sp.wait_ge(d_ready, e - 1)
                    load_expert(sp, s, e, p)
            sp.wait_ge(added, 16 * CT * E)
            for n in range(NB):
                sp.dma_start(s.act[:, QT * n:QT * (n + 1), :], rows(s.acc)[:, QT * n:QT * (n + 1), :]).then_inc(back[n], 16)
            for n in range(NB):
                sp.wait_ge(normed, QT * (n + 1))
                sp.dma_start(rows(s.out)[:, QT * n:QT * (n + 1), :], s.act[:, QT * n:QT * (n + 1), :]).then_inc(stored, 16)
            sp.wait_ge(stored, 16 * NB)

        @block.gpsimd
        def _(pool):
            def gather(e, p):
                pool.tensor_copy(token[:, p, :], s.token[:, :, ds(e, 1)].rearrange("p c o -> p (c o)")).then_inc(token_ready, 1)
                pool.wait_ge(token_ready, e + 1)
                pool.sem_inc(tick, 1)
                for c in range(CT):
                    pool.indirect_dma_start(out=xg[:, p, c, :], out_offset=None, in_=s.x2,
                                            in_offset=bass.IndirectOffsetOnAxis(ap=token[:, p, c:c + 1], axis=0)).then_inc(gathered[p], 16)

            def scatter(e, p, first=False):
                pool.wait_ge(out_ready, e + 3)
                if not first:
                    pool.wait_ge(added, 16 * CT * e)
                pool.sem_inc(tick, 1)
                for c in range(CT):
                    pool.indirect_dma_start(out=s.acc, out_offset=bass.IndirectOffsetOnAxis(ap=token[:, p, c:c + 1], axis=0),
                                            in_=rows_out[:, p, c, :], in_offset=None, compute_op=ALU.add).then_inc(added, 16)

            gather(0, 0)
            gather(1, 1)
            scatter(0, 0, first=True)
            with pool.Fori(1, E // 2) as pair:
                for p in range(2):
                    e = 2 * pair + p
                    pool.wait_ge(added, 16 * CT * (e - 1))
                    pool.wait_ge(xT_ready, e - 1)
                    gather(e, p)
                    scatter(e - 1, 1 - p)
            scatter(E - 1, 1)

        @block.tensor
        def _(pe):
            def turn_rows(pair, p):
                e = 2 * pair + p
                pe.wait_ge(gathered[p], 16 * CT * (pair + 1))
                pe.wait_ge(xT_taken, e + 1)
                for c in range(CT):
                    for k in range(KD):
                        mm = pe.transpose(x_ps[:, k, c * P:(c + 1) * P], xg[:, p, c, k * P:(k + 1) * P], s.ident[:, :])
                mm.then_inc(xT_ready, 1)

            def gate_up(pair, p):
                e = 2 * pair + p
                pe.wait_ge(xT_taken, e + 2)
                pe.wait_ge(s.w_loaded["gate", p], 16 * (pair + 1))
                pe.wait_ge(s.w_loaded["up", p], 16 * (pair + 1))
                for i in range(FT):
                    bank = gu_ps[i % 4]
                    pe.wait_ge(h_ready, FT * e + i + 1)
                    for a, weight in ((0, s.wg_sb), (1, s.wu_sb)):
                        for k in range(KD):
                            mm = pe.matmul(bank[:, a, :], weight[:, p, k, i * P:(i + 1) * P], xgT[:, p, k, :],
                                           start=(k == 0), stop=(k == KD - 1))
                    mm.then_inc(gu_ready, 1)

            def down(pair, p):
                e = 2 * pair + p
                pe.wait_ge(h_ready, FT * e + FT + 4)
                pe.wait_ge(s.w_loaded["down", p], 16 * (pair + 1))
                pe.wait_ge(out_ready, e + 1)
                for c in range(CT):
                    for i in range(FT):
                        mm = pe.matmul(d_ps[p][:, c, :], hidden[:, p, i, c * P:(c + 1) * P], s.wd_sb[:, p, i, :],
                                       start=(i == 0), stop=(i == FT - 1))
                mm.then_inc(d_ready, 1)

            def expert(pair, p, last=False):
                gate_up(pair, p)
                if not last:
                    turn_rows(pair + p, 1 - p)
                down(pair, p)

            turn_rows(0, 0)
            with pe.Fori(0, E // 2 - 1) as pair:
                for p in range(2):
                    expert(pair, p)
            expert(E // 2 - 1, 0)
            expert(E // 2 - 1, 1, last=True)

        @block.scalar
        def _(act):
            act.sem_inc(xT_taken, 1)

            def take_rows(e, p):
                act.wait_ge(xT_ready, e + 1)
                act.copy(xgT[:, p, :, :], x_ps[:, :, :]).then_inc(xT_taken, 1)

            def expert(pair, p, last=False):
                e = 2 * pair + p
                for i in range(FT):
                    act.wait_ge(gu_ready, FT * e + i + 1)
                    act.wait_ge(h_ready, FT * e + i + 3)
                    act.activation(gelu[:, i % 2, :], gu_ps[i % 4][:, 0, :], ACT.Gelu).then_inc(g_taken, 1)
                if not last:
                    take_rows(e + 1, 1 - p)

            take_rows(0, 0)
            with act.Fori(0, E // 2 - 1) as pair:
                for p in range(2):
                    expert(pair, p)
            expert(E // 2 - 1, 0)
            expert(E // 2 - 1, 1, last=True)
            act.wait_ge(var_ready, 1)
            act.activation(nrm[:, 1, :], nrm[:, 0, :], ACT.Sqrt).then_inc(root_ready, 1)

        @block.vector
        def _(dve):
            dve.sem_inc(h_ready, 4)
            dve.sem_inc(out_ready, 2)

            def scale_rows(pair, p):
                e = 2 * pair + p
                dve.wait_ge(token_ready, e + 1)
                dve.wait_ge(d_ready, e + 1)
                for c in range(CT):
                    ins = dve.tensor_scalar(rows_out[:, p, c, :], d_ps[p][:, c, :],
                                            s.weight[:, c, ds(e, 1)], None, ALU.mult)
                ins.then_inc(out_ready, 1)

            def products(pair, p):
                e = 2 * pair + p
                for i in range(FT):
                    dve.wait_ge(g_taken, FT * e + i + 1)
                    dve.tensor_tensor(hidden[:, p, i, :], gelu[:, i % 2, :], gu_ps[i % 4][:, 1, :],
                                      ALU.mult).then_inc(h_ready, 1)

            with dve.Fori(0, E // 2) as pair:
                for p in range(2):
                    products(pair, p)
                    scale_rows(pair, p)

            link = chain(dve, step)
            for n in range(NB):
                dve.wait_ge(back[n], 16)
                for t in range(QT * n, QT * (n + 1)):
                    last = dve.bn_stats(all_stats[:, t, :], s.act[:, t, :])
            link(last)
            for t in range(NT):
                last = dve.bn_aggr(mvs[:, t, :], all_stats[:, t, :])
            link(last)
            norm_scale(dve, link, mvs[:, :, 1], (nrm[:, 0, :], nrm[:, 1, :]), root_ready, var_ready, nrm[:, 2, :])
            for t in range(NT):
                dve.tensor_scalar(s.act[:, t, :], s.act[:, t, :], mvs[:, t, 0:1], nrm[:, 2, t:t + 1],
                                  ALU.subtract, ALU.mult).then_inc(normed, 1)


def program(nc, arg, upto=9, dump=None):
    s = Shared()
    s.xT, s.ctxT, s.x, s.mask = arg["xT"], arg["ctxT"], arg["x"], arg["mask"]
    s.w_q, s.w_k, s.w_v, s.w_o = arg["wq"], arg["wk"], arg["wv"], arg["wo"]
    s.w_cq, s.w_ck, s.w_cv, s.w_co = arg["cwq"], arg["cwk"], arg["cwv"], arg["cwo"]
    s.b = {"q": arg["bq"], "k": arg["bk"], "v": arg["bv"], "o": arg["bo"],
           "cq": arg["cbq"], "ck": arg["cbk"], "cv": arg["cbv"], "co": arg["cbo"]}
    s.gate_w, s.out = arg["gate"], arg["out"]
    s.w_gate, s.w_up, s.w_down = arg["wg"], arg["wu"], arg["wd"]
    s.s_gate, s.s_up, s.s_down = arg["sg"], arg["su"], arg["sd"]

    def dram(name, shape, dt=F32):
        return nc.dram_tensor(name, shape, dt, kind="Internal").ap()

    s.k_parts = dram("k_parts", (3, D, S2), BF16)
    s.q_parts = dram("q_parts", (3, D, T), BF16)
    s.mask_parts = dram("mask_parts", (1, 6, S2), BF16)
    s.x2 = dram("x2_rows", (T, D))
    s.acc = dram("acc_rows", (T, D))
    with ExitStack() as ctx:
        def sb(name, shape, dt=F32):
            return ctx.enter_context(nc.sbuf_tensor(name, shape, dt))

        s.consts = ctx.enter_context(nc.semaphore("consts"))
        s.ident = sb("ident", [P, P])
        s.ident_b = sb("ident_b", [P, P], BF16)
        s.act = sb("activations", [P, NT, D])
        s.actT = sb("activationsT", [P, KD, T])
        s.qT = s.actT
        with ExitStack() as attention:
            s.cv = attention.enter_context(nc.sbuf_tensor("cv", [P, NKT, H, VW], F32))
            s.k_stack_space = attention.enter_context(nc.sbuf_tensor("k_stack", [P, H * S2], BF16))
            s.k_stack = s.k_stack_space[:, :].rearrange("p (h n) -> p h n", h=H)
            with ExitStack() as first:
                s.kT = first.enter_context(nc.sbuf_tensor("kT", [P, KD, T], F32))
                s.v = first.enter_context(nc.sbuf_tensor("v", [P, NT, D], F32))
                s.wo = first.enter_context(nc.sbuf_tensor("w_out", [P, KD, D], F32))
                project_inputs(nc, s)
                if upto >= 1:
                    self_attention(nc, s)
            if upto >= 2:
                cross_attention(nc, s)
        if upto >= 3:
            s.wg_sb = sb("wg_sb", [P, 2, KD, FI])
            s.wu_sb = sb("wu_sb", [P, 2, KD, FI])
            s.wd_sb = sb("wd_sb", [P, 2, FT, D])
            s.weight = sb("weight", [P, CT, E])
            s.token = sb("token", [P, CT, E], U32)
            s.w_loaded = {(n, p): ctx.enter_context(nc.semaphore(f"w_{n}{p}"))
                          for n in ("gate", "up", "down") for p in range(2)}
            route(nc, s)
            experts(nc, s)
        if dump:
            dump(nc, s)


def kernel(**inputs):
    import numpy as np
    import concourse.bacc as bacc
    from concourse.bass_utils import run_bass_kernel_spmd

    arrays = layout(np, inputs)
    nc = bacc.Bacc("TRN2", target_bir_lowering=False, num_devices=1)
    arg = {n: nc.dram_tensor(f"in_{n}", a.shape, mybir.dt.from_np(a.dtype), kind="ExternalInput").ap()
           for n, a in arrays.items()}
    arg["out"] = nc.dram_tensor("out_0", (T, D), F32, kind="ExternalOutput").ap()
    program(nc, arg)
    r = run_bass_kernel_spmd(nc, [{f"in_{n}": a for n, a in arrays.items()}], core_ids=[0])
    return r.results[0]["out_0"].reshape(1, T, D)


def layout(np, inputs):
    a = {n: np.asarray(v) for n, v in inputs.items()}

    def cut(m):
        m = m.reshape(*m.shape[:-2], m.shape[-2] // P, P, m.shape[-1])
        return np.ascontiguousarray(np.swapaxes(m, -3, -2))

    def turned(m):
        return cut(np.swapaxes(m, -1, -2))

    def column(v):
        return np.ascontiguousarray(v.reshape(KD, P).T)

    out = {"x": cut(a["x"][0]), "xT": turned(a["x"][0]), "ctxT": turned(a["ctx_1024"][0]),
           "mask": np.ascontiguousarray(a["mask_BxS2_if1"][0])}
    for n, k in (("q", "q"), ("k", "k"), ("v", "v"), ("o", "o")):
        out["w" + n] = turned(a[f"L0_attn_W{k}"])
        out["cw" + n] = turned(a[f"L0_xattn_W_{k}"])
        out["b" + n] = a[f"L0_attn_b{k}"]
        out["cb" + n] = a[f"L0_xattn_b_{k}"]
        if n in "qk":
            out["b" + n], out["cb" + n] = column(out["b" + n]), column(out["cb" + n])
    out["gate"] = turned(a["L0_ffn_gate_w"])
    for n, k in (("wg", "Wg"), ("wu", "Wu"), ("wd", "Wd"), ("sg", "Sg"), ("su", "Su"), ("sd", "Sd")):
        out[n] = turned(a[f"L0_ffn_{k}"])
    return out
```

```python
from contextlib import ExitStack

import concourse.bass as bass
from concourse import mybir

F32 = mybir.dt.float32
BF16 = mybir.dt.bfloat16
I32 = mybir.dt.int32
U32 = mybir.dt.uint32
ACT = mybir.ActivationFunctionType
ALU = mybir.AluOpType
AX = mybir.AxisListType
ds = bass.ds

P = 128
T = 2048
D = 256
KD = D // P
NT = T // P
S2 = 1601
H = 16
HD = D // H
NKT = -(-S2 // P)
LASTK = S2 - (NKT - 1) * P
E = 16
CAP = T * 2 // E
CT = CAP // P
FI = 1024
FT = FI // P
FS = 512
ST = FS // P
EPS = 1e-5
BLK = 512
NB = T // BLK
QT = BLK // P
G = 4
NG = H // G
VW = 32
NEG = 1.0e9

Q_PARTS = (0, 0, 1, 1, 0, 2)
K_PARTS = (0, 1, 0, 1, 2, 0)
R_MASK = HD * len(Q_PARTS)
R_MAX = R_MASK + 3
R_ALL = R_MAX + 3


class Shared:
    pass


def chain(engine, sem, before=0):
    done = [0]

    def link(ins):
        done[0] += 1
        ins.then_inc(sem, 1)
        engine.wait_ge(sem, before + done[0])

    link.done = done
    return link


def identity(nc, pool, tile, sem, before):
    pool.memset(tile[:, :], 0.0).then_inc(sem, 1)
    pool.wait_ge(sem, before + 1)
    pool.affine_select(out=tile[:, :], in_=tile[:, :], compare_op=ALU.not_equal, fill=1.0, base=0,
                       pattern=[[-1, P]], channel_multiplier=1).then_inc(sem, 1)


def project_inputs(nc, s):
    with ExitStack() as ctx:
        def sb(name, shape, dt=F32):
            return ctx.enter_context(nc.sbuf_tensor(name, shape, dt))

        def sem(name):
            return ctx.enter_context(nc.semaphore(name))

        xT = sb("xT", [P, KD, T])
        ctxT = sb("ctxT", [P, KD, S2])
        w = {n: sb(f"w_{n}", [P, KD, D]) for n in ("q", "k", "v", "ck", "cv")}
        b_col = {n: sb(f"bcol_{n}", [P, KD]) for n in ("q", "k", "ck")}
        b_row = {n: sb(f"brow_{n}", [P, D]) for n in ("v", "cv", "o")}
        mask_i = sb("mask_i", [P, S2], I32)
        keep_key = sb("keep_key", [P, S2])
        ck = sb("ck", [P, S2])
        space = s.k_stack_space

        def scratch(at, words):
            return space[:, 2 * at:2 * (at + words)]

        W3 = (3 * S2 + 1) // 2
        part = scratch(0, W3)[:, 0:3 * S2].rearrange("p (c n) -> p c n", c=3)
        mask_part = scratch(W3, 2 * W3)[0:1, 0:6 * S2].rearrange("p (c n) -> p c n", c=6)
        rest = scratch(3 * W3, S2).bitcast(F32)
        mask_bias = scratch(3 * W3 + S2, S2).bitcast(F32)[0:1, :]
        pj = [ctx.enter_context(nc.psum_tensor(f"pj{i}", [P, BLK], F32)) for i in range(4)]

        loaded = {n: sem(f"loaded_{n}") for n in ("x", "ctx", "wq", "wk", "wv", "wck", "wcv", "b", "mask", "xn")}
        ready = sem("product_ready")
        taken = sem("product_taken")
        ck_ready = sem("ck_ready")
        parts_ready = sem("parts_ready")
        parts_out = sem("parts_out")
        mask_ready = sem("mask_ready")
        mask_out = sem("mask_out")
        ones_set = sem("ones_set")
        dve_step = sem("dve_step")
        block = ctx.enter_context(nc.Block())

        keys = [(a, min(BLK, S2 - a)) for a in range(0, S2, BLK)]
        groups = [("ck", h, a, n) for h in range(KD) for a, n in keys]
        groups += [("cv", j, j * P, D) for j in range(NKT)]
        groups += [(n, h, a * BLK, BLK) for n in ("q", "k") for h in range(KD) for a in range(NB)]
        groups += [("v", j, j * P, D) for j in range(NT)]

        @block.sync
        def _(sp):
            sp.dma_start(w["ck"][:, :, :], s.w_ck).then_inc(loaded["wck"], 16)
            sp.dma_start(ctxT[:, :, :], s.ctxT).then_inc(loaded["ctx"], 16)
            for n in ("q", "k", "ck"):
                sp.dma_start(b_col[n][:, :], s.b[n]).then_inc(loaded["b"], 16)
            for n in ("v", "cv", "o"):
                sp.dma_start(b_row[n][:, :], s.b[n].partition_broadcast(P)).then_inc(loaded["b"], 16)
            sp.dma_start(mask_i[:, :], s.mask.partition_broadcast(P)).then_inc(loaded["mask"], 16)
            sp.dma_start(w["cv"][:, :, :], s.w_cv).then_inc(loaded["wcv"], 16)
            sp.dma_start(w["q"][:, :, :], s.w_q).then_inc(loaded["wq"], 16)
            sp.dma_start(xT[:, :, :], s.xT).then_inc(loaded["x"], 16)
            sp.dma_start(w["k"][:, :, :], s.w_k).then_inc(loaded["wk"], 16)
            sp.dma_start(w["v"][:, :, :], s.w_v).then_inc(loaded["wv"], 16)
            sp.dma_start(s.act[:, :, :], s.x).then_inc(loaded["xn"], 16)
            sp.dma_start(s.wo[:, :, :], s.w_o).then_inc(loaded["xn"], 16)
            sp.wait_ge(mask_ready, 1)
            sp.wait_ge(ones_set, 3)
            sp.dma_start(s.mask_parts, mask_part[:, :, :]).then_inc(mask_out, 16)
            for h in range(KD):
                sp.wait_ge(parts_ready, h + 1)
                sp.dma_start(s.k_parts[:, h * P:(h + 1) * P, :].rearrange("c p n -> p c n"),
                             part[:, :, :]).then_inc(parts_out, 16)
            sp.wait_ge(parts_out, 16 * KD)
            sp.wait_ge(mask_out, 16)

        @block.gpsimd
        def _(pool):
            identity(nc, pool, s.ident, s.consts, 0)
            identity(nc, pool, s.ident_b, s.consts, 2)
            pool.memset(s.cv[:, :, :, HD:HD + 1], 1.0).then_inc(ones_set, 1)
            pool.memset(s.cv[:, :, :, HD + 1:VW], 0.0).then_inc(ones_set, 1)
            pool.memset(mask_part[:, 3:6, :], 1.0).then_inc(ones_set, 1)
            pool.wait_ge(ones_set, 3)

        @block.tensor
        def _(pe):
            seen = set()
            for n, (kind, i, a, cols) in enumerate(groups):
                for need in {"ck": ("wck", "ctx"), "cv": ("wcv",), "q": ("wq", "x"), "k": ("wk",), "v": ("wv",)}[kind]:
                    if need not in seen:
                        pe.wait_ge(loaded[need], 16)
                        seen.add(need)
                if n >= 4:
                    pe.wait_ge(taken, n - 3)
                src = ctxT if kind in ("ck", "cv") else xT
                for k in range(KD):
                    if kind in ("cv", "v"):
                        rows = min(P, src.shape[2] - a)
                        out, lhsT, rhs = pj[n % 4][0:rows, 0:D], src[:, k, a:a + rows], w[kind][:, k, :]
                    else:
                        out, lhsT, rhs = pj[n % 4][:, 0:cols], w[kind][:, k, i * P:(i + 1) * P], src[:, k, a:a + cols]
                    mm = pe.matmul(out, lhsT, rhs, start=(k == 0), stop=(k == KD - 1))
                mm.then_inc(ready, 1)

        @block.scalar
        def _(act):
            act.wait_ge(loaded["b"], 16 * 6)
            for n, (kind, i, a, cols) in enumerate(groups):
                if kind not in ("ck", "q", "k"):
                    continue
                act.wait_ge(ready, n + 1)
                if n:
                    act.wait_ge(taken, n)
                if kind == "ck":
                    if i and a == 0:
                        act.wait_ge(parts_ready, i)
                    out = ck[:, a:a + cols]
                else:
                    out = (s.qT if kind == "q" else s.kT)[:, i, a:a + cols]
                act.activation(out, pj[n % 4][:, 0:cols], ACT.Identity,
                               bias=b_col[kind][:, i:i + 1]).then_inc(taken, 1)

        @block.vector
        def _(dve):
            link = chain(dve, dve_step)
            dve.wait_ge(loaded["mask"], 16)
            link(dve.tensor_scalar(keep_key[:, :], mask_i[:, :], 0.0, None, ALU.not_equal))
            link(dve.tensor_scalar(mask_bias[:, :], keep_key[0:1, :], 1.0, NEG, ALU.subtract, ALU.mult))
            for c in range(3):
                link(dve.tensor_copy(mask_part[:, c, :], mask_bias[:, :]))
                if c < 2:
                    link(dve.tensor_tensor(mask_bias[:, :], mask_bias[:, :], mask_part[:, c, :], ALU.subtract))
            dve.engine_nop().then_inc(mask_ready, 1)
            dve.wait_ge(loaded["b"], 16 * 6)
            n_keys = len(keys)
            for h in range(KD):
                dve.wait_ge(taken, (h + 1) * n_keys)
                if h:
                    dve.wait_ge(parts_out, 16 * h)
                link(dve.tensor_tensor(ck[:, :], ck[:, :], keep_key[:, :], ALU.mult))
                link(dve.tensor_copy(part[:, 0, :], ck[:, :]))
                link(dve.tensor_tensor(rest[:, :], ck[:, :], part[:, 0, :], ALU.subtract))
                link(dve.tensor_copy(part[:, 1, :], rest[:, :]))
                dve.tensor_tensor(part[:, 2, :], rest[:, :], part[:, 1, :], ALU.subtract).then_inc(parts_ready, 1)
            for n, (kind, i, a, cols) in enumerate(groups):
                if kind not in ("cv", "v"):
                    continue
                dve.wait_ge(ready, n + 1)
                dve.wait_ge(taken, n)
                rows = min(P, (S2 if kind == "cv" else T) - a)
                if kind == "cv":
                    out = s.cv[0:rows, i, :, 0:HD]
                    dve.tensor_tensor(out, pj[n % 4][0:rows, 0:D].rearrange("p (h d) -> p h d", h=H),
                                      b_row["cv"][0:rows, :].rearrange("p (h d) -> p h d", h=H), ALU.add).then_inc(taken, 1)
                else:
                    dve.tensor_tensor(s.v[:, i, :], pj[n % 4][:, 0:D], b_row["v"][:, :], ALU.add).then_inc(taken, 1)
            dve.wait_ge(loaded["xn"], 32)
            dve.tensor_tensor(s.act[:, :, :], s.act[:, :, :],
                              b_row["o"][:, :].unsqueeze(1).broadcast_to([P, NT, D]), ALU.add)


def row(tile, t):
    return tile[:, ds(t, 1), :].rearrange("p o d -> p (o d)")


def norm_scale(dve, link, var, scratch, root_ready, var_ready, out):
    a, b = scratch
    link(dve.tensor_scalar(a, var, EPS, None, ALU.add))
    dve.engine_nop().then_inc(var_ready, 1)
    dve.wait_ge(root_ready, 1)
    link(dve.reciprocal(out, b))
    link(dve.tensor_tensor(b, out, out, ALU.mult))
    link(dve.tensor_tensor(b, b, a, ALU.mult))
    link(dve.tensor_scalar(b, b, -0.5, 1.5, ALU.mult, ALU.add))
    link(dve.tensor_tensor(out, out, b, ALU.mult))


def self_attention(nc, s):
    with ExitStack() as ctx:
        def sb(name, shape, dt=F32):
            return ctx.enter_context(nc.sbuf_tensor(name, shape, dt))

        def ps(name, shape, dt=F32):
            return ctx.enter_context(nc.psum_tensor(name, shape, dt))

        def sem(name):
            return ctx.enter_context(nc.semaphore(name))

        HALF = T // 2
        q_tile = sb("q_tile", [P, KD, P])
        th_half = sb("th_half", [P, T])
        th_full = sb("th_full", [P, T])
        w = sb("w", [P, T])
        probs = sb("probs", [P, T])
        probsT = sb("probsT", [P, NT, P])
        oT = sb("oT", [P, KD, P])
        neg_max = sb("neg_max", [P, 1])
        shift = sb("shift", [P, 1])
        row_sums = sb("row_sums", [P, NT])
        r_sum = sb("r_sum", [P, 1])
        stats = sb("stats", [P, 6])
        z = sb("z", [P, D])
        all_stats = sb("all_stats", [P, NT, 6])
        mvs = sb("mvs", [P, NT, 2])
        nrm = sb("nrm", [P, 3, NT])
        scores = ps("scores", [P, T])
        turned = [ps(f"turned{i}", [P, 4, P]) for i in range(2)]
        out_T = ps("out_T", [P, KD, P])
        y = ps("y", [P, D])

        q_ready = sem("q_ready")
        scores_ready = sem("scores_ready")
        th_ready = sem("th_ready")
        scores_free = sem("scores_free")
        shift_ready = sem("shift_ready")
        probs_ready = sem("probs_ready")
        turned_ready = sem("turned_ready")
        probsT_ready = sem("probsT_ready")
        outT_ready = sem("outT_ready")
        oT_ready = sem("oT_ready")
        y_ready = sem("y_ready")
        z_ready = sem("z_ready")
        w_step = sem("w_step")
        z_step = sem("z_step")
        n_step = sem("n_step")
        var_ready = sem("var_ready")
        root_ready = sem("root_ready")
        x1_ready = sem("x1_ready")
        x1T_ready = sem("x1T_ready")
        x1T_taken = sem("x1T_taken")
        k_stacked = sem("k_stacked")
        block = ctx.enter_context(nc.Block())

        @block.sync
        def _(sp):
            for j, c in enumerate(K_PARTS):
                sp.dma_start(s.k_stack[HD * j:HD * (j + 1), :, :],
                             s.k_parts[c].rearrange("(h d) n -> d h n", h=H)).then_inc(k_stacked, 16)
            for h in range(H):
                sp.dma_start(s.k_stack[R_MASK:R_ALL, h, :], s.mask_parts[0]).then_inc(k_stacked, 16)
            sp.wait_ge(k_stacked, 16 * (len(K_PARTS) + H))

        @block.gpsimd
        def _(pool):
            with pool.Fori(0, NT) as t:
                pool.wait_ge(scores_free, 2 * t + 2)
                pool.tensor_copy(q_tile[:, :, :], s.qT[:, :, ds(t * P, P)]).then_inc(q_ready, 1)

        @block.tensor
        def _(pe):
            def score_tile(t):
                pe.wait_ge(q_ready, t + 1)
                for c in range(2):
                    pe.wait_ge(scores_free, 2 * t + c + 1)
                    for b in range(2):
                        cols = slice(c * HALF + b * BLK, c * HALF + (b + 1) * BLK)
                        for k in range(KD):
                            mm = pe.matmul(scores[:, cols], q_tile[:, k, :], s.kT[:, k, cols],
                                           start=(k == 0), stop=(k == KD - 1))
                    mm.then_inc(scores_ready, 1)

            def value_tile(t):
                pe.wait_ge(probs_ready, t + 1)

                def products(g, half):
                    for j in range(4 * g, 4 * g + 4):
                        mm = pe.matmul(out_T[:, half, :], s.v[:, j, half * P:(half + 1) * P], probsT[:, j, :],
                                       start=(j == 0), stop=(j == NT - 1))
                    return mm

                for g in range(4):
                    pe.wait_ge(probsT_ready, 4 * t + g + 1)
                    for j in range(4):
                        c = 4 * g + j
                        mm = pe.transpose(turned[g % 2][:, j, :], probs[:, c * P:(c + 1) * P], s.ident[:, :])
                    mm.then_inc(turned_ready, 1)
                    if g == 1:
                        pe.wait_ge(oT_ready, t + 1)
                    if g >= 1:
                        pe.wait_ge(probsT_ready, 4 * t + g + 2)
                        products(g - 1, 0)
                pe.wait_ge(probsT_ready, 4 * t + 6)
                products(3, 0)
                for g in range(4):
                    mm = products(g, 1)
                mm.then_inc(outT_ready, 1)

            def project_tile(t):
                pe.wait_ge(oT_ready, t + 2)
                pe.wait_ge(z_ready, t + 1)
                for k in range(KD):
                    mm = pe.matmul(y[:, :], oT[:, k, :], s.wo[:, k, :], start=(k == 0), stop=(k == KD - 1))
                mm.then_inc(y_ready, 1)

            score_tile(0)
            score_tile(1)
            value_tile(0)
            with pe.Fori(2, NT) as t:
                score_tile(t)
                project_tile(t - 2)
                value_tile(t - 1)
            project_tile(NT - 2)
            value_tile(NT - 1)
            project_tile(NT - 1)

            transpose_tiles(pe, s.act, s.ident, turned, x1_ready, x1T_ready, x1T_taken)

        @block.scalar
        def _(act):
            act.sem_inc(probsT_ready, 2)
            act.sem_inc(oT_ready, 1)

            def tanhs(t):
                for c in range(2):
                    cols = slice(c * HALF, (c + 1) * HALF)
                    act.wait_ge(scores_ready, 2 * t + c + 1)
                    act.wait_ge(scores_free, 2 * t + c + 1)
                    act.activation(th_half[:, cols], scores[:, cols], ACT.Tanh, scale=0.5)
                    act.activation(th_full[:, cols], scores[:, cols], ACT.Tanh).then_inc(th_ready, 1)

            def exps(t, sums):
                act.wait_ge(shift_ready, t + 1)
                act.activation(probs[:, :], w[:, :], ACT.Exp, bias=shift[:, :], scale=0.1,
                               accum_out=sums).then_inc(probs_ready, 1)

            def evacuate(t):
                for g in range(4):
                    act.wait_ge(turned_ready, 4 * t + g + 1)
                    act.copy(probsT[:, 4 * g:4 * g + 4, :], turned[g % 2][:, :, :]).then_inc(probsT_ready, 1)
                act.wait_ge(outT_ready, t + 1)
                act.copy(oT[:, :, :], out_T[:, :, :]).then_inc(oT_ready, 1)

            tanhs(0)
            exps(0, row_sums[:, 0:1])
            with act.Fori(1, NT) as t:
                tanhs(t)
                evacuate(t - 1)
                exps(t, row_sums[:, ds(t, 1)])
            evacuate(NT - 1)

            act.wait_ge(var_ready, 1)
            act.activation(nrm[:, 1, :], nrm[:, 0, :], ACT.Sqrt).then_inc(root_ready, 1)
            take_tiles(act, s.actT, turned, x1T_ready, x1T_taken)

        @block.vector
        def _(dve):
            dve.sem_inc(scores_free, 2)
            dve.sem_inc(z_ready, 1)

            def w_tile(t, first=False):
                link = chain(dve, w_step, 3 * t)
                if not first:
                    dve.wait_ge(probs_ready, t)
                for c in range(2):
                    cols = slice(c * HALF, (c + 1) * HALF)
                    dve.wait_ge(th_ready, 2 * t + c + 1)
                    link(dve.scalar_tensor_tensor(out=th_half[:, cols], in0=th_full[:, cols], scalar=1.5,
                                                  in1=th_half[:, cols], op0=ALU.mult, op1=ALU.add))
                    dve.scalar_tensor_tensor(out=w[:, cols], in0=scores[:, cols], scalar=0.0,
                                             in1=th_half[:, cols], op0=ALU.max, op1=ALU.add).then_inc(scores_free, 1)
                dve.wait_ge(scores_free, 2 * t + 4)
                link(dve.tensor_reduce(neg_max[:, :], w[:, :], AX.X, ALU.max, negate=True))
                dve.tensor_scalar(shift[:, :], neg_max[:, :], 0.1, None, ALU.mult).then_inc(shift_ready, 1)

            def z_tile(t):
                link = chain(dve, z_step, 4 * t)
                dve.wait_ge(y_ready, t + 1)
                link(dve.reciprocal(r_sum[:, :], row_sums[:, ds(t, 1)]))
                dve.scalar_tensor_tensor(out=z[:, :], in0=y[:, :], scalar=r_sum[:, :], in1=row(s.act, t),
                                         op0=ALU.mult, op1=ALU.add).then_inc(z_ready, 1)
                dve.wait_ge(z_ready, t + 2)
                link(dve.bn_stats(stats[:, :], z[:, :]))
                link(dve.tensor_scalar(row(s.act, t), z[:, :], 1.0, None, ALU.mult))
                link(dve.tensor_scalar(row(all_stats, t), stats[:, :], 1.0, None, ALU.mult))

            w_tile(0, first=True)
            w_tile(1)
            with dve.Fori(2, NT) as t:
                w_tile(t)
                z_tile(t - 2)
            z_tile(NT - 2)
            z_tile(NT - 1)

            link = chain(dve, n_step)
            for t in range(NT):
                last = dve.bn_aggr(mvs[:, t, :], all_stats[:, t, :])
            link(last)
            norm_scale(dve, link, mvs[:, :, 1], (nrm[:, 0, :], nrm[:, 1, :]), root_ready, var_ready, nrm[:, 2, :])
            for t in range(NT):
                dve.tensor_scalar(s.act[:, t, :], s.act[:, t, :], mvs[:, t, 0:1], nrm[:, 2, t:t + 1],
                                  ALU.subtract, ALU.mult).then_inc(x1_ready, 1)


def transpose_tiles(pe, src, ident, banks, src_ready, ready, taken):
    for n in range(NT // 2):
        if n >= 2:
            pe.wait_ge(taken, n - 1)
        pe.wait_ge(src_ready, 2 * n + 2)
        for k in range(KD):
            for j in range(2):
                mm = pe.transpose(banks[n % 2][:, 2 * k + j, :], src[:, 2 * n + j, k * P:(k + 1) * P], ident[:, :])
        mm.then_inc(ready, 1)


def take_tiles(act, dst, banks, ready, taken):
    for n in range(NT // 2):
        act.wait_ge(ready, n + 1)
        act.copy(dst[:, :, 2 * n * P:(2 * n + 2) * P],
                 banks[n % 2][:, :, :].rearrange("p (k c) d -> p k (c d)", k=KD)).then_inc(taken, 1)


def cross_attention(nc, s):
    with ExitStack() as ctx:
        s.q_stack = ctx.enter_context(nc.sbuf_tensor("q_stack", [P, NB * NG, G, BLK], BF16))
        stack_queries(nc, s)
        s.ctx = s.actT[:, :, :].rearrange("p k t -> p (k t)").rearrange("p (t d) -> p t d", t=NT)
        attend(nc, s)
    cross_output(nc, s)


def stack_queries(nc, s):
    with ExitStack() as ctx:
        def sb(name, shape, dt=F32):
            return ctx.enter_context(nc.sbuf_tensor(name, shape, dt))

        def sem(name):
            return ctx.enter_context(nc.semaphore(name))

        QSCALE = float(HD) ** -0.5
        w = sb("w_cq", [P, KD, D])
        b = sb("b_cq", [P, KD])
        q = sb("cq", [P, 2, KD, BLK])
        rest = sb("cq_rest", [P, KD, BLK])
        part = sb("cq_part", [P, 2, 3, KD, BLK], BF16)
        pq = [ctx.enter_context(nc.psum_tensor(f"pq{i}", [P, KD, BLK], F32)) for i in range(2)]
        loaded = sem("cq_loaded")
        b_scaled = sem("cq_b_scaled")
        ready = sem("cq_product")
        scaled = sem("cq_scaled")
        split = sem("cq_split")
        parts_out = [sem(f"cq_parts_out{i}") for i in range(NB)]
        stacked = sem("cq_stacked")
        ones = sem("cq_ones")
        step = sem("cq_step")
        block = ctx.enter_context(nc.Block())

        @block.sync
        def _(sp):
            sp.dma_start(w[:, :, :], s.w_cq).then_inc(loaded, 16)
            sp.dma_start(b[:, :], s.b["cq"]).then_inc(loaded, 16)
            for n in range(NB):
                sp.wait_ge(split, n + 1)
                for c in range(3):
                    sp.dma_start(s.q_parts[c, :, n * BLK:(n + 1) * BLK].rearrange("(k p) t -> p k t", p=P),
                                 part[:, n % 2, c, :, :]).then_inc(parts_out[n], 16)
            sp.wait_ge(parts_out[NB - 1], 48)

        @block.gpsimd
        def _(pool):
            pool.memset(s.q_stack[R_MASK:R_ALL, 0:NB * NG // 2, :, :], 1.0).then_inc(ones, 1)
            pool.wait_ge(ones, 1)
            for n in range(NB):
                pool.wait_ge(parts_out[n], 48)
                for j, c in enumerate(Q_PARTS):
                    pool.dma_start(s.q_stack[HD * j:HD * (j + 1), NG * n:NG * (n + 1), :, :].rearrange("p g h t -> p (g h) t"),
                                   s.q_parts[c, :, n * BLK:(n + 1) * BLK].rearrange("(h d) t -> d h t", h=H)).then_inc(stacked, 16)
            pool.wait_ge(stacked, 16 * NB * len(Q_PARTS))

        @block.tensor
        def _(pe):
            pe.wait_ge(loaded, 32)
            for n in range(NB):
                if n >= 2:
                    pe.wait_ge(scaled, n - 1)
                for half in range(KD):
                    for k in range(KD):
                        mm = pe.matmul(pq[n % 2][:, half, :], w[:, k, half * P:(half + 1) * P],
                                       s.actT[:, k, n * BLK:(n + 1) * BLK], start=(k == 0), stop=(k == KD - 1))
                mm.then_inc(ready, 1)

        @block.scalar
        def _(act):
            act.wait_ge(b_scaled, 1)
            for n in range(NB):
                act.wait_ge(ready, n + 1)
                if n >= 2:
                    act.wait_ge(split, n - 1)
                for half in range(KD):
                    ins = act.activation(q[:, n % 2, half, :], pq[n % 2][:, half, :], ACT.Identity,
                                         bias=b[:, half:half + 1], scale=QSCALE)
                ins.then_inc(scaled, 1)

        @block.vector
        def _(dve):
            dve.memset(s.q_stack[R_MASK:R_ALL, NB * NG // 2:, :, :], 1.0)
            dve.wait_ge(loaded, 32)
            dve.tensor_scalar(b[:, :], b[:, :], QSCALE, None, ALU.mult).then_inc(b_scaled, 1)
            link = chain(dve, step)
            for n in range(NB):
                dve.wait_ge(scaled, n + 1)
                if n >= 2:
                    dve.wait_ge(parts_out[n - 2], 48)
                src, out = q[:, n % 2, :, :], part[:, n % 2, :, :, :]
                link(dve.tensor_copy(out[:, 0], src))
                link(dve.tensor_tensor(rest[:, :, :], src, out[:, 0], ALU.subtract))
                link(dve.tensor_copy(out[:, 1], rest[:, :, :]))
                dve.tensor_tensor(out[:, 2], rest[:, :, :], out[:, 1], ALU.subtract).then_inc(split, 1)


def ring_entries(it, static):
    NIT = NB * NG
    entries = [("chunk", c) for c in range(2 * QT * G)] if static + 2 < NIT else []
    if static >= 1:
        entries.insert(5, ("context", it - 1))
    if static + 1 < NIT:
        entries.insert(11, ("rows", it + 1))
    return entries


def attend(nc, s):
    with ExitStack() as ctx:
        def sb(name, shape, dt=F32):
            return ctx.enter_context(nc.sbuf_tensor(name, shape, dt))

        def ps(name, shape, dt=F32):
            return ctx.enter_context(nc.psum_tensor(name, shape, dt))

        def sem(name):
            return ctx.enter_context(nc.semaphore(name))

        NIT = NB * NG
        HALF_KEYS = -(-S2 // 2)
        CHUNKS = ((0, HALF_KEYS), (HALF_KEYS, S2))
        NCH = 2 * QT * G
        STEPS = NKT
        E_IT = STEPS * G
        SLOTS = 3 * STEPS
        RING0 = 2 * NCH + 1
        RING1 = RING0 + NCH + 1
        R_IT = NCH + 2
        LAST = NG * (NB - 1) + 1

        probs = sb("xprobs", [P, 2, G, BLK])
        out_sb = sb("xout_sb", [P, BLK])
        chunk_max = sb("chunk_max", [P, 2, QT, G])
        max_rest = sb("max_rest", [P, 2, QT, G])
        max_part = sb("max_part", [P, QT, 3 * G], BF16)
        max_rows = sb("max_rows", [3 * G, QT, P], BF16)
        r_den = sb("r_den", [P, QT, G])
        a_ps = [ps(f"a_ps{i}", [P, 2 * BLK]) for i in range(2)]
        e_ps = [ps(f"e_ps{i}", [P, BLK]) for i in range(3)]
        o_ps = ps("o_ps", [P, BLK])
        turned = [a[:, 0:QT * P].rearrange("p (q c) -> p q c", q=QT) for a in a_ps]
        rows_ps = [a[:, 0:QT * P // 2].bitcast(BF16)[0:3 * G, :].rearrange("p (q c) -> p q c", q=QT) for a in a_ps]

        ring_ready = sem("ring_ready")
        ring_free = sem("ring_free")
        max_split = sem("max_split")
        rows_in = sem("rows_in")
        s_ready = sem("s_ready")
        exp_done = sem("exp_done")
        pv_done = sem("pv_done")
        out_taken = sem("out_taken")
        rows_taken = sem("rows_taken")
        m_step = sem("m_step")
        c_step = sem("c_step")
        block = ctx.enter_context(nc.Block())

        def ring_base(it, static):
            if static == 0:
                return RING0
            if static <= LAST:
                return RING1 + R_IT * (it - 1)
            return RING1 + R_IT * (LAST - 1) + sum(len(ring_entries(i, i)) for i in range(LAST, static))

        def run(engine, iteration):
            iteration(0, 0)
            with engine.Fori(0, NB - 1) as r:
                for g in range(1, NG + 1):
                    iteration(NG * r + g, g)
            for it in range(LAST, NIT):
                iteration(it, it)

        @block.sync
        def _(sp):
            with sp.Fori(0, NIT) as it:
                sp.wait_ge(rows_taken, it + 1)
                for c in range(3):
                    sp.dma_start(s.q_stack[R_MAX + c:R_MAX + c + 1, ds(it, 1), :, :].rearrange("p o h t -> p o (h t)"),
                                 max_rows[G * c:G * (c + 1), :, :]).then_inc(rows_in, 16)
            sp.wait_ge(rows_in, 48 * NIT)

        @block.tensor
        def _(pe):
            def max_chunk(it, g, c, at, bank):
                qt, h, half = c // (2 * G), c // 2 % G, c % 2
                a, b = CHUNKS[half]
                pe.wait_ge(ring_free, at + 1)
                for k in range(a, b, BLK):
                    n = min(BLK, b - k)
                    mm = pe.matmul(a_ps[bank][:, k - a:k - a + n],
                                   s.q_stack[0:R_MAX, ds(it, 1), h, qt * P:(qt + 1) * P].rearrange("p o t -> p (o t)"),
                                   s.k_stack[0:R_MAX, G * g + h, k:k + n], start=True, stop=True)
                mm.then_inc(ring_ready, 1)

            def turn_rows(it, at, bank):
                pe.wait_ge(max_split, it + 1)
                pe.wait_ge(ring_free, at + 1)
                for qt in range(QT):
                    mm = pe.transpose(rows_ps[bank][:, qt, :], max_part[:, qt, :], s.ident_b[:, :])
                mm.then_inc(ring_ready, 1)

            def turn_context(it, at, bank):
                pe.wait_ge(out_taken, it + 2)
                pe.wait_ge(ring_free, at + 1)
                for qt in range(QT):
                    mm = pe.transpose(turned[bank][:, qt, :], out_sb[:, qt * P:(qt + 1) * P], s.ident[:, :])
                mm.then_inc(ring_ready, 1)

            def values(it, g, j):
                rows = P if j < NKT - 1 else LASTK
                if j == 0:
                    pe.wait_ge(out_taken, it + 1)
                for h in range(G):
                    pe.wait_ge(exp_done, E_IT * it + G * j + h + 4)
                    mm = pe.matmul(o_ps[VW * h:VW * (h + 1), :], s.cv[0:rows, j, G * g + h, :],
                                   probs[0:rows, (g * STEPS + j) % 2, h, :], start=(j == 0), stop=(j == NKT - 1))
                mm.then_inc(pv_done, 1)

            def score_tile(it, g, j, h):
                rows, n = P if j < NKT - 1 else LASTK, G * j + h
                pe.wait_ge(exp_done, E_IT * it + (n + 1 if n >= 3 else (3, 1, 2)[n]))
                pe.matmul(e_ps[n % 3][0:rows, :], s.k_stack[0:R_ALL, G * g + h, j * P:j * P + rows],
                          s.q_stack[0:R_ALL, ds(it, 1), h, :].rearrange("p o t -> p (o t)"),
                          start=True, stop=True).then_inc(s_ready, 1)

            def iteration(it, static):
                g = static % NG
                base, even = ring_base(it, static), ring_base(static, static)
                entries = ring_entries(it, static)
                slots = [None] * SLOTS
                for k, entry in enumerate(entries):
                    slots[k * SLOTS // R_IT if len(entries) > 2 else 6 * (k + 1)] = (k, entry)

                def ring(slot):
                    if slots[slot] is None:
                        return
                    k, (kind, what) = slots[slot]
                    if kind == "chunk":
                        max_chunk(it + 2, (g + 2) % NG, what, base + k, (even + k) % 2)
                    elif kind == "rows":
                        turn_rows(what, base + k, (even + k) % 2)
                    else:
                        turn_context(what, base + k, (even + k) % 2)

                pe.wait_ge(rows_in, 48 * (it + 1))
                for j in range(STEPS):
                    ring(3 * j)
                    if j:
                        values(it, g, j - 1)
                    elif static:
                        values(it - 1, (g - 1) % NG, STEPS - 1)
                    ring(3 * j + 1)
                    score_tile(it, g, j, 0)
                    score_tile(it, g, j, 1)
                    ring(3 * j + 2)
                    score_tile(it, g, j, 2)
                    score_tile(it, g, j, 3)

            for it in range(2):
                for c in range(NCH):
                    max_chunk(it, it, c, (NCH + 1) * it + c, ((NCH + 1) * it + c) % 2)
                if it == 0:
                    turn_rows(0, NCH, NCH % 2)
            run(pe, iteration)
            values(NIT - 1, NG - 1, STEPS - 1)
            end = ring_base(NIT, NIT)
            turn_context(NIT - 1, end, end % 2)

        @block.scalar
        def _(act):
            act.sem_inc(exp_done, 3)
            act.sem_inc(out_taken, 1)

            def take_outputs(it):
                act.wait_ge(pv_done, STEPS * (it + 1) + 2)
                act.copy(out_sb[:, :], o_ps[:, :]).then_inc(out_taken, 1)

            def iteration(it, static):
                if static:
                    take_outputs(it - 1)
                for j in range(STEPS):
                    rows = P if j < NKT - 1 else LASTK
                    act.wait_ge(pv_done, STEPS * it + j + 1)
                    for h in range(G):
                        n = G * j + h
                        act.wait_ge(s_ready, E_IT * it + n + 1)
                        act.activation(probs[0:rows, (static * STEPS + j) % 2, h, :], e_ps[n % 3][0:rows, :],
                                       ACT.Exp).then_inc(exp_done, 1)

            run(act, iteration)
            take_outputs(NIT - 1)

        @block.vector
        def _(dve):
            dve.sem_inc(ring_free, 2)
            dve.sem_inc(pv_done, 2)

            def take_chunk(c, at, bank):
                qt, h, half = c // (2 * G), c // 2 % G, c % 2
                a, b = CHUNKS[half]
                dve.wait_ge(ring_ready, at + 1)
                dve.tensor_reduce(chunk_max[:, half, qt, h:h + 1], a_ps[bank][:, 0:b - a], AX.X,
                                  ALU.max).then_inc(ring_free, 1)

            def split_maxima(it, taken):
                link = chain(dve, m_step, 4 * it)
                dve.wait_ge(ring_free, taken + 2)
                m, rest = max_rest[:, 0, :, :], max_rest[:, 1, :, :]
                link(dve.tensor_tensor(m, chunk_max[:, 0, :, :], chunk_max[:, 1, :, :], ALU.max))
                link(dve.tensor_scalar(max_part[:, :, 0:G], m, -1.0, None, ALU.mult))
                link(dve.scalar_tensor_tensor(out=rest, in0=m, scalar=-1.0, in1=max_part[:, :, 0:G],
                                              op0=ALU.mult, op1=ALU.subtract))
                link(dve.tensor_copy(max_part[:, :, G:2 * G], rest))
                dve.tensor_tensor(max_part[:, :, 2 * G:3 * G], rest, max_part[:, :, G:2 * G],
                                  ALU.subtract).then_inc(max_split, 1)

            def take_rows(it, at, bank, first=False):
                dve.wait_ge(ring_ready, at + 1)
                if not first:
                    dve.wait_ge(rows_in, 48 * it)
                dve.tensor_copy(max_rows[:, :, :], rows_ps[bank]).then_inc(rows_taken, 1)
                dve.wait_ge(rows_taken, it + 1)
                dve.sem_inc(ring_free, 1)

            def take_context(it, static, at, bank):
                link = chain(dve, c_step, it)
                dve.wait_ge(ring_ready, at + 1)
                dve.wait_ge(ring_free, at + 2)
                heads = turned[bank].rearrange("p q (h v) -> p q h v", h=G)
                link(dve.reciprocal(r_den[:, :, :], heads[:, :, :, HD]))
                g = static % NG
                block_at = (it - g) * (QT // NG)
                dve.tensor_tensor(s.ctx[:, ds(block_at, QT), G * HD * g:G * HD * (g + 1)].rearrange("p q (h d) -> p q h d", h=G),
                                  heads[:, :, :, 0:HD], r_den[:, :, :].unsqueeze(3).broadcast_to([P, QT, G, HD]),
                                  ALU.mult).then_inc(ring_free, 1)

            def iteration(it, static):
                base, even = ring_base(it, static), ring_base(static, static)
                entries = ring_entries(it, static)
                for k, (kind, what) in enumerate(entries):
                    if kind == "chunk":
                        take_chunk(what, base + k, (even + k) % 2)
                    elif kind == "rows":
                        take_rows(what, base + k, (even + k) % 2)
                    else:
                        take_context(what, static - 1, base + k, (even + k) % 2)
                if static + 2 < NIT:
                    split_maxima(it + 2, base + len(entries))

            for it in range(2):
                for c in range(NCH):
                    take_chunk(c, (NCH + 1) * it + c, ((NCH + 1) * it + c) % 2)
                split_maxima(it, (NCH + 1) * it + NCH)
                if it == 0:
                    take_rows(0, NCH, NCH % 2, first=True)
            run(dve, iteration)
            end = ring_base(NIT, NIT)
            take_context(NIT - 1, NIT - 1, end, end % 2)


def cross_output(nc, s):
    with ExitStack() as ctx:
        def sb(name, shape, dt=F32):
            return ctx.enter_context(nc.sbuf_tensor(name, shape, dt))

        def sem(name):
            return ctx.enter_context(nc.semaphore(name))

        w = sb("w_co", [P, KD, D])
        b = sb("b_co", [P, D])
        turned_sb = sb("ctxT_sb", [P, 2, KD, P])
        all_stats = sb("all_stats2", [P, NT, 6])
        mvs = sb("mvs2", [P, NT, 2])
        nrm = sb("nrm2", [P, 3, NT])
        turned = [ctx.enter_context(nc.psum_tensor(f"ctxT{i}", [P, KD, P], F32)) for i in range(2)]
        y = [ctx.enter_context(nc.psum_tensor(f"y2{i}", [P, D], F32)) for i in range(2)]
        banks = [ctx.enter_context(nc.psum_tensor(f"x2T{i}", [P, 4, P], F32)) for i in range(2)]
        loaded = sem("co_loaded")
        turned_ready = sem("co_turned")
        turned_taken = sem("co_taken")
        y_ready = sem("co_y")
        z_ready = sem("co_z")
        biased = sem("co_biased")
        step = sem("co_step")
        var_ready, root_ready = sem("var_ready2"), sem("root_ready2")
        x2_ready, x2T_ready, x2T_taken = sem("x2_ready"), sem("x2T_ready"), sem("x2T_taken")
        block = ctx.enter_context(nc.Block())

        @block.sync
        def _(sp):
            sp.dma_start(w[:, :, :], s.w_co).then_inc(loaded, 16)
            sp.dma_start(b[:, :], s.b["co"].partition_broadcast(P)).then_inc(loaded, 16)

        @block.tensor
        def _(pe):
            pe.wait_ge(loaded, 32)
            for t in range(NT + 1):
                if t < NT:
                    if t >= 2:
                        pe.wait_ge(turned_taken, t - 1)
                    for k in range(KD):
                        mm = pe.transpose(turned[t % 2][:, k, :], s.ctx[:, t, k * P:(k + 1) * P], s.ident[:, :])
                    mm.then_inc(turned_ready, 1)
                if t:
                    u = t - 1
                    pe.wait_ge(turned_taken, u + 1)
                    if u >= 2:
                        pe.wait_ge(z_ready, u - 1)
                    for k in range(KD):
                        mm = pe.matmul(y[u % 2][:, :], turned_sb[:, u % 2, k, :], w[:, k, :], start=(k == 0), stop=(k == KD - 1))
                    mm.then_inc(y_ready, 1)
            transpose_tiles(pe, s.act, s.ident, banks, x2_ready, x2T_ready, x2T_taken)

        @block.scalar
        def _(act):
            for t in range(NT):
                act.wait_ge(turned_ready, t + 1)
                if t >= 2:
                    act.wait_ge(y_ready, t - 1)
                act.copy(turned_sb[:, t % 2, :, :], turned[t % 2][:, :, :]).then_inc(turned_taken, 1)
            act.wait_ge(var_ready, 1)
            act.activation(nrm[:, 1, :], nrm[:, 0, :], ACT.Sqrt).then_inc(root_ready, 1)
            take_tiles(act, s.actT, banks, x2T_ready, x2T_taken)

        @block.vector
        def _(dve):
            link = chain(dve, step)
            dve.wait_ge(loaded, 32)
            link(dve.tensor_tensor(s.act[:, :, :], s.act[:, :, :],
                                   b[:, :].unsqueeze(1).broadcast_to([P, NT, D]), ALU.add))
            for t in range(NT):
                dve.wait_ge(y_ready, t + 1)
                dve.tensor_tensor(s.act[:, t, :], y[t % 2][:, :], s.act[:, t, :], ALU.add).then_inc(z_ready, 1)
                dve.wait_ge(z_ready, t + 1)
                link(dve.bn_stats(all_stats[:, t, :], s.act[:, t, :]))
            for t in range(NT):
                last = dve.bn_aggr(mvs[:, t, :], all_stats[:, t, :])
            link(last)
            norm_scale(dve, link, mvs[:, :, 1], (nrm[:, 0, :], nrm[:, 1, :]), root_ready, var_ready, nrm[:, 2, :])
            for t in range(NT):
                dve.tensor_scalar(s.act[:, t, :], s.act[:, t, :], mvs[:, t, 0:1], nrm[:, 2, t:t + 1],
                                  ALU.subtract, ALU.mult).then_inc(x2_ready, 1)


def route(nc, s):
    with ExitStack() as ctx:
        def sb(name, shape, dt=F32):
            return ctx.enter_context(nc.sbuf_tensor(name, shape, dt))

        def ps(name, shape, dt=F32):
            return ctx.enter_context(nc.psum_tensor(name, shape, dt))

        def sem(name):
            return ctx.enter_context(nc.semaphore(name))

        R = 16
        SPREAD = R // CT
        SEARCH = 8
        TOP_BIT = 1 << 30
        NONE = 2 * CAP

        gate = sb("gate", [P, KD, E])
        sg, su = sb("sg", [P, KD, FS]), sb("su", [P, KD, FS])
        sd = sb("sd", [P, ST, D])
        gelu = sb("s_gelu", [P, 2, BLK])
        up = sb("s_up", [P, 2, BLK])
        hidden = sb("s_hidden", [P, ST, BLK])
        down = sb("s_down", [P, QT, D])
        probs = sb("gate_probs", [P, NT, E])
        stat = sb("gate_stat", [P, 2, NT])
        ones = sb("ones_b", [P, P], BF16)
        upto = sb("upto_b", [P, P], BF16)
        spread = sb("spread", [R, SPREAD, P])
        digits_i = sb("digits_i", [P, R], I32)
        digits = sb("digits", [P, R])
        number_i = sb("number_i", [P, NT], I32)
        number = sb("number", [P, NT])
        at_least = sb("at_least", [P, NT, E], BF16)
        bit = sb("bit", [P, E], I32)
        thr = sb("thr", [P, E], I32)
        cand = sb("cand", [P, E], I32)
        inc = sb("inc", [P, E], I32)
        count = sb("count", [P, E])
        above = sb("above", [P, 2, NT, E], BF16)
        need = sb("need", [P, E])
        place = sb("place", [P, NT, E])
        chosen = sb("chosen", [P, NT, E])
        place_i = sb("place_i", [P, NT, E], I32)
        digit_i = sb("digit_i", [P, 2, NT, E], I32)
        low_hot = sb("low_hot", [P, NT, E, R], mybir.dt.float16)
        high_hot = sb("high_hot", [P, NT, E, R], mybir.dt.float16)
        lists = sb("lists", [R, E, R])
        logit_ps = ps("logit_ps", [P, NT, E])
        count_ps = ps("count_ps", [P, NT, E])
        place_ps = ps("place_ps", [P, 2, NT, E])
        g_ps = [ps(f"g_ps{i}", [P, BLK]) for i in range(2)]
        u_ps = [ps(f"u_ps{i}", [P, BLK]) for i in range(2)]
        y_ps = ps("y_ps", [P, D])

        loaded = sem("r_loaded")
        x2_out = sem("x2_out")
        scores_out = sem("scores_out")
        const_step = sem("const_step")
        logits_ready = sem("logits_ready")
        shifted = sem("logits_shifted")
        exp_ready = sem("gate_exp")
        probs_ready = sem("gate_probs_ready")
        compared = sem("compared")
        counted = sem("counted")
        split = sem("split")
        placed = sem("placed")
        low_ready = sem("low_ready")
        lists_taken = sem("lists_taken")
        gu_ready = sem("s_gu_ready")
        gu_taken = sem("s_gu_taken")
        h_ready = sem("s_h_ready")
        y_ready = sem("s_y_ready")
        y_taken = sem("s_y_taken")
        acc_ready = sem("acc_ready")
        acc_out = sem("acc_out")
        tick = sem("r_tick")
        step = sem("r_step")
        search_step = sem("search_step")
        block = ctx.enter_context(nc.Block())
        rows = lambda ap: ap.rearrange("(t p) d -> p t d", p=P)

        @block.sync
        def _(sp):
            sp.dma_start(gate[:, :, :], s.gate_w).then_inc(loaded, 16)
            sp.dma_start(sg[:, :, :], s.s_gate).then_inc(loaded, 16)
            sp.dma_start(su[:, :, :], s.s_up).then_inc(loaded, 16)
            sp.dma_start(sd[:, :, :], s.s_down).then_inc(loaded, 16)
            sp.dma_start(rows(s.x2)[:, :, 0:D], s.act[:, :, :]).then_inc(x2_out, 16)
            for e in range(2):
                load_expert(sp, s, e, e)
            sp.wait_ge(probs_ready, 1)
            sp.dma_start(rows(s.x2)[:, :, D:D + E], probs[:, :, :]).then_inc(scores_out, 16)
            with sp.Fori(0, NB) as n:
                sp.wait_ge(acc_ready, n + 2)
                sp.dma_start(rows(s.acc)[:, ds(QT * n, QT), :], s.act[:, ds(QT * n, QT), :]).then_inc(acc_out, 16)
            sp.wait_ge(acc_out, 16 * NB)
            sp.wait_ge(scores_out, 16)

        @block.gpsimd
        def _(pool):
            link = chain(pool, const_step)
            pool.memset(ones[:, :], 1.0)
            pool.memset(spread[:, :, :], 0.0)
            pool.iota(digits_i[:, :], pattern=[[1, R]], base=0, channel_multiplier=0)
            link(pool.iota(number_i[:, :], pattern=[[P, NT]], base=0, channel_multiplier=1))
            pool.affine_select(out=upto[:, :], in_=ones[:, :], compare_op=ALU.is_ge, fill=0.0, base=0,
                               pattern=[[1, P]], channel_multiplier=-1)
            pool.affine_select(out=spread[:, :, :], in_=spread[:, :, :], compare_op=ALU.not_equal, fill=1.0,
                               base=0, pattern=[[-1, SPREAD], [1, P]], channel_multiplier=-SPREAD)
            pool.tensor_copy(digits[:, :], digits_i[:, :])
            link(pool.tensor_copy(number[:, :], number_i[:, :]))
            pool.sem_inc(h_ready, 2)
            pool.sem_inc(acc_ready, 1)
            with pool.Fori(0, NB) as n:
                for i in range(ST):
                    pool.wait_ge(gu_taken, ST * n + i + 3)
                    pool.tensor_tensor(hidden[:, i, :], gelu[:, i % 2, :], up[:, i % 2, :], ALU.mult).then_inc(h_ready, 1)
                pool.wait_ge(y_taken, QT * n + QT + 1)
                pool.sem_inc(tick, 1)
                pool.wait_ge(x2_out, 16)
                at = s.act[:, ds(QT * n, QT), :]
                pool.tensor_tensor(at, at, down[:, :, :], ALU.add).then_inc(acc_ready, 1)

        @block.tensor
        def _(pe):
            pe.wait_ge(loaded, 64)
            for t in range(NT):
                for k in range(KD):
                    mm = pe.matmul(logit_ps[:, t, :], s.actT[:, k, t * P:(t + 1) * P], gate[:, k, :],
                                   start=(k == 0), stop=(k == KD - 1))
            mm.then_inc(logits_ready, 1)
            pe.wait_ge(const_step, 2)

            def count_step(n, k):
                pe.wait_ge(compared, SEARCH * n + k + 1)
                pe.matmul(count_ps[:, :, :], ones[:, :], at_least[:, :, :], start=True, stop=True).then_inc(counted, 1)

            with pe.Fori(0, NB) as n:
                for i in range(ST):
                    pe.wait_ge(gu_taken, ST * n + i + 1)
                    for out, weight in ((g_ps, sg), (u_ps, su)):
                        for k in range(KD):
                            mm = pe.matmul(out[i % 2][:, :], weight[:, k, i * P:(i + 1) * P],
                                           s.actT[:, k, ds(n * BLK, BLK)], start=(k == 0), stop=(k == KD - 1))
                    mm.then_inc(gu_ready, 1)
                    count_step(n, i)
                for q in range(QT):
                    pe.wait_ge(y_taken, QT * n + q + 1)
                    for i in range(ST):
                        pe.wait_ge(h_ready, ST * n + i + 3)
                        mm = pe.matmul(y_ps[:, :], hidden[:, i, q * P:(q + 1) * P], sd[:, i, :],
                                       start=(i == 0), stop=(i == ST - 1))
                    mm.then_inc(y_ready, 1)
                    count_step(n, ST + q)

            pe.wait_ge(split, 1)
            for a in range(2):
                pe.matmul(place_ps[:, a, :, :], upto[:, :], above[:, a, :, :], start=True, stop=False)
                for j in range(NT - 1):
                    pe.matmul(place_ps[:, a, j + 1:NT, :], ones[:, :],
                              above[:, a, j:j + 1, :].broadcast_to([P, NT - 1 - j, E]), start=False, stop=(j == NT - 2))
            for j in range(NT):
                mm = pe.matmul(count_ps[:, 0, :], ones[:, :], above[:, 0, j, :], start=(j == 0), stop=(j == NT - 1))
            mm.then_inc(placed, 1)
            pe.wait_ge(low_ready, 1)
            for e in range(E):
                for j in range(NT):
                    mm = pe.matmul(place_ps[0:R, e // 8, 2 * (e % 8):2 * (e % 8) + 1, :].rearrange("p o r -> p (o r)"),
                                   low_hot[:, j, e, :], high_hot[:, j, e, :], start=(j == 0), stop=(j == NT - 1))
            mm.then_inc(placed, 1)
            pe.wait_ge(lists_taken, 1)
            pe.wait_ge(const_step, 2)
            by_tile = lists[:, :, :].rearrange("p e (c b) -> p (e c) b", b=SPREAD)
            for b in range(SPREAD):
                mm = pe.matmul(count_ps[:, 0:CT, :].rearrange("p c e -> p (c e)"), spread[:, b, :], by_tile[:, :, b],
                               start=(b == 0), stop=(b == SPREAD - 1))
            mm.then_inc(placed, 1)

        @block.scalar
        def _(act):
            act.sem_inc(gu_taken, 2)
            act.sem_inc(y_taken, 1)
            act.wait_ge(shifted, 1)
            act.activation(probs[:, :, :], probs[:, :, :], ACT.Exp).then_inc(exp_ready, 1)
            with act.Fori(0, NB) as n:
                for i in range(ST):
                    act.wait_ge(gu_ready, ST * n + i + 1)
                    act.wait_ge(h_ready, ST * n + i + 1)
                    act.activation(gelu[:, i % 2, :], g_ps[i % 2][:, :], ACT.Gelu)
                    act.copy(up[:, i % 2, :], u_ps[i % 2][:, :]).then_inc(gu_taken, 1)
                act.wait_ge(acc_ready, n + 1)
                for q in range(QT):
                    act.wait_ge(y_ready, QT * n + q + 1)
                    act.copy(down[:, q, :], y_ps[:, :]).then_inc(y_taken, 1)

        @block.vector
        def _(dve):
            link = chain(dve, step)
            wide = [P, NT, E]

            def over_tiles(ap):
                return ap.unsqueeze(1).broadcast_to(wide)

            dve.memset(thr[:, :], 0)
            dve.memset(bit[:, :], TOP_BIT)
            link(dve.memset(cand[:, :], TOP_BIT))
            dve.wait_ge(logits_ready, 1)
            link(dve.tensor_reduce(stat[:, 0, :], logit_ps[:, :, :], AX.X, ALU.max))
            dve.tensor_tensor(probs[:, :, :], logit_ps[:, :, :], stat[:, 0, :].unsqueeze(2).broadcast_to(wide),
                              ALU.subtract).then_inc(shifted, 1)
            dve.wait_ge(exp_ready, 1)
            link(dve.tensor_reduce(stat[:, 0, :], probs[:, :, :], AX.X, ALU.add))
            link(dve.reciprocal(stat[:, 1, :], stat[:, 0, :]))
            dve.tensor_tensor(probs[:, :, :], probs[:, :, :], stat[:, 1, :].unsqueeze(2).broadcast_to(wide),
                              ALU.mult).then_inc(probs_ready, 1)
            dve.wait_ge(probs_ready, 1)

            with dve.Fori(0, NB) as n:
                for k in range(SEARCH):
                    at = SEARCH * n + k
                    found = chain(dve, search_step, 5 * at)
                    dve.tensor_tensor(at_least[:, :, :], probs[:, :, :], over_tiles(cand[:, :].bitcast(F32)),
                                      ALU.is_ge).then_inc(compared, 1)
                    dve.wait_ge(counted, at + 1)
                    found(dve.tensor_reduce(count[:, :], count_ps[:, :, :].rearrange("p t e -> p e t"), AX.X, ALU.add))
                    found(dve.scalar_tensor_tensor(out=inc[:, :], in0=count[:, :], scalar=float(CAP), in1=bit[:, :],
                                                   op0=ALU.is_ge, op1=ALU.mult))
                    found(dve.tensor_tensor(thr[:, :], thr[:, :], inc[:, :], ALU.bitwise_or))
                    found(dve.tensor_scalar(bit[:, :], bit[:, :], 1, None, ALU.logical_shift_right))
                    found(dve.tensor_tensor(cand[:, :], thr[:, :], bit[:, :], ALU.bitwise_or))

            limit = over_tiles(thr[:, :].bitcast(F32))
            dve.tensor_tensor(above[:, 0, :, :], probs[:, :, :], limit, ALU.is_gt)
            dve.tensor_tensor(above[:, 1, :, :], probs[:, :, :], limit, ALU.is_equal).then_inc(split, 1)
            dve.wait_ge(placed, 1)
            link(dve.tensor_scalar(need[:, :], count_ps[:, 0, :], -1.0, float(CAP), ALU.mult, ALU.add))
            up_to_need = over_tiles(need[:, :])
            link(dve.tensor_tensor(chosen[:, :, :], place_ps[:, 1, :, :], up_to_need, ALU.is_le))
            link(dve.tensor_tensor(chosen[:, :, :], chosen[:, :, :], above[:, 1, :, :], ALU.mult))
            link(dve.tensor_tensor(chosen[:, :, :], chosen[:, :, :], above[:, 0, :, :], ALU.add))
            link(dve.tensor_tensor(place[:, :, :], place_ps[:, 1, :, :], up_to_need, ALU.min))
            link(dve.tensor_tensor(place[:, :, :], place_ps[:, 0, :, :], place[:, :, :], ALU.add))
            link(dve.scalar_tensor_tensor(out=place[:, :, :], in0=place[:, :, :], scalar=-1.0 - NONE, in1=chosen[:, :, :],
                                          op0=ALU.add, op1=ALU.mult))
            link(dve.tensor_scalar(place_i[:, :, :], place[:, :, :], float(NONE), None, ALU.add))
            link(dve.tensor_scalar(digit_i[:, 0, :, :], place_i[:, :, :], R - 1, None, ALU.bitwise_and))
            link(dve.tensor_scalar(digit_i[:, 1, :, :], place_i[:, :, :], R.bit_length() - 1, None, ALU.logical_shift_right))
            dve.wait_ge(const_step, 2)
            hot = [P, NT * E, R]
            flat = lambda tile: tile.rearrange("p t e r -> p (t e) r")
            for a, out in ((1, high_hot), (0, low_hot)):
                link(dve.tensor_tensor(flat(out[:, :, :, :]),
                                       digit_i[:, a, :, :].rearrange("p t e -> p (t e)").unsqueeze(2).broadcast_to(hot),
                                       digits[:, :].unsqueeze(1).broadcast_to(hot), ALU.is_equal))
            high = high_hot[:, :, :, :].rearrange("p t e r -> p t (e r)")
            dve.tensor_tensor(high, high, number[:, :].unsqueeze(2).broadcast_to([P, NT, E * R]),
                              ALU.mult).then_inc(low_ready, 1)
            dve.wait_ge(placed, 2)
            for half in range(2):
                ins = dve.tensor_copy(lists[:, 8 * half:8 * (half + 1), :],
                                      place_ps[0:R, half, :, :].rearrange("p (e o) r -> p e o r", o=2)[:, :, 0, :])
            ins.then_inc(lists_taken, 1)
            dve.wait_ge(placed, 3)
            dve.tensor_copy(s.token[:, :, :], count_ps[:, 0:CT, :].rearrange("p c e -> p (c e)").rearrange("p (e c) -> p c e", c=CT))


def load_expert(sp, s, e, p):
    for name, dst, src in (("gate", s.wg_sb, s.w_gate), ("up", s.wu_sb, s.w_up), ("down", s.wd_sb, s.w_down)):
        sp.dma_start(dst[:, p, :, :], src[ds(e, 1)].rearrange("o p k n -> p (o k) n")).then_inc(s.w_loaded[name, p], 16)


def experts(nc, s):
    with ExitStack() as ctx:
        def sb(name, shape, dt=F32):
            return ctx.enter_context(nc.sbuf_tensor(name, shape, dt))

        def ps(name, shape, dt=F32):
            return ctx.enter_context(nc.psum_tensor(name, shape, dt))

        def sem(name):
            return ctx.enter_context(nc.semaphore(name))

        token = sb("token_e", [P, 2, CT], U32)
        xg = sb("xg", [P, 2, CT, D + E])
        xgT = sb("xgT", [P, 2, KD, CAP])
        gelu = sb("e_gelu", [P, 2, CAP])
        hidden = sb("e_hidden", [P, 2, FT, CAP])
        rows_out = sb("rows_out", [P, 2, CT, D])
        all_stats = sb("all_stats3", [P, NT, 6])
        mvs = sb("mvs3", [P, NT, 2])
        nrm = sb("nrm3", [P, 3, NT])
        x_ps = ps("xg_ps", [P, KD, CAP])
        gu_ps = [ps(f"gu_ps{i}", [P, 2, CAP]) for i in range(4)]
        d_ps = [ps(f"d_ps{i}", [P, CT, D]) for i in range(2)]

        token_ready = sem("token_ready")
        gathered = [sem(f"gathered{p}") for p in range(2)]
        xT_ready = sem("xgT_ready")
        xT_taken = sem("xgT_taken")
        gu_ready = sem("gu_ready")
        g_taken = sem("g_taken")
        h_ready = sem("h_ready")
        d_ready = sem("d_ready")
        out_ready = sem("out_ready")
        tick = sem("tick")
        added = sem("added")
        back = [sem(f"rows_back{i}") for i in range(NB)]
        var_ready, root_ready, step = sem("var_ready3"), sem("root_ready3"), sem("n3_step")
        normed = sem("normed")
        stored = sem("stored")
        block = ctx.enter_context(nc.Block())
        rows = lambda ap: ap.rearrange("(t p) d -> p t d", p=P)

        @block.sync
        def _(sp):
            with sp.Fori(1, E // 2) as pair:
                for p in range(2):
                    e = 2 * pair + p
                    sp.wait_ge(d_ready, e - 1)
                    load_expert(sp, s, e, p)
            sp.wait_ge(added, 16 * CT * E)
            for n in range(NB):
                sp.dma_start(s.act[:, QT * n:QT * (n + 1), :], rows(s.acc)[:, QT * n:QT * (n + 1), :]).then_inc(back[n], 16)
            for n in range(NB):
                sp.wait_ge(normed, QT * (n + 1))
                sp.dma_start(rows(s.out)[:, QT * n:QT * (n + 1), :], s.act[:, QT * n:QT * (n + 1), :]).then_inc(stored, 16)
            sp.wait_ge(stored, 16 * NB)

        @block.gpsimd
        def _(pool):
            def gather(e, p):
                pool.tensor_copy(token[:, p, :], s.token[:, :, ds(e, 1)].rearrange("p c o -> p (c o)")).then_inc(token_ready, 1)
                pool.wait_ge(token_ready, e + 1)
                pool.sem_inc(tick, 1)
                for c in range(CT):
                    pool.indirect_dma_start(out=xg[:, p, c, :], out_offset=None, in_=s.x2,
                                            in_offset=bass.IndirectOffsetOnAxis(ap=token[:, p, c:c + 1], axis=0)).then_inc(gathered[p], 16)

            def scatter(e, p, first=False):
                pool.wait_ge(out_ready, e + 3)
                if not first:
                    pool.wait_ge(added, 16 * CT * e)
                pool.sem_inc(tick, 1)
                for c in range(CT):
                    pool.indirect_dma_start(out=s.acc, out_offset=bass.IndirectOffsetOnAxis(ap=token[:, p, c:c + 1], axis=0),
                                            in_=rows_out[:, p, c, :], in_offset=None, compute_op=ALU.add).then_inc(added, 16)

            gather(0, 0)
            gather(1, 1)
            scatter(0, 0, first=True)
            with pool.Fori(1, E // 2) as pair:
                for p in range(2):
                    e = 2 * pair + p
                    pool.wait_ge(added, 16 * CT * (e - 1))
                    pool.wait_ge(xT_ready, e - 1)
                    gather(e, p)
                    scatter(e - 1, 1 - p)
            scatter(E - 1, 1)

        @block.tensor
        def _(pe):
            def turn_rows(pair, p):
                e = 2 * pair + p
                pe.wait_ge(gathered[p], 16 * CT * (pair + 1))
                pe.wait_ge(xT_taken, e + 1)
                for c in range(CT):
                    for k in range(KD):
                        mm = pe.transpose(x_ps[:, k, c * P:(c + 1) * P], xg[:, p, c, k * P:(k + 1) * P], s.ident[:, :])
                mm.then_inc(xT_ready, 1)

            def gate_up(pair, p):
                e = 2 * pair + p
                pe.wait_ge(xT_taken, e + 2)
                pe.wait_ge(s.w_loaded["gate", p], 16 * (pair + 1))
                pe.wait_ge(s.w_loaded["up", p], 16 * (pair + 1))
                for i in range(FT):
                    bank = gu_ps[i % 4]
                    pe.wait_ge(h_ready, FT * e + i + 1)
                    for a, weight in ((0, s.wg_sb), (1, s.wu_sb)):
                        for k in range(KD):
                            mm = pe.matmul(bank[:, a, :], weight[:, p, k, i * P:(i + 1) * P], xgT[:, p, k, :],
                                           start=(k == 0), stop=(k == KD - 1))
                    mm.then_inc(gu_ready, 1)

            def down(pair, p):
                e = 2 * pair + p
                pe.wait_ge(h_ready, FT * e + FT + 4)
                pe.wait_ge(s.w_loaded["down", p], 16 * (pair + 1))
                pe.wait_ge(out_ready, e + 1)
                for c in range(CT):
                    for i in range(FT):
                        mm = pe.matmul(d_ps[p][:, c, :], hidden[:, p, i, c * P:(c + 1) * P], s.wd_sb[:, p, i, :],
                                       start=(i == 0), stop=(i == FT - 1))
                mm.then_inc(d_ready, 1)

            def expert(pair, p, last=False):
                gate_up(pair, p)
                if not last:
                    turn_rows(pair + p, 1 - p)
                down(pair, p)

            turn_rows(0, 0)
            with pe.Fori(0, E // 2 - 1) as pair:
                for p in range(2):
                    expert(pair, p)
            expert(E // 2 - 1, 0)
            expert(E // 2 - 1, 1, last=True)

        @block.scalar
        def _(act):
            act.sem_inc(xT_taken, 1)

            def take_rows(e, p):
                act.wait_ge(xT_ready, e + 1)
                act.copy(xgT[:, p, :, :], x_ps[:, :, :]).then_inc(xT_taken, 1)

            def expert(pair, p, last=False):
                e = 2 * pair + p
                for i in range(FT):
                    act.wait_ge(gu_ready, FT * e + i + 1)
                    act.wait_ge(h_ready, FT * e + i + 3)
                    act.activation(gelu[:, i % 2, :], gu_ps[i % 4][:, 0, :], ACT.Gelu).then_inc(g_taken, 1)
                if not last:
                    take_rows(e + 1, 1 - p)

            take_rows(0, 0)
            with act.Fori(0, E // 2 - 1) as pair:
                for p in range(2):
                    expert(pair, p)
            expert(E // 2 - 1, 0)
            expert(E // 2 - 1, 1, last=True)
            act.wait_ge(var_ready, 1)
            act.activation(nrm[:, 1, :], nrm[:, 0, :], ACT.Sqrt).then_inc(root_ready, 1)

        @block.vector
        def _(dve):
            dve.sem_inc(h_ready, 4)
            dve.sem_inc(out_ready, 2)

            def scale_rows(pair, p):
                e = 2 * pair + p
                dve.wait_ge(token_ready, e + 1)
                dve.wait_ge(d_ready, e + 1)
                for c in range(CT):
                    ins = dve.tensor_scalar(rows_out[:, p, c, :], d_ps[p][:, c, :],
                                            xg[:, p, c, ds(e + D, 1)], None, ALU.mult)
                ins.then_inc(out_ready, 1)

            def products(pair, p):
                e = 2 * pair + p
                for i in range(FT):
                    dve.wait_ge(g_taken, FT * e + i + 1)
                    dve.tensor_tensor(hidden[:, p, i, :], gelu[:, i % 2, :], gu_ps[i % 4][:, 1, :],
                                      ALU.mult).then_inc(h_ready, 1)

            with dve.Fori(0, E // 2) as pair:
                for p in range(2):
                    products(pair, p)
                    scale_rows(pair, p)

            link = chain(dve, step)
            for n in range(NB):
                dve.wait_ge(back[n], 16)
                for t in range(QT * n, QT * (n + 1)):
                    last = dve.bn_stats(all_stats[:, t, :], s.act[:, t, :])
            link(last)
            for t in range(NT):
                last = dve.bn_aggr(mvs[:, t, :], all_stats[:, t, :])
            link(last)
            norm_scale(dve, link, mvs[:, :, 1], (nrm[:, 0, :], nrm[:, 1, :]), root_ready, var_ready, nrm[:, 2, :])
            for t in range(NT):
                dve.tensor_scalar(s.act[:, t, :], s.act[:, t, :], mvs[:, t, 0:1], nrm[:, 2, t:t + 1],
                                  ALU.subtract, ALU.mult).then_inc(normed, 1)


def program(nc, arg, upto=9, dump=None):
    s = Shared()
    s.xT, s.ctxT, s.x, s.mask = arg["xT"], arg["ctxT"], arg["x"], arg["mask"]
    s.w_q, s.w_k, s.w_v, s.w_o = arg["wq"], arg["wk"], arg["wv"], arg["wo"]
    s.w_cq, s.w_ck, s.w_cv, s.w_co = arg["cwq"], arg["cwk"], arg["cwv"], arg["cwo"]
    s.b = {"q": arg["bq"], "k": arg["bk"], "v": arg["bv"], "o": arg["bo"],
           "cq": arg["cbq"], "ck": arg["cbk"], "cv": arg["cbv"], "co": arg["cbo"]}
    s.gate_w, s.out = arg["gate"], arg["out"]
    s.w_gate, s.w_up, s.w_down = arg["wg"], arg["wu"], arg["wd"]
    s.s_gate, s.s_up, s.s_down = arg["sg"], arg["su"], arg["sd"]

    def dram(name, shape, dt=F32):
        return nc.dram_tensor(name, shape, dt, kind="Internal").ap()

    s.k_parts = dram("k_parts", (3, D, S2), BF16)
    s.q_parts = dram("q_parts", (3, D, T), BF16)
    s.mask_parts = dram("mask_parts", (1, 6, S2), BF16)
    s.x2 = dram("x2_rows", (T, D + E))
    s.acc = dram("acc_rows", (T, D))
    with ExitStack() as ctx:
        def sb(name, shape, dt=F32):
            return ctx.enter_context(nc.sbuf_tensor(name, shape, dt))

        s.consts = ctx.enter_context(nc.semaphore("consts"))
        s.ident = sb("ident", [P, P])
        s.ident_b = sb("ident_b", [P, P], BF16)
        s.act = sb("activations", [P, NT, D])
        s.actT = sb("activationsT", [P, KD, T])
        s.qT = s.actT
        with ExitStack() as attention:
            s.cv = attention.enter_context(nc.sbuf_tensor("cv", [P, NKT, H, VW], F32))
            s.k_stack_space = attention.enter_context(nc.sbuf_tensor("k_stack", [P, H * S2], BF16))
            s.k_stack = s.k_stack_space[:, :].rearrange("p (h n) -> p h n", h=H)
            with ExitStack() as first:
                s.kT = first.enter_context(nc.sbuf_tensor("kT", [P, KD, T], F32))
                s.v = first.enter_context(nc.sbuf_tensor("v", [P, NT, D], F32))
                s.wo = first.enter_context(nc.sbuf_tensor("w_out", [P, KD, D], F32))
                project_inputs(nc, s)
                if upto >= 1:
                    self_attention(nc, s)
            if upto >= 2:
                cross_attention(nc, s)
        if upto >= 3:
            s.wg_sb = sb("wg_sb", [P, 2, KD, FI])
            s.wu_sb = sb("wu_sb", [P, 2, KD, FI])
            s.wd_sb = sb("wd_sb", [P, 2, FT, D])
            s.token = sb("token", [P, CT, E], U32)
            s.w_loaded = {(n, p): ctx.enter_context(nc.semaphore(f"w_{n}{p}"))
                          for n in ("gate", "up", "down") for p in range(2)}
            route(nc, s)
            experts(nc, s)
        if dump:
            dump(nc, s)


def kernel(**inputs):
    import numpy as np
    import concourse.bacc as bacc
    from concourse.bass_utils import run_bass_kernel_spmd

    arrays = layout(np, inputs)
    nc = bacc.Bacc("TRN2", target_bir_lowering=False, num_devices=1)
    arg = {n: nc.dram_tensor(f"in_{n}", a.shape, mybir.dt.from_np(a.dtype), kind="ExternalInput").ap()
           for n, a in arrays.items()}
    arg["out"] = nc.dram_tensor("out_0", (T, D), F32, kind="ExternalOutput").ap()
    program(nc, arg)
    r = run_bass_kernel_spmd(nc, [{f"in_{n}": a for n, a in arrays.items()}], core_ids=[0])
    return r.results[0]["out_0"].reshape(1, T, D)


def layout(np, inputs):
    a = {n: np.asarray(v) for n, v in inputs.items()}

    def cut(m):
        m = m.reshape(*m.shape[:-2], m.shape[-2] // P, P, m.shape[-1])
        return np.ascontiguousarray(np.swapaxes(m, -3, -2))

    def turned(m):
        return cut(np.swapaxes(m, -1, -2))

    def column(v):
        return np.ascontiguousarray(v.reshape(KD, P).T)

    out = {"x": cut(a["x"][0]), "xT": turned(a["x"][0]), "ctxT": turned(a["ctx_1024"][0]),
           "mask": np.ascontiguousarray(a["mask_BxS2_if1"][0])}
    for n, k in (("q", "q"), ("k", "k"), ("v", "v"), ("o", "o")):
        out["w" + n] = turned(a[f"L0_attn_W{k}"])
        out["cw" + n] = turned(a[f"L0_xattn_W_{k}"])
        out["b" + n] = a[f"L0_attn_b{k}"]
        out["cb" + n] = a[f"L0_xattn_b_{k}"]
        if n in "qk":
            out["b" + n], out["cb" + n] = column(out["b" + n]), column(out["cb" + n])
    out["gate"] = turned(a["L0_ffn_gate_w"])
    for n, k in (("wg", "Wg"), ("wu", "Wu"), ("wd", "Wd"), ("sg", "Sg"), ("su", "Su"), ("sd", "Sd")):
        out[n] = turned(a[f"L0_ffn_{k}"])
    return out
```

```python
from contextlib import ExitStack

import concourse.bass as bass
from concourse import mybir

F32 = mybir.dt.float32
BF16 = mybir.dt.bfloat16
F32R = mybir.dt.float32r
F16 = mybir.dt.float16
I32 = mybir.dt.int32
U32 = mybir.dt.uint32
ACT = mybir.ActivationFunctionType
ALU = mybir.AluOpType
AX = mybir.AxisListType
ds = bass.ds

P = 128
T = 2048
D = 256
KD = D // P
NT = T // P
S2 = 1601
H = 16
HD = D // H
NKT = -(-S2 // P)
LASTK = S2 - (NKT - 1) * P
E = 16
CAP = T * 2 // E
CT = CAP // P
FI = 1024
FT = FI // P
FS = 512
ST = FS // P
EPS = 1e-5
QSCALE = float(HD) ** -0.5
BLK = 512
NB = T // BLK
QT = BLK // P
G = 4
NG = H // G
VW = 32
NEG = 1.0e9

Q_PARTS = (0, 0, 1, 1, 0, 2)
K_PARTS = (0, 1, 0, 1, 2, 0)
R_MASK = HD * len(Q_PARTS)
R_MAX = R_MASK + 3
R_ALL = R_MAX + 3


class Shared:
    pass


def chain(engine, sem, before=0):
    done = [0]

    def link(ins):
        done[0] += 1
        ins.then_inc(sem, 1)
        engine.wait_ge(sem, before + done[0])

    link.done = done
    return link


def identity(nc, pool, tile, sem, before):
    pool.memset(tile[:, :], 0.0).then_inc(sem, 1)
    pool.wait_ge(sem, before + 1)
    pool.affine_select(out=tile[:, :], in_=tile[:, :], compare_op=ALU.not_equal, fill=1.0, base=0,
                       pattern=[[-1, P]], channel_multiplier=1).then_inc(sem, 1)


def products(pe, out, stationary, moving, start, stop):
    for n, (a, b) in enumerate(((0, 0), (0, 1), (1, 0))):
        mm = pe.matmul(out, stationary[a], moving[b], start=(start and n == 0), stop=(stop and n == 2))
    return mm


def both(ap):
    return ap(0), ap(1)


def project_inputs(nc, s):
    with ExitStack() as ctx:
        def sb(name, shape, dt=F32):
            return ctx.enter_context(nc.sbuf_tensor(name, shape, dt))

        def sem(name):
            return ctx.enter_context(nc.semaphore(name))

        xT = sb("xT", [P, KD, T])
        ctxT = sb("ctxT", [P, KD, S2])
        w = {n: sb(f"w_{n}", [P, KD, D]) for n in ("q", "k", "v", "ck", "cv")}
        b_col = {n: sb(f"bcol_{n}", [P, KD]) for n in ("q", "k", "v", "ck")}
        b_row = {n: sb(f"brow_{n}", [P, D]) for n in ("cv", "o")}
        vT = sb("vT", [P, 2, KD, BLK])
        keep_key, ck = (s.act[:, :, :].rearrange("p t d -> p (t d)")[:, i * S2:(i + 1) * S2] for i in range(2))
        space = s.k_stack_space[0]

        def scratch(at, words):
            return space[:, 2 * at:2 * (at + words)]

        W3 = (3 * S2 + 1) // 2
        part = scratch(0, W3)[:, 0:3 * S2].rearrange("p (c n) -> p c n", c=3)
        rest = scratch(W3, S2).bitcast(F32)
        mask_rows = sb("mask_rows", [NKT, P], I32)
        mask_bias = sb("mask_bias", [NKT, P])
        mask_part = sb("mask_part", [NKT, 6, P], BF16)
        mask_i = scratch(W3 + S2, S2).bitcast(I32)
        pj = [ctx.enter_context(nc.psum_tensor(f"pj{i}", [P, BLK], F32)) for i in range(4)]

        loaded = {n: sem(f"loaded_{n}") for n in ("x", "ctx0", "ctx1", "ctx2", "ctx3", "wq", "wk", "wv", "wo", "wck", "wcv", "b", "mask", "mask_rows", "xn")}
        ready = sem("product_ready")
        taken = sem("product_taken")
        high_made = sem("high_made")
        parts_ready = sem("parts_ready")
        parts_out = sem("parts_out")
        mask_ready = sem("mask_ready")
        mask_out = sem("mask_out")
        ones_set = sem("ones_set")
        dve_step = sem("dve_step")
        block = ctx.enter_context(nc.Block())

        keys = [(a, min(BLK, S2 - a)) for a in range(0, S2, BLK)]
        def width_groups(kind, halves=range(KD)):
            return [(kind, h, a * BLK, BLK) for h in halves for a in range(NB)]

        def v_block(b):
            return [("vT", h, b * BLK, BLK) for h in range(KD)]

        groups = [("ck", 0, a, n) for a, n in keys]
        groups += [("cv", j, j * P, D) for j in range(NKT)]
        groups += width_groups("q")
        groups += [("ck", h, a, n) for h in range(1, KD) for a, n in keys]
        groups += v_block(0) + v_block(1)
        groups += width_groups("k")
        for b in range(NB):
            if b >= 1 and b + 1 < NB:
                groups += v_block(b + 1)
            groups += [("vo", j, j * P, D) for j in range(QT * b, QT * (b + 1))]
        ck_groups = [n for n, group in enumerate(groups) if group[0] == "ck"]

        @block.sync
        def _(sp):
            sp.dma_start(w["ck"][:, :, :], s.w_ck).then_inc(loaded["wck"], 16)
            for a, n in keys:
                sp.dma_start(ctxT[:, :, a:a + n], s.ctxT[:, :, a:a + n]).then_inc(loaded[f"ctx{a // BLK}"], 16)
            for n in ("q", "k", "v", "ck"):
                sp.dma_start(b_col[n][:, :], s.b[n]).then_inc(loaded["b"], 16)
            for n in ("cv", "o"):
                sp.dma_start(b_row[n][:, :], s.b[n].partition_broadcast(P)).then_inc(loaded["b"], 16)
            sp.dma_start(w["cv"][:, :, :], s.w_cv).then_inc(loaded["wcv"], 16)
            sp.dma_start(mask_i[:, :], s.mask.partition_broadcast(P)).then_inc(loaded["mask"], 16)
            sp.wait_ge(ones_set, 2)
            full = (NKT - 1) * P
            sp.dma_start(mask_rows[0:NKT - 1, :], s.mask[0:full].rearrange("(r n) -> r n", n=P)).then_inc(loaded["mask_rows"], 16)
            sp.dma_start(mask_rows[NKT - 1:NKT, 0:LASTK], s.mask[full:S2].unsqueeze(0)).then_inc(loaded["mask_rows"], 16)
            sp.dma_start(w["q"][:, :, :], s.w_q).then_inc(loaded["wq"], 16)
            sp.dma_start(xT[:, :, :], s.xT).then_inc(loaded["x"], 16)
            sp.dma_start(w["k"][:, :, :], s.w_k).then_inc(loaded["wk"], 16)
            sp.dma_start(w["v"][:, :, :], s.w_v).then_inc(loaded["wv"], 16)
            sp.dma_start(s.w_out[:, :, :], s.w_o).then_inc(loaded["wo"], 16)
            sp.wait_ge(mask_ready, 1)
            sp.dma_start(s.mask_parts[:, 0:full].rearrange("c (r n) -> r c n", n=P), mask_part[0:NKT - 1, :, :]).then_inc(mask_out, 16)
            sp.dma_start(s.mask_parts[:, full:S2].unsqueeze(0), mask_part[NKT - 1:NKT, :, 0:LASTK]).then_inc(mask_out, 16)
            for h in range(KD):
                sp.wait_ge(parts_ready, h + 1)
                sp.dma_start(s.k_parts[:, h * P:(h + 1) * P, :].rearrange("c p n -> p c n"),
                             part[:, :, :]).then_inc(parts_out, 16)
            sp.dma_start(s.act[:, :, :], s.x).then_inc(loaded["xn"], 16)
            sp.wait_ge(parts_out, 16 * KD)
            sp.wait_ge(mask_out, 32)

        @block.gpsimd
        def _(pool):
            for i, value in enumerate((EPS, -0.5, 1.5)):
                pool.memset(s.norm_consts[:, i, :], value)
            pool.memset(mask_rows[:, :], 0).then_inc(ones_set, 1)
            pool.memset(mask_part[:, 3:6, :], 1.0).then_inc(ones_set, 1)
            identity(nc, pool, s.ident, s.consts, 0)
            identity(nc, pool, s.ident_b, s.consts, 2)
            pool.memset(s.cv[:, :, :, HD:HD + 1], 1.0).then_inc(ones_set, 1)
            pool.memset(s.cv[:, :, :, HD + 1:VW], 0.0).then_inc(ones_set, 1)
            pool.wait_ge(ones_set, 4)
            pool.wait_ge(loaded["xn"], 16)
            pool.wait_ge(loaded["b"], 16 * 6)
            pool.tensor_tensor(s.act[:, :, :], s.act[:, :, :],
                               b_row["o"][:, :].unsqueeze(1).broadcast_to([P, NT, D]), ALU.add)
        @block.tensor
        def _(pe):
            seen = set()
            for n, (kind, i, a, cols) in enumerate(groups):
                for need in {"ck": ("wck", f"ctx{a // BLK}"), "cv": ("wcv",), "q": ("wq", "x"), "k": ("wk",), "vT": ("wv",), "vo": ("wo",)}[kind]:
                    if need not in seen:
                        pe.wait_ge(loaded[need], 16)
                        seen.add(need)
                if n >= 4:
                    pe.wait_ge(taken, n - 3)
                if kind == "vo":
                    pe.wait_ge(taken, groups.index(("vT", KD - 1, i // QT * BLK, BLK)) + 1)
                src = ctxT if kind in ("ck", "cv") else xT
                for k in range(KD):
                    if kind == "vo":
                        out, lhsT, rhs = pj[n % 4][:, 0:D], vT[:, i // QT % 2, k, i % QT * P:(i % QT + 1) * P], s.w_out[:, k, :]
                    elif kind == "cv":
                        rows = min(P, src.shape[2] - a)
                        out, lhsT, rhs = pj[n % 4][0:rows, 0:D], src[:, k, a:a + rows], w[kind][:, k, :]
                    else:
                        out, lhsT, rhs = pj[n % 4][:, 0:cols], w[kind[0] if kind == "vT" else kind][:, k, i * P:(i + 1) * P], src[:, k, a:a + cols]
                    mm = pe.matmul(out, lhsT, rhs, start=(k == 0), stop=(k == KD - 1))
                mm.then_inc(ready, 1)

        @block.scalar
        def _(act):
            act.wait_ge(loaded["b"], 16 * 6)
            for n, (kind, i, a, cols) in enumerate(groups):
                if kind == "cv":
                    continue
                act.wait_ge(ready, n + 1)
                if n:
                    act.wait_ge(taken, n)
                if kind == "vo":
                    act.copy(s.v[:, 0, i, :], pj[n % 4][:, 0:D]).then_inc(high_made, 1)
                    continue
                if kind == "ck":
                    if i and a == 0:
                        act.wait_ge(parts_ready, i)
                    out = ck[:, a:a + cols]
                elif kind == "vT":
                    out = vT[:, a // BLK % 2, i, :]
                else:
                    out = s.qT[:, i, a:a + cols] if kind == "q" else s.kT[:, 0, i, a:a + cols]
                act.activation(out, pj[n % 4][:, 0:cols], ACT.Identity,
                               bias=b_col["v" if kind == "vT" else kind][:, i:i + 1]).then_inc(high_made if kind == "k" else taken, 1)

        @block.vector
        def _(dve):
            link = chain(dve, dve_step)
            dve.wait_ge(loaded["mask"], 16)
            link(dve.tensor_scalar(keep_key[:, :], mask_i[:, :], 0.0, None, ALU.not_equal))
            dve.wait_ge(loaded["mask_rows"], 32)
            link(dve.tensor_scalar(mask_bias[:, :], mask_rows[:, :], 0.0, None, ALU.not_equal))
            link(dve.tensor_scalar(mask_bias[:, :], mask_bias[:, :], 1.0, NEG, ALU.subtract, ALU.mult))
            for c in range(3):
                link(dve.tensor_copy(mask_part[:, c, :], mask_bias[:, :]))
                if c < 2:
                    link(dve.tensor_tensor(mask_bias[:, :], mask_bias[:, :], mask_part[:, c, :], ALU.subtract))
            dve.engine_nop().then_inc(mask_ready, 1)
            dve.wait_ge(loaded["b"], 16 * 6)

            def split_keys(h):
                dve.wait_ge(taken, ck_groups[(h + 1) * len(keys) - 1] + 1)
                if h:
                    dve.wait_ge(parts_out, 16 * h)
                link(dve.tensor_tensor(ck[:, :], ck[:, :], keep_key[:, :], ALU.mult))
                link(dve.tensor_copy(part[:, 0, :], ck[:, :]))
                link(dve.tensor_tensor(rest[:, :], ck[:, :], part[:, 0, :], ALU.subtract))
                link(dve.tensor_copy(part[:, 1, :], rest[:, :]))
                dve.tensor_tensor(part[:, 2, :], rest[:, :], part[:, 1, :], ALU.subtract).then_inc(parts_ready, 1)

            highs, halves = 0, 0
            for n, (kind, i, a, cols) in enumerate(groups):
                if (kind, halves) in (("q", 0), ("vT", 1)):
                    split_keys(halves)
                    halves += 1
                if kind == "cv":
                    dve.wait_ge(ready, n + 1)
                    dve.wait_ge(taken, n)
                    rows = min(P, S2 - a)
                    dve.tensor_tensor(s.cv[0:rows, i, :, 0:HD], pj[n % 4][0:rows, 0:D].rearrange("p (h d) -> p h d", h=H),
                                      b_row["cv"][0:rows, :].rearrange("p (h d) -> p h d", h=H), ALU.add).then_inc(taken, 1)
                if kind in ("k", "vo"):
                    highs += 1
                    dve.wait_ge(high_made, highs)
                if kind == "k":
                    dve.scalar_tensor_tensor(out=s.kT[:, 1, i, a:a + cols], in0=pj[n % 4][:, 0:cols],
                                             scalar=b_col["k"][:, i:i + 1], in1=s.kT[:, 0, i, a:a + cols].bitcast(F32),
                                             op0=ALU.add, op1=ALU.subtract).then_inc(taken, 1)
                if kind == "vo":
                    dve.tensor_tensor(s.v[:, 1, i, :], pj[n % 4][:, 0:D], s.v[:, 0, i, :].bitcast(F32),
                                      ALU.subtract).then_inc(taken, 1)


def scale_queries(act, s, product, q, part, half):
    for out in (q, part[:, 0]):
        ins = act.activation(out[:, half, :], product, ACT.Identity, bias=s.b_cq_sb[:, half:half + 1], scale=QSCALE)
    return ins


def split_queries(engine, link, q, rest, part):
    link(engine.tensor_tensor(rest, q, part[:, 0], ALU.subtract))
    link(engine.tensor_copy(part[:, 1], rest))
    return engine.tensor_tensor(part[:, 2], rest, part[:, 1], ALU.subtract)


def parts_to_dram(engine, s, part, n, split, count, out):
    engine.wait_ge(split, count)
    for c in range(3):
        engine.dma_start(s.q_parts[c, :, n * BLK:(n + 1) * BLK].rearrange("(k p) t -> p k t", p=P),
                         part[:, c, :, :]).then_inc(out, 16)


def stack_keys(sp, s, part, done):
    heads = H // 2
    for j, c in enumerate(K_PARTS):
        sp.dma_start(s.k_stack[part][HD * j:HD * (j + 1), :, :],
                     s.k_parts[c, part * HD * heads:(part + 1) * HD * heads, :].rearrange("(h d) n -> d h n", h=heads)).then_inc(done, 16)
    sp.dma_start(s.k_stack[part][R_MASK:R_ALL, :, :],
                 s.mask_parts.unsqueeze(1).broadcast_to([R_ALL - R_MASK, heads, S2])).then_inc(done, 16)


def row(tile, t):
    return tile[:, ds(t, 1), :].rearrange("p o d -> p (o d)")


def norm_scale(pool, link, consts, var, square, out):
    eps, minus_half, one_and_half = consts
    link(pool.tensor_tensor(var, var, eps, ALU.add))
    link(pool.tensor_tensor(out, var, minus_half, ALU.pow))
    link(pool.tensor_tensor(square, out, out, ALU.mult))
    link(pool.tensor_tensor(square, square, var, ALU.mult))
    link(pool.tensor_tensor(square, square, minus_half, ALU.mult))
    link(pool.tensor_tensor(square, square, one_and_half, ALU.add))
    return pool.tensor_tensor(out, out, square, ALU.mult)


def norm_consts(s, width):
    return [s.norm_consts[:, i, 0:width] for i in range(3)]


def self_attention(nc, s):
    with ExitStack() as ctx:
        def sb(name, shape, dt=F32):
            return ctx.enter_context(nc.sbuf_tensor(name, shape, dt))

        def ps(name, shape, dt=F32):
            return ctx.enter_context(nc.psum_tensor(name, shape, dt))

        def sem(name):
            return ctx.enter_context(nc.semaphore(name))

        HALF = T // 2
        K_STACKED = 16 * (len(K_PARTS) + 3)
        q_tile = sb("q_tile", [P, 2, KD, P], F32R)
        th_half = sb("th_half", [P, HALF])
        th_full = sb("th_full", [P, HALF])
        w = sb("w", [P, T])
        probs = sb("probs", [P, T])
        probsT = sb("probsT", [P, 2, NT, P], F32R)
        staged = sb("staged", [P, 4, P])
        neg_max = sb("neg_max", [P, 2])
        shift = sb("shift", [P, 1])
        row_sums = sb("row_sums", [P, NT, 2])
        r_sum = sb("r_sum", [P, 1])
        stats = sb("stats", [P, 6])
        mv = sb("mv", [P, 2])
        scale = sb("scale", [P, 2])
        z = sb("z", [P, D])
        x1_tile = sb("x1_tile", [P, D])
        scores = ps("scores", [P, T])
        turned = [ps(f"turned{i}", [P, 4, P]) for i in range(2)]
        y = ps("y", [P, D])
        x1T_ps = ps("x1T_ps", [P, KD, P])

        q_tick = sem("q_tick")
        q_high = sem("q_high")
        q_ready = sem("q_ready")
        scores_ready = sem("scores_ready")
        th_ready = sem("th_ready")
        th_free = sem("th_free")
        scores_free = sem("scores_free")
        shift_ready = sem("shift_ready")
        probs_ready = sem("probs_ready")
        turned_ready = sem("turned_ready")
        probsT_high = sem("probsT_high")
        low_by_dve = sem("low_by_dve")
        low_by_pool = sem("low_by_pool")
        y_ready = sem("y_ready")
        z_ready = sem("z_ready")
        w_step = sem("w_step")
        z_step = sem("z_step")
        z_tick = sem("z_tick")
        n_step = sem("n_step")
        var_ready = sem("var_ready")
        scale_ready = sem("scale_ready")
        x1_ready = sem("x1_ready")
        x1T_ready = sem("x1T_ready")
        x1T_taken = sem("x1T_taken")
        k_stacked = sem("k_stacked")
        cq_bias = sem("cq_bias")
        cq_made = sem("cq0_made")
        cq_scaled = sem("cq0_scaled")
        cq_split = sem("cq0_split")
        cq_out = sem("cq0_out")
        cq_step = sem("cq0_step")
        block = ctx.enter_context(nc.Block())
        cq = th_half[:, :].rearrange("p (k n) -> p k n", k=KD)
        cq_rest = th_full[:, :].rearrange("p (k n) -> p k n", k=KD)
        cq_part = w[:, 0:3 * KD * BLK // 2].bitcast(BF16).rearrange("p (c k n) -> p c k n", c=3, k=KD)

        def low_part(engine, t, g):
            group, src, done = slice(4 * g, 4 * g + 4), turned[g % 2], low_by_dve
            if g == 1:
                src, done = staged, low_by_pool
            engine.wait_ge(probsT_high, 4 * t + g + 1)
            engine.tensor_tensor(probsT[:, 1, group, :], src[:, :, :], probsT[:, 0, group, :].bitcast(F32),
                                 ALU.subtract).then_inc(done, 1)

        @block.sync
        def _(sp):
            sp.dma_start(s.w_cq_sb[:, :, :], s.w_cq).then_inc(k_stacked, 16)
            sp.dma_start(s.b_cq_sb[:, :], s.b["cq"]).then_inc(k_stacked, 16)
            stack_keys(sp, s, 0, k_stacked)
            sp.wait_ge(k_stacked, K_STACKED)
            parts_to_dram(sp, s, cq_part, 0, cq_split, 1, cq_out)
            sp.wait_ge(cq_out, 48)

        @block.gpsimd
        def _(pool):
            def take_q(t):
                pool.tensor_copy(q_tile[:, 0, :, :], s.qT[:, :, ds(t * P, P)]).then_inc(q_high, 1)
                pool.wait_ge(q_high, t + 1)
                pool.sem_inc(q_tick, 1)
                pool.tensor_tensor(q_tile[:, 1, :, :], s.qT[:, :, ds(t * P, P)], q_tile[:, 0, :, :].bitcast(F32),
                                   ALU.subtract).then_inc(q_ready, 1)

            def next_q(t):
                pool.wait_ge(scores_ready, 2 * t)
                take_q(t)

            def norm(t):
                link = chain(pool, n_step, 6 * t)
                pool.wait_ge(var_ready, t + 1)
                norm_scale(pool, link, norm_consts(s, 1), mv[:, 1:2], scale[:, 0:1], scale[:, 1:2]).then_inc(scale_ready, 1)

            take_q(0)
            next_q(1)
            next_q(2)
            low_part(pool, 0, 1)
            with pool.Fori(2, NT - 1) as t:
                norm(t - 2)
                low_part(pool, t - 1, 1)
                next_q(t + 1)
            norm(NT - 3)
            low_part(pool, NT - 2, 1)
            norm(NT - 2)
            low_part(pool, NT - 1, 1)
            norm(NT - 1)

        @block.tensor
        def _(pe):
            def score_half(t, c):
                if c == 0:
                    pe.wait_ge(q_ready, t + 1)
                pe.wait_ge(scores_free, 2 * t + c + 1)
                for b in range(2):
                    cols = slice(c * HALF + b * BLK, c * HALF + (b + 1) * BLK)
                    for k in range(KD):
                        mm = products(pe, scores[:, cols], both(lambda c: q_tile[:, c, k, :]),
                                      both(lambda c: s.kT[:, c, k, cols]), start=(k == 0), stop=(k == KD - 1))
                mm.then_inc(scores_ready, 1)

            def wait_split(t, g):
                if g == 1:
                    pe.wait_ge(low_by_pool, t + 1)
                else:
                    pe.wait_ge(low_by_dve, 3 * t + 2 + {-2: -1, -1: 0, 0: 1, 2: 2, 3: 3}[g])

            def turn_probs(t, g):
                pe.wait_ge(probs_ready, 2 * t + g // 2 + 1)
                wait_split(t, g - 2)
                for j in range(4):
                    c = 4 * g + j
                    mm = pe.transpose(turned[g % 2][:, j, :], probs[:, c * P:(c + 1) * P], s.ident[:, :])
                mm.then_inc(turned_ready, 1)

            def add_values(t, g):
                wait_split(t, g)
                if g == 0:
                    pe.wait_ge(z_ready, t + 1)
                for j in range(4 * g, 4 * g + 4):
                    mm = products(pe, y[:, :], both(lambda c: probsT[:, c, j, :]), both(lambda c: s.v[:, c, j, :]),
                                  start=(j == 0), stop=(j == NT - 1))
                if g == 3:
                    mm.then_inc(y_ready, 1)

            def value_tile(t, scores_between=None):
                turn_probs(t, 0)
                if scores_between is not None:
                    score_half(scores_between, 1)
                for g in range(1, 4):
                    turn_probs(t, g)
                    add_values(t, g - 1)
                add_values(t, 3)

            def turn_x1(t):
                pe.wait_ge(x1_ready, t + 1)
                pe.wait_ge(x1T_taken, t + 1)
                for k in range(KD):
                    mm = pe.transpose(x1T_ps[:, k, :], x1_tile[:, k * P:(k + 1) * P], s.ident[:, :])
                mm.then_inc(x1T_ready, 1)

            pe.sem_inc(x1T_ready, 1)
            score_half(0, 0)
            score_half(0, 1)
            score_half(1, 0)
            value_tile(0, 1)
            with pe.Fori(2, NT) as t:
                score_half(t, 0)
                value_tile(t - 1, t)
                turn_x1(t - 2)
            pe.wait_ge(k_stacked, K_STACKED)
            pe.wait_ge(scores_free, 2 * NT + 2)
            for half in range(KD):
                for k in range(KD):
                    mm = pe.matmul(scores[:, half * BLK:(half + 1) * BLK], s.w_cq_sb[:, k, half * P:(half + 1) * P],
                                   s.actT[:, k, 0:BLK], start=(k == 0), stop=(k == KD - 1))
                mm.then_inc(cq_made, 1)
            value_tile(NT - 1)
            turn_x1(NT - 2)
            turn_x1(NT - 1)

        @block.scalar
        def _(act):
            def tanhs(t, c, between=lambda: None):
                cols = slice(c * HALF, (c + 1) * HALF)
                act.wait_ge(scores_ready, 2 * t + c + 1)
                act.wait_ge(th_free, 2 * t + c + 1)
                act.activation(th_half[:, :], scores[:, cols], ACT.Tanh, scale=0.5)
                between()
                act.activation(th_full[:, :], scores[:, cols], ACT.Tanh).then_inc(th_ready, 1)

            def exps(t):
                act.wait_ge(shift_ready, t + 1)
                for c in range(2):
                    cols = slice(c * HALF, (c + 1) * HALF)
                    act.activation(probs[:, cols], w[:, cols], ACT.Exp, bias=shift[:, :], scale=0.1,
                                   accum_out=row(row_sums, t)[:, c:c + 1]).then_inc(probs_ready, 1)

            def high_part(t, g):
                act.wait_ge(turned_ready, 4 * t + g + 1)
                if g == 1:
                    act.copy(staged[:, :, :], turned[1][:, :, :])
                act.copy(probsT[:, 0, 4 * g:4 * g + 4, :], turned[g % 2][:, :, :]).then_inc(probsT_high, 1)

            def take_x1(t):
                act.wait_ge(x1T_ready, t + 2)
                act.copy(s.actT[:, :, ds(t * P, P)], x1T_ps[:, :, :]).then_inc(x1T_taken, 1)

            def tile_beside(t):
                tanhs(t, 0, between=lambda: high_part(t - 1, 0))
                high_part(t - 1, 1)
                tanhs(t, 1, between=lambda: high_part(t - 1, 2))
                high_part(t - 1, 3)
                exps(t)

            act.sem_inc(x1T_taken, 1)
            tanhs(0, 0)
            tanhs(0, 1)
            exps(0)
            tile_beside(1)
            with act.Fori(2, NT) as t:
                tile_beside(t)
                take_x1(t - 2)
            act.wait_ge(cq_bias, 1)
            act.wait_ge(probs_ready, 2 * NT)
            for half in range(KD):
                act.wait_ge(cq_made, half + 1)
                scale_queries(act, s, scores[:, half * BLK:(half + 1) * BLK], cq, cq_part, half).then_inc(cq_scaled, 1)
            for g in range(4):
                high_part(NT - 1, g)
            take_x1(NT - 2)
            take_x1(NT - 1)

        @block.vector
        def _(dve):
            dve.sem_inc(scores_free, 2)
            dve.sem_inc(th_free, 1)
            dve.sem_inc(low_by_dve, 2)
            dve.sem_inc(z_ready, 1)

            def tanh_sum(t, c, first=False):
                dve.wait_ge(th_ready, 2 * t + c + 1)
                if not first:
                    dve.wait_ge(probs_ready, 2 * t + c - 1)
                dve.scalar_tensor_tensor(out=w[:, c * HALF:(c + 1) * HALF], in0=th_full[:, :], scalar=1.5, in1=th_half[:, :],
                                         op0=ALU.mult, op1=ALU.add).then_inc(th_free, 1)

            def add_relu(t, c):
                cols = slice(c * HALF, (c + 1) * HALF)
                dve.wait_ge(th_free, 2 * t + c + 2)
                dve.scalar_tensor_tensor(out=w[:, cols], in0=scores[:, cols], scalar=0.0, in1=w[:, cols],
                                         op0=ALU.max, op1=ALU.add).then_inc(scores_free, 1)

            def maximum(t, c):
                dve.wait_ge(scores_free, 2 * t + c + 3)
                dve.tensor_reduce(neg_max[:, c:c + 1], w[:, c * HALF:(c + 1) * HALF], AX.X, ALU.max, negate=True).then_inc(w_step, 1)

            def exp_shift(t):
                dve.wait_ge(w_step, 2 * t + 2)
                dve.tensor_scalar(shift[:, :], neg_max[:, 0:1], neg_max[:, 1:2], 0.1, ALU.min, ALU.mult).then_inc(shift_ready, 1)

            def tile_beside(t, before=None):
                low_part(dve, t - 1, 0)
                tanh_sum(t, 0)
                add_relu(t, 0)
                if before is not None:
                    x1_rows(before)
                low_part(dve, t - 1, 2)
                maximum(t, 0)
                tanh_sum(t, 1)
                low_part(dve, t - 1, 3)
                add_relu(t, 1)
                maximum(t, 1)
                exp_shift(t)

            def z_tile(t):
                link = chain(dve, z_step, 3 * t)
                dve.wait_ge(y_ready, t + 1)
                link(dve.tensor_tensor(r_sum[:, :], row(row_sums, t)[:, 0:1], row(row_sums, t)[:, 1:2], ALU.add))
                link(dve.reciprocal(r_sum[:, :], r_sum[:, :]))
                dve.scalar_tensor_tensor(out=z[:, :], in0=y[:, :], scalar=r_sum[:, :], in1=row(s.act, t),
                                         op0=ALU.mult, op1=ALU.add).then_inc(z_ready, 1)
                dve.wait_ge(z_ready, t + 2)
                link(dve.bn_stats(stats[:, :], z[:, :]))
                dve.sem_inc(z_tick, 1)
                dve.bn_aggr(mv[:, :], stats[:, :]).then_inc(var_ready, 1)

            def x1_rows(t):
                dve.wait_ge(scale_ready, t + 1)
                dve.wait_ge(x1T_ready, t + 1)
                dve.tensor_scalar(x1_tile[:, :], z[:, :], mv[:, 0:1], scale[:, 1:2], ALU.subtract, ALU.mult).then_inc(x1_ready, 1)
                dve.wait_ge(x1_ready, t + 1)
                dve.tensor_scalar(row(s.act, t), x1_tile[:, :], 1.0, None, ALU.mult)

            for c in range(2):
                tanh_sum(0, c, first=True)
                add_relu(0, c)
                maximum(0, c)
            exp_shift(0)
            tile_beside(1)
            with dve.Fori(2, NT) as t:
                z_tile(t - 2)
                tile_beside(t, before=t - 2)
            dve.wait_ge(k_stacked, K_STACKED)
            dve.tensor_scalar(s.b_cq_sb[:, :], s.b_cq_sb[:, :], QSCALE, None, ALU.mult).then_inc(cq_bias, 1)
            z_tile(NT - 2)
            low_part(dve, NT - 1, 0)
            x1_rows(NT - 2)
            low_part(dve, NT - 1, 2)
            low_part(dve, NT - 1, 3)
            dve.wait_ge(cq_scaled, KD)
            split_queries(dve, chain(dve, cq_step), cq, cq_rest, cq_part).then_inc(cq_split, 1)
            z_tile(NT - 1)
            x1_rows(NT - 1)


def transpose_tiles(pe, src, ident, banks, src_ready, ready, taken):
    for n in range(NT // 2):
        if n >= 2:
            pe.wait_ge(taken, n - 1)
        pe.wait_ge(src_ready, 2 * n + 2)
        for k in range(KD):
            for j in range(2):
                mm = pe.transpose(banks[n % 2][:, 2 * k + j, :], src[:, 2 * n + j, k * P:(k + 1) * P], ident[:, :])
        mm.then_inc(ready, 1)


def take_tiles(act, dst, banks, ready, taken):
    for n in range(NT // 2):
        act.wait_ge(ready, n + 1)
        act.copy(dst[:, :, 2 * n * P:(2 * n + 2) * P],
                 banks[n % 2][:, :, :].rearrange("p (k c) d -> p k (c d)", k=KD)).then_inc(taken, 1)


def cross_attention(nc, s):
    with ExitStack() as ctx:
        s.k_stack[1] = ctx.enter_context(nc.sbuf_tensor("k_stack1", [P, H // 2 * S2], BF16))[:, :].rearrange("p (h n) -> p h n", n=S2)
        s.q_stack = ctx.enter_context(nc.sbuf_tensor("q_stack", [P, NB * NG, G, BLK], BF16))
        s.ctx = s.actT[:, :, :].rearrange("p k t -> p (k t)").rearrange("p (t d) -> p t d", t=NT)
        attend(nc, s)


def ring_entries(it, static):
    NIT = NB * NG
    entries = [("chunk", c) for c in range(2 * QT * G)] if static + 2 < NIT else []
    if static >= 1:
        entries.insert(5, ("context", it - 1))
    if static + 1 < NIT:
        entries.insert(11, ("rows", it + 1))
    return entries


def attend(nc, s):
    with ExitStack() as ctx:
        def sb(name, shape, dt=F32):
            return ctx.enter_context(nc.sbuf_tensor(name, shape, dt))

        def ps(name, shape, dt=F32):
            return ctx.enter_context(nc.psum_tensor(name, shape, dt))

        def sem(name):
            return ctx.enter_context(nc.semaphore(name))

        NIT = NB * NG
        HALF_KEYS = -(-S2 // 2)
        CHUNKS = ((0, HALF_KEYS), (HALF_KEYS, S2))
        NCH = 2 * QT * G
        STEPS = NKT
        E_IT = STEPS * G
        SLOTS = 3 * STEPS
        RING0 = 2 * NCH + 1
        RING1 = RING0 + NCH + 1
        R_IT = NCH + 2
        LAST = NG * (NB - 1) + 1

        PIECE_AT = {6 + 6 * i: (2 + i // 4, i // 2 % 2, i % 2) for i in range(8)}

        q_part = sb("cq_part", [P, 3, KD, BLK], BF16)
        probs = sb("xprobs", [P, 2, G, BLK])
        q, q_rest = probs[:, 0, 0:KD, :], probs[:, 0, KD:2 * KD, :]
        out_sb = sb("xout_sb", [P, BLK])
        chunk_max = sb("chunk_max", [P, 2, QT, G])
        max_rest = sb("max_rest", [P, 2, QT, G])
        max_part = sb("max_part", [P, QT, 3 * G], BF16)
        max_rows = sb("max_rows", [3 * G, QT, P], BF16)
        r_den = sb("r_den", [P, QT, G])
        a_ps = [ps(f"a_ps{i}", [P, 2 * BLK]) for i in range(2)]
        e_ps = [ps(f"e_ps{i}", [P, BLK]) for i in range(3)]
        o_ps = ps("o_ps", [P, BLK])
        q_ps = [e_ps[0:2], (e_ps[2], o_ps)]
        turned = [a[:, 0:QT * P].rearrange("p (q c) -> p q c", q=QT) for a in a_ps]
        rows_ps = [a[:, 0:QT * P // 2].bitcast(BF16)[0:3 * G, :].rearrange("p (q c) -> p q c", q=QT) for a in a_ps]

        q_made = sem("cq_made")
        q_scaled = sem("cq_scaled")
        q_split = sem("cq_split")
        q_step = sem("cq_step")
        parts_out = [sem(f"cq_parts_out{i}") for i in range(NB)]
        stacked = [sem(f"cq_stacked{i}") for i in range(NB)]
        k_stacked = sem("k_stacked_others")
        out_weights = sem("co_weights")
        ones_in = sem("cq_ones_in")
        ring_ready = sem("ring_ready")
        ring_free = sem("ring_free")
        max_split = sem("max_split")
        rows_in = sem("rows_in")
        s_ready = sem("s_ready")
        exp_done = sem("exp_done")
        pv_done = sem("pv_done")
        out_taken = sem("out_taken")
        rows_taken = sem("rows_taken")
        m_step = sem("m_step")
        c_step = sem("c_step")
        block = ctx.enter_context(nc.Block())

        def ring_base(it, static):
            if static == 0:
                return RING0
            if static <= LAST:
                return RING1 + R_IT * (it - 1)
            return RING1 + R_IT * (LAST - 1) + sum(len(ring_entries(i, i)) for i in range(LAST, static))

        def run(engine, iteration):
            iteration(0, 0)
            with engine.Fori(0, NB - 1) as r:
                for g in range(1, NG + 1):
                    iteration(NG * r + g, g)
            for it in range(LAST, NIT):
                iteration(it, it)

        def stack_block(engine, n):
            for j, c in enumerate(Q_PARTS):
                engine.dma_start(s.q_stack[HD * j:HD * (j + 1), NG * n:NG * (n + 1), :, :].rearrange("p g h t -> p (g h) t"),
                                 s.q_parts[c, :, n * BLK:(n + 1) * BLK].rearrange("(h d) t -> d h t", h=H)).then_inc(stacked[n], 16)

        @block.gpsimd
        def _(pool):
            for n in range(1, NB):
                pool.wait_ge(q_scaled, KD * n)
                split_queries(pool, chain(pool, q_step, 2 * (n - 1)), q, q_rest, q_part).then_inc(q_split, 1)
                parts_to_dram(pool, s, q_part, n, q_split, n, parts_out[n])
                pool.wait_ge(parts_out[n], 48)
                stack_block(pool, n)
            pool.wait_ge(out_weights, 32)
            pool.tensor_tensor(s.act[:, :, :], s.act[:, :, :],
                               s.b_co_row[:, :].unsqueeze(1).broadcast_to([P, NT, D]), ALU.add)

        @block.sync
        def _(sp):
            sp.dma_start(s.q_stack[R_MASK:R_MAX, :, :, :].rearrange("p i h t -> p (i h) t"),
                         s.mask_parts[3:6, 0:BLK].unsqueeze(1).broadcast_to([3, NB * NG * G, BLK])).then_inc(ones_in, 16)
            stack_block(sp, 0)
            stack_keys(sp, s, 1, k_stacked)
            sp.dma_start(s.w_out[:, :, :], s.w_co).then_inc(out_weights, 16)
            sp.dma_start(s.b_co_row[:, :], s.b["co"].partition_broadcast(P)).then_inc(out_weights, 16)
            with sp.Fori(0, NIT) as it:
                sp.wait_ge(rows_taken, it + 1)
                for c in range(3):
                    sp.dma_start(s.q_stack[R_MAX + c:R_MAX + c + 1, ds(it, 1), :, :].rearrange("p o h t -> p o (h t)"),
                                 max_rows[G * c:G * (c + 1), :, :]).then_inc(rows_in, 16)
            sp.wait_ge(rows_in, 48 * NIT)

        @block.tensor
        def _(pe):
            def project_queries(n, half, k):
                if n >= 3 and k == 0:
                    pe.wait_ge(q_scaled, KD * (n - 3) + half + 1)
                mm = pe.matmul(q_ps[n % 2][half][:, :], s.w_cq_sb[:, k, half * P:(half + 1) * P],
                               s.actT[:, k, n * BLK:(n + 1) * BLK], start=(k == 0), stop=(k == KD - 1))
                if k == KD - 1:
                    mm.then_inc(q_made, 1)

            def max_chunk(it, g, c, at, bank):
                qt, h, half = c // (2 * G), c // 2 % G, c % 2
                a, b = CHUNKS[half]
                pe.wait_ge(ring_free, at + 1)
                for k in range(a, b, BLK):
                    n = min(BLK, b - k)
                    mm = pe.matmul(a_ps[bank][:, k - a:k - a + n],
                                   s.q_stack[0:R_MAX, ds(it, 1), h, qt * P:(qt + 1) * P].rearrange("p o t -> p (o t)"),
                                   s.k_stack[g // 2][0:R_MAX, G * (g % 2) + h, k:k + n], start=True, stop=True)
                mm.then_inc(ring_ready, 1)

            def turn_rows(it, at, bank):
                pe.wait_ge(max_split, it + 1)
                pe.wait_ge(ring_free, at + 1)
                for qt in range(QT):
                    mm = pe.transpose(rows_ps[bank][:, qt, :], max_part[:, qt, :], s.ident_b[:, :])
                mm.then_inc(ring_ready, 1)

            def turn_context(it, at, bank):
                pe.wait_ge(out_taken, it + 2)
                pe.wait_ge(ring_free, at + 1)
                for qt in range(QT):
                    mm = pe.transpose(turned[bank][:, qt, :], out_sb[:, qt * P:(qt + 1) * P], s.ident[:, :])
                mm.then_inc(ring_ready, 1)

            def values(it, g, j):
                rows = P if j < NKT - 1 else LASTK
                if j == 0:
                    pe.wait_ge(out_taken, it + 1)
                for h in range(G):
                    pe.wait_ge(exp_done, E_IT * it + G * j + h + 4)
                    mm = pe.matmul(o_ps[VW * h:VW * (h + 1), :], s.cv[0:rows, j, G * g + h, :],
                                   probs[0:rows, (g * STEPS + j) % 2, h, :], start=(j == 0), stop=(j == NKT - 1))
                mm.then_inc(pv_done, 1)

            def score_tile(it, g, j, h):
                rows, n = P if j < NKT - 1 else LASTK, G * j + h
                pe.wait_ge(exp_done, E_IT * it + (n + 1 if n >= 3 else (3, 1, 2)[n]))
                pe.matmul(e_ps[n % 3][0:rows, :], s.k_stack[g // 2][0:R_ALL, G * (g % 2) + h, j * P:j * P + rows],
                          s.q_stack[0:R_ALL, ds(it, 1), h, :].rearrange("p o t -> p (o t)"),
                          start=True, stop=True).then_inc(s_ready, 1)

            def iteration(it, static):
                g = static % NG
                base, even = ring_base(it, static), ring_base(static, static)
                entries = ring_entries(it, static)
                slots = [None] * SLOTS
                for k, entry in enumerate(entries):
                    slots[k * SLOTS // R_IT if len(entries) > 2 else 6 * (k + 1)] = (k, entry)

                def ring(slot):
                    if slots[slot] is None:
                        return
                    k, (kind, what) = slots[slot]
                    if kind == "chunk":
                        max_chunk(it + 2, (g + 2) % NG, what, base + k, (even + k) % 2)
                    elif kind == "rows":
                        turn_rows(what, base + k, (even + k) % 2)
                    else:
                        turn_context(what, base + k, (even + k) % 2)

                pe.wait_ge(rows_in, 48 * (it + 1))
                if static == 2:
                    for n in range(1, NB):
                        pe.wait_ge(stacked[n], 16 * len(Q_PARTS))
                for j in range(STEPS):
                    ring(3 * j)
                    score_tile(it, g, j, 0)
                    score_tile(it, g, j, 1)
                    ring(3 * j + 1)
                    if j:
                        values(it, g, j - 1)
                    elif static:
                        values(it - 1, (g - 1) % NG, STEPS - 1)
                    ring(3 * j + 2)
                    score_tile(it, g, j, 2)
                    score_tile(it, g, j, 3)

            for half in range(KD):
                for k in range(KD):
                    project_queries(1, half, k)
            pe.wait_ge(ones_in, 16)
            pe.wait_ge(stacked[0], 16 * len(Q_PARTS))
            for it in range(2):
                for c in range(NCH):
                    if NCH * it + c in PIECE_AT:
                        project_queries(*PIECE_AT[NCH * it + c])
                    max_chunk(it, it, c, (NCH + 1) * it + c, ((NCH + 1) * it + c) % 2)
                if it == 0:
                    turn_rows(0, NCH, NCH % 2)
            pe.wait_ge(k_stacked, 16 * (len(K_PARTS) + 1))
            pe.wait_ge(q_scaled, KD * (NB - 1))
            run(pe, iteration)
            values(NIT - 1, NG - 1, STEPS - 1)
            end = ring_base(NIT, NIT)
            turn_context(NIT - 1, end, end % 2)

        @block.scalar
        def _(act):
            act.sem_inc(exp_done, 3)
            act.sem_inc(out_taken, 1)
            for n in range(1, NB):
                if n > 1:
                    act.wait_ge(parts_out[n - 1], 48)
                for half in range(KD):
                    act.wait_ge(q_made, KD * (n - 1) + half + 1)
                    scale_queries(act, s, q_ps[n % 2][half][:, :], q, q_part, half).then_inc(q_scaled, 1)

            def take_outputs(it):
                act.wait_ge(pv_done, STEPS * (it + 1) + 2)
                act.copy(out_sb[:, :], o_ps[:, :]).then_inc(out_taken, 1)

            def iteration(it, static):
                if static:
                    take_outputs(it - 1)
                for j in range(STEPS):
                    rows = P if j < NKT - 1 else LASTK
                    act.wait_ge(pv_done, STEPS * it + j + 1)
                    for h in range(G):
                        n = G * j + h
                        act.wait_ge(s_ready, E_IT * it + n + 1)
                        act.activation(probs[0:rows, (static * STEPS + j) % 2, h, :], e_ps[n % 3][0:rows, :],
                                       ACT.Exp).then_inc(exp_done, 1)

            act.wait_ge(q_split, NB - 1)
            run(act, iteration)
            take_outputs(NIT - 1)

        @block.vector
        def _(dve):
            dve.sem_inc(ring_free, 2)
            dve.sem_inc(pv_done, 2)

            def take_chunk(c, at, bank):
                qt, h, half = c // (2 * G), c // 2 % G, c % 2
                a, b = CHUNKS[half]
                dve.wait_ge(ring_ready, at + 1)
                dve.tensor_reduce(chunk_max[:, half, qt, h:h + 1], a_ps[bank][:, 0:b - a], AX.X,
                                  ALU.max).then_inc(ring_free, 1)

            def split_maxima(it, taken):
                link = chain(dve, m_step, 4 * it)
                dve.wait_ge(ring_free, taken + 2)
                m, rest = max_rest[:, 0, :, :], max_rest[:, 1, :, :]
                link(dve.tensor_tensor(m, chunk_max[:, 0, :, :], chunk_max[:, 1, :, :], ALU.max))
                link(dve.tensor_scalar(max_part[:, :, 0:G], m, -1.0, None, ALU.mult))
                link(dve.scalar_tensor_tensor(out=rest, in0=m, scalar=-1.0, in1=max_part[:, :, 0:G],
                                              op0=ALU.mult, op1=ALU.subtract))
                link(dve.tensor_copy(max_part[:, :, G:2 * G], rest))
                dve.tensor_tensor(max_part[:, :, 2 * G:3 * G], rest, max_part[:, :, G:2 * G],
                                  ALU.subtract).then_inc(max_split, 1)

            def take_rows(it, at, bank, first=False):
                dve.wait_ge(ring_ready, at + 1)
                if not first:
                    dve.wait_ge(rows_in, 48 * it)
                dve.tensor_copy(max_rows[:, :, :], rows_ps[bank]).then_inc(rows_taken, 1)
                dve.wait_ge(rows_taken, it + 1)
                dve.sem_inc(ring_free, 1)

            def take_context(it, static, at, bank):
                link = chain(dve, c_step, it)
                dve.wait_ge(ring_ready, at + 1)
                dve.wait_ge(ring_free, at + 2)
                heads = turned[bank].rearrange("p q (h v) -> p q h v", h=G)
                link(dve.reciprocal(r_den[:, :, :], heads[:, :, :, HD]))
                g = static % NG
                block_at = (it - g) * (QT // NG)
                dve.tensor_tensor(s.ctx[:, ds(block_at, QT), G * HD * g:G * HD * (g + 1)].rearrange("p q (h d) -> p q h d", h=G),
                                  heads[:, :, :, 0:HD], r_den[:, :, :].unsqueeze(3).broadcast_to([P, QT, G, HD]),
                                  ALU.mult).then_inc(ring_free, 1)

            def iteration(it, static):
                base, even = ring_base(it, static), ring_base(static, static)
                entries = ring_entries(it, static)
                for k, (kind, what) in enumerate(entries):
                    if kind == "chunk":
                        take_chunk(what, base + k, (even + k) % 2)
                    elif kind == "rows":
                        take_rows(what, base + k, (even + k) % 2)
                    else:
                        take_context(what, static - 1, base + k, (even + k) % 2)
                if static + 2 < NIT:
                    split_maxima(it + 2, base + len(entries))

            for it in range(2):
                for c in range(NCH):
                    take_chunk(c, (NCH + 1) * it + c, ((NCH + 1) * it + c) % 2)
                split_maxima(it, (NCH + 1) * it + NCH)
                if it == 0:
                    take_rows(0, NCH, NCH % 2, first=True)
            run(dve, iteration)
            end = ring_base(NIT, NIT)
            take_context(NIT - 1, NIT - 1, end, end % 2)


def cross_output(nc, s):
    with ExitStack() as ctx:
        def sb(name, shape, dt=F32):
            return ctx.enter_context(nc.sbuf_tensor(name, shape, dt))

        def sem(name):
            return ctx.enter_context(nc.semaphore(name))

        turned_sb = sb("ctxT_sb", [P, 2, KD, P])
        stats = sb("stats2", [P, NT, 6])
        mv = sb("mv2", [P, NT, 2])
        scale = sb("scale2", [P, 2, NT])
        turned = [ctx.enter_context(nc.psum_tensor(f"ctxT{i}", [P, KD, P], F32)) for i in range(2)]
        y = [ctx.enter_context(nc.psum_tensor(f"y2{i}", [P, D], F32)) for i in range(2)]
        banks = [ctx.enter_context(nc.psum_tensor(f"x2T{i}", [P, 4, P], F32)) for i in range(2)]
        turned_ready = sem("co_turned")
        turned_taken = sem("co_taken")
        y_ready = sem("co_y")
        z_ready = sem("co_z")
        step = sem("co_step")
        norm_step = sem("co_norm_step")
        var_ready = sem("var_ready2")
        scale_ready = sem("scale_ready2")
        x2_ready, x2T_ready, x2T_taken = sem("x2_ready"), sem("x2T_ready"), sem("x2T_taken")
        block = ctx.enter_context(nc.Block())

        @block.sync
        def _(sp):
            for dst, src in ((s.gate_sb, s.gate_w), (s.sg_sb, s.s_gate), (s.su_sb, s.s_up), (s.sd_sb, s.s_down)):
                sp.dma_start(dst[:, :, :], src).then_inc(s.r_loaded, 16)
            sp.wait_ge(s.r_loaded, 64)

        @block.tensor
        def _(pe):
            for t in range(NT + 1):
                if t < NT:
                    if t >= 2:
                        pe.wait_ge(turned_taken, t - 1)
                    for k in range(KD):
                        mm = pe.transpose(turned[t % 2][:, k, :], s.ctx[:, t, k * P:(k + 1) * P], s.ident[:, :])
                    mm.then_inc(turned_ready, 1)
                if t:
                    u = t - 1
                    pe.wait_ge(turned_taken, u + 1)
                    if u >= 2:
                        pe.wait_ge(z_ready, u - 1)
                    for k in range(KD):
                        mm = pe.matmul(y[u % 2][:, :], turned_sb[:, u % 2, k, :], s.w_out[:, k, :], start=(k == 0), stop=(k == KD - 1))
                    mm.then_inc(y_ready, 1)
            transpose_tiles(pe, s.act, s.ident, banks, x2_ready, x2T_ready, x2T_taken)

        @block.scalar
        def _(act):
            for t in range(NT):
                act.wait_ge(turned_ready, t + 1)
                if t >= 2:
                    act.wait_ge(y_ready, t - 1)
                act.copy(turned_sb[:, t % 2, :, :], turned[t % 2][:, :, :]).then_inc(turned_taken, 1)
            take_tiles(act, s.actT, banks, x2T_ready, x2T_taken)

        @block.gpsimd
        def _(pool):
            link = chain(pool, norm_step)
            for n in range(NB):
                tiles = slice(QT * n, QT * (n + 1))
                pool.wait_ge(var_ready, QT * (n + 1))
                norm_scale(pool, link, norm_consts(s, QT), mv[:, tiles, 1], scale[:, 0, tiles], scale[:, 1, tiles]).then_inc(scale_ready, 1)

        @block.vector
        def _(dve):
            link = chain(dve, step)

            LAG = QT + 2

            def norm(t):
                dve.wait_ge(scale_ready, t // QT + 1)
                dve.tensor_scalar(s.act[:, t, :], s.act[:, t, :], mv[:, t, 0:1], scale[:, 1, t:t + 1],
                                  ALU.subtract, ALU.mult).then_inc(x2_ready, 1)

            for t in range(NT):
                dve.wait_ge(y_ready, t + 1)
                dve.tensor_tensor(s.act[:, t, :], y[t % 2][:, :], s.act[:, t, :], ALU.add).then_inc(z_ready, 1)
                dve.wait_ge(z_ready, t + 1)
                link(dve.bn_stats(stats[:, t, :], s.act[:, t, :]))
                dve.bn_aggr(mv[:, t, :], stats[:, t, :]).then_inc(var_ready, 1)
                if t >= LAG:
                    norm(t - LAG)
            for t in range(NT - LAG, NT):
                norm(t)


def route(nc, s):
    with ExitStack() as ctx:
        def sb(name, shape, dt=F32):
            return ctx.enter_context(nc.sbuf_tensor(name, shape, dt))

        def ps(name, shape, dt=F32):
            return ctx.enter_context(nc.psum_tensor(name, shape, dt))

        def sem(name):
            return ctx.enter_context(nc.semaphore(name))

        R = 16
        SPREAD = R // CT
        STEP_AT = (2, 5, 8, 10, 13, 16)
        SEARCH = 10
        BITS = SEARCH * (NB - 1) + 1
        assert BITS == 31 and SEARCH == len(STEP_AT) + QT and NT * E == D
        TOP_BIT = 1 << 30
        NONE = 2 * CAP

        gate, sg, su, sd = s.gate_sb, s.sg_sb, s.su_sb, s.sd_sb
        gelu = sb("s_gelu", [P, 2, BLK])
        up = sb("s_up", [P, 2, BLK])
        hidden = sb("s_hidden", [P, ST, BLK])
        down = sb("s_down", [P, QT, D])
        probs = sb("gate_probs", [P, NT, E])
        stat = sb("gate_stat", [P, 2, NT])
        ones = sb("ones_b", [P, P], BF16)
        upto = sb("upto_b", [P, P], BF16)
        spread = sb("spread", [R, SPREAD, P], F16)
        digits_i = sb("digits_i", [P, R], I32)
        digits = sb("digits", [P, R])
        number_i = sb("number_i", [P, NT], I32)
        number = sb("number", [P, NT])
        at_least = sb("at_least", [P, NT, E], BF16)
        bit = sb("bit", [P, E], I32)
        thr = sb("thr", [P, E], I32)
        cand = sb("cand", [P, E], I32)
        inc = sb("inc", [P, E], I32)
        count = sb("count", [P, E])
        above = sb("above", [P, 2, NT, E], BF16)
        need = sb("need", [P, E])
        place = sb("place", [P, NT, E])
        chosen = sb("chosen", [P, NT, E])
        place_i = sb("place_i", [P, NT, E], I32)
        digit_i = sb("digit_i", [P, 2, NT, E], I32)
        low_hot = sb("low_hot", [P, NT, E, R], F16)
        high_hot = sb("high_hot", [P, NT, E, R], F16)
        lists = sb("lists", [R, E, R], F16)
        logit_ps = ps("logit_ps", [P, NT, E])
        count_ps = ps("count_ps", [P, NT, E])
        place_ps = ps("place_ps", [P, 2, NT, E])
        g_ps = [ps(f"g_ps{i}", [P, BLK]) for i in range(2)]
        u_ps = [ps(f"u_ps{i}", [P, BLK]) for i in range(2)]
        y_ps = [ps("y_ps", [P, D])[:, :], logit_ps[:, :, :].rearrange("p t e -> p (t e)")]

        x2_out = sem("x2_out")
        scores_out = sem("scores_out")
        const_step = sem("const_step")
        logits_ready = sem("logits_ready")
        shifted = sem("logits_shifted")
        exp_ready = sem("gate_exp")
        probs_ready = sem("gate_probs_ready")
        compared = sem("compared")
        counted = sem("counted")
        split = sem("split")
        placed = sem("placed")
        low_ready = sem("low_ready")
        lists_taken = sem("lists_taken")
        gu_ready = sem("s_gu_ready")
        gu_taken = sem("s_gu_taken")
        h_ready = sem("s_h_ready")
        y_ready = sem("s_y_ready")
        y_taken = sem("s_y_taken")
        acc_ready = sem("acc_ready")
        acc_out = sem("acc_out")
        tick = sem("r_tick")
        step = sem("r_step")
        search_step = sem("search_step")
        block = ctx.enter_context(nc.Block())
        rows = lambda ap: ap.rearrange("(t p) d -> p t d", p=P)

        @block.sync
        def _(sp):
            sp.dma_start(rows(s.x2)[:, :, 0:D], s.act[:, :, :]).then_inc(x2_out, 16)
            for name in WEIGHTS:
                load_weight(sp, s, name, 0)
            sp.wait_ge(probs_ready, 1)
            sp.dma_start(rows(s.x2)[:, :, D:D + E], probs[:, :, :]).then_inc(scores_out, 16)
            with sp.Fori(0, NB) as n:
                sp.wait_ge(acc_ready, n + 2)
                sp.dma_start(rows(s.acc)[:, ds(QT * n, QT), :], s.act[:, ds(QT * n, QT), :]).then_inc(acc_out, 16)
            sp.wait_ge(acc_out, 16 * NB)
            sp.wait_ge(scores_out, 16)

        @block.gpsimd
        def _(pool):
            link = chain(pool, const_step)
            pool.memset(ones[:, :], 1.0)
            pool.memset(spread[:, :, :], 0.0)
            pool.iota(digits_i[:, :], pattern=[[1, R]], base=0, channel_multiplier=0)
            link(pool.iota(number_i[:, :], pattern=[[P, NT]], base=0, channel_multiplier=1))
            pool.affine_select(out=upto[:, :], in_=ones[:, :], compare_op=ALU.is_ge, fill=0.0, base=0,
                               pattern=[[1, P]], channel_multiplier=-1)
            pool.affine_select(out=spread[:, :, :], in_=spread[:, :, :], compare_op=ALU.not_equal, fill=1.0,
                               base=0, pattern=[[-1, SPREAD], [1, P]], channel_multiplier=-SPREAD)
            pool.tensor_copy(digits[:, :], digits_i[:, :])
            link(pool.tensor_copy(number[:, :], number_i[:, :]))
            pool.sem_inc(h_ready, 2)
            pool.sem_inc(acc_ready, 1)
            with pool.Fori(0, NB) as n:
                for i in range(ST):
                    pool.wait_ge(gu_taken, ST * n + i + 3)
                    pool.tensor_tensor(hidden[:, i, :], gelu[:, i % 2, :], up[:, i % 2, :], ALU.mult).then_inc(h_ready, 1)
                pool.wait_ge(y_taken, QT * n + QT + 2)
                pool.sem_inc(tick, 1)
                pool.wait_ge(x2_out, 16)
                at = s.act[:, ds(QT * n, QT), :]
                pool.tensor_tensor(at, at, down[:, :, :], ALU.add).then_inc(acc_ready, 1)

        @block.tensor
        def _(pe):
            for t in range(NT):
                for k in range(KD):
                    mm = pe.matmul(logit_ps[:, t, :], s.actT[:, k, t * P:(t + 1) * P], gate[:, k, :],
                                   start=(k == 0), stop=(k == KD - 1))
            mm.then_inc(logits_ready, 1)
            pe.wait_ge(const_step, 2)

            def count_step(at):
                pe.wait_ge(compared, at + 1)
                pe.matmul(count_ps[:, :, :], ones[:, :], at_least[:, :, :], start=True, stop=True).then_inc(counted, 1)

            def gate_up(n, i, behind=lambda products: None):
                pe.wait_ge(gu_taken, ST * n + i + 1)
                done = 2 * KD * i
                for out, weight in ((g_ps, sg), (u_ps, su)):
                    for k in range(KD):
                        mm = pe.matmul(out[i % 2][:, :], weight[:, k, i * P:(i + 1) * P],
                                       s.actT[:, k, ds(n * BLK, BLK)], start=(k == 0), stop=(k == KD - 1))
                        done += 1
                        if done == 2 * KD * (i + 1):
                            mm.then_inc(gu_ready, 1)
                        behind(done)

            def down_tile(n, q):
                pe.wait_ge(y_taken, QT * n + q + 1)
                for i in range(ST):
                    pe.wait_ge(h_ready, ST * n + i + 3)
                    mm = pe.matmul(y_ps[q % 2], hidden[:, i, q * P:(q + 1) * P], sd[:, i, :],
                                   start=(i == 0), stop=(i == ST - 1))
                mm.then_inc(y_ready, 1)

            with pe.Fori(0, NB - 1) as n:
                def step_behind(products):
                    if products in STEP_AT:
                        count_step(SEARCH * n + STEP_AT.index(products))

                for i in range(ST):
                    gate_up(n, i, step_behind)
                for q in range(QT):
                    down_tile(n, q)
                    count_step(SEARCH * n + len(STEP_AT) + q)
            count_step(BITS - 1)
            gate_up(NB - 1, 0)

            pe.wait_ge(split, 1)
            for a in range(2):
                pe.matmul(place_ps[:, a, :, :], upto[:, :], above[:, a, :, :], start=True, stop=False)
                for j in range(NT - 1):
                    pe.matmul(place_ps[:, a, j + 1:NT, :], ones[:, :],
                              above[:, a, j:j + 1, :].broadcast_to([P, NT - 1 - j, E]), start=False, stop=(j == NT - 2))
            for j in range(NT):
                mm = pe.matmul(count_ps[:, 0, :], ones[:, :], above[:, 0, j, :], start=(j == 0), stop=(j == NT - 1))
            mm.then_inc(placed, 1)
            for i in range(1, ST):
                gate_up(NB - 1, i)
            for q in range(QT):
                down_tile(NB - 1, q)
            pe.wait_ge(low_ready, 1)
            for e in range(E):
                for j in range(NT):
                    mm = pe.matmul(place_ps[0:R, e // 8, 2 * (e % 8):2 * (e % 8) + 1, :].rearrange("p o r -> p (o r)"),
                                   low_hot[:, j, e, :], high_hot[:, j, e, :], start=(j == 0), stop=(j == NT - 1))
            mm.then_inc(placed, 1)
            pe.wait_ge(lists_taken, 1)
            pe.wait_ge(const_step, 2)
            by_tile = lists[:, :, :].rearrange("p e (c b) -> p (e c) b", b=SPREAD)
            for b in range(SPREAD):
                mm = pe.matmul(count_ps[:, 0:CT, :].rearrange("p c e -> p (c e)"), spread[:, b, :], by_tile[:, :, b],
                               start=(b == 0), stop=(b == SPREAD - 1))
            mm.then_inc(placed, 1)

        @block.scalar
        def _(act):
            act.sem_inc(gu_taken, 2)
            act.sem_inc(y_taken, 2)
            act.wait_ge(shifted, 1)
            act.activation(probs[:, :, :], probs[:, :, :], ACT.Exp).then_inc(exp_ready, 1)
            with act.Fori(0, NB) as n:
                for i in range(ST):
                    act.wait_ge(gu_ready, ST * n + i + 1)
                    act.wait_ge(h_ready, ST * n + i + 1)
                    act.activation(gelu[:, i % 2, :], g_ps[i % 2][:, :], ACT.Gelu)
                    act.copy(up[:, i % 2, :], u_ps[i % 2][:, :]).then_inc(gu_taken, 1)
                act.wait_ge(acc_ready, n + 1)
                for q in range(QT):
                    act.wait_ge(y_ready, QT * n + q + 1)
                    act.copy(down[:, q, :], y_ps[q % 2]).then_inc(y_taken, 1)

        @block.vector
        def _(dve):
            link = chain(dve, step)
            wide = [P, NT, E]

            def over_tiles(ap):
                return ap.unsqueeze(1).broadcast_to(wide)

            dve.memset(thr[:, :], 0)
            dve.memset(bit[:, :], TOP_BIT)
            link(dve.memset(cand[:, :], TOP_BIT))
            dve.wait_ge(logits_ready, 1)
            link(dve.tensor_reduce(stat[:, 0, :], logit_ps[:, :, :], AX.X, ALU.max))
            dve.tensor_tensor(probs[:, :, :], logit_ps[:, :, :], stat[:, 0, :].unsqueeze(2).broadcast_to(wide),
                              ALU.subtract).then_inc(shifted, 1)
            dve.wait_ge(exp_ready, 1)
            link(dve.tensor_reduce(stat[:, 0, :], probs[:, :, :], AX.X, ALU.add))
            link(dve.reciprocal(stat[:, 1, :], stat[:, 0, :]))
            dve.tensor_tensor(probs[:, :, :], probs[:, :, :], stat[:, 1, :].unsqueeze(2).broadcast_to(wide),
                              ALU.mult).then_inc(probs_ready, 1)
            dve.wait_ge(probs_ready, 1)

            def search(at):
                found = chain(dve, search_step, 5 * at)
                dve.tensor_tensor(at_least[:, :, :], probs[:, :, :], over_tiles(cand[:, :].bitcast(F32)),
                                  ALU.is_ge).then_inc(compared, 1)
                dve.wait_ge(counted, at + 1)
                found(dve.tensor_reduce(count[:, :], count_ps[:, :, :].rearrange("p t e -> p e t"), AX.X, ALU.add))
                found(dve.scalar_tensor_tensor(out=inc[:, :], in0=count[:, :], scalar=float(CAP), in1=bit[:, :],
                                               op0=ALU.is_ge, op1=ALU.mult))
                found(dve.tensor_tensor(thr[:, :], thr[:, :], inc[:, :], ALU.bitwise_or))
                found(dve.tensor_scalar(bit[:, :], bit[:, :], 1, None, ALU.logical_shift_right))
                found(dve.tensor_tensor(cand[:, :], thr[:, :], bit[:, :], ALU.bitwise_or))

            with dve.Fori(0, NB - 1) as n:
                for k in range(SEARCH):
                    search(SEARCH * n + k)
            search(BITS - 1)

            limit = over_tiles(thr[:, :].bitcast(F32))
            dve.tensor_tensor(above[:, 0, :, :], probs[:, :, :], limit, ALU.is_gt)
            dve.tensor_tensor(above[:, 1, :, :], probs[:, :, :], limit, ALU.is_equal).then_inc(split, 1)
            dve.wait_ge(placed, 1)
            link(dve.tensor_scalar(need[:, :], count_ps[:, 0, :], -1.0, float(CAP), ALU.mult, ALU.add))
            up_to_need = over_tiles(need[:, :])
            link(dve.tensor_tensor(chosen[:, :, :], place_ps[:, 1, :, :], up_to_need, ALU.is_le))
            link(dve.tensor_tensor(chosen[:, :, :], chosen[:, :, :], above[:, 1, :, :], ALU.mult))
            link(dve.tensor_tensor(chosen[:, :, :], chosen[:, :, :], above[:, 0, :, :], ALU.add))
            link(dve.tensor_tensor(place[:, :, :], place_ps[:, 1, :, :], up_to_need, ALU.min))
            link(dve.tensor_tensor(place[:, :, :], place_ps[:, 0, :, :], place[:, :, :], ALU.add))
            link(dve.scalar_tensor_tensor(out=place[:, :, :], in0=place[:, :, :], scalar=-1.0 - NONE, in1=chosen[:, :, :],
                                          op0=ALU.add, op1=ALU.mult))
            link(dve.tensor_scalar(place_i[:, :, :], place[:, :, :], float(NONE), None, ALU.add))
            link(dve.tensor_scalar(digit_i[:, 0, :, :], place_i[:, :, :], R - 1, None, ALU.bitwise_and))
            link(dve.tensor_scalar(digit_i[:, 1, :, :], place_i[:, :, :], R.bit_length() - 1, None, ALU.logical_shift_right))
            dve.wait_ge(const_step, 2)
            hot = [P, NT * E, R]
            flat = lambda tile: tile.rearrange("p t e r -> p (t e) r")
            for a, out in ((1, high_hot), (0, low_hot)):
                link(dve.tensor_tensor(flat(out[:, :, :, :]),
                                       digit_i[:, a, :, :].rearrange("p t e -> p (t e)").unsqueeze(2).broadcast_to(hot),
                                       digits[:, :].unsqueeze(1).broadcast_to(hot), ALU.is_equal))
            high = high_hot[:, :, :, :].rearrange("p t e r -> p t (e r)")
            dve.tensor_tensor(high, high, number[:, :].unsqueeze(2).broadcast_to([P, NT, E * R]),
                              ALU.mult).then_inc(low_ready, 1)
            dve.wait_ge(placed, 2)
            for half in range(2):
                ins = dve.tensor_copy(lists[:, 8 * half:8 * (half + 1), :],
                                      place_ps[0:R, half, :, :].rearrange("p (e o) r -> p e o r", o=2)[:, :, 0, :])
            ins.then_inc(lists_taken, 1)
            dve.wait_ge(placed, 3)
            dve.tensor_copy(s.token[:, :, :], count_ps[:, 0:CT, :].rearrange("p c e -> p (c e)").rearrange("p (e c) -> p c e", c=CT))


WEIGHTS = ("gate", "up", "down")


def load_weight(sp, s, name, e):
    sp.dma_start(s.w_raw[name][:, :], s.w_dram[name][ds(e, 1)].rearrange("o p k n -> p (o k n)")).then_inc(s.w_loaded[name], 16)


def experts(nc, s):
    with ExitStack() as ctx:
        def sb(name, shape, dt=F32):
            return ctx.enter_context(nc.sbuf_tensor(name, shape, dt))

        def ps(name, shape, dt=F32):
            return ctx.enter_context(nc.psum_tensor(name, shape, dt))

        def sem(name):
            return ctx.enter_context(nc.semaphore(name))

        WORDS = KD * FI
        assert WORDS == FT * D
        W_PIECES = 4
        PIECE = WORDS // W_PIECES
        W_ALL = W_PIECES * len(WEIGHTS)
        WITH_TILE = (1, 1, 1, 0, 1, 1, 1, 0)

        load_numbers = sb("load_numbers", [P, 2, CT], U32)
        store_numbers = sb("store_numbers", [P, CT], U32)
        xg = sb("xg", [P, 2, CT, D + E])
        xgT = sb("xgT", [P, 2, 2, KD, CAP], F32R)
        gelu = sb("e_gelu", [P, 2, CAP])
        product = sb("e_product", [P, 2, CAP])
        hidden = sb("e_hidden", [P, 2, FT, CAP], F32R)
        rows_out = sb("rows_out", [P, 2, CT, D])
        w_parts = {n: sb(f"w_parts_{n}", [P, 2, 2, WORDS], F32R) for n in WEIGHTS}
        all_stats = sb("all_stats3", [P, NT, 6])
        mvs = sb("mvs3", [P, NT, 2])
        scale = sb("scale3", [P, 2, NT])
        x_ps = ps("xg_ps", [P, KD, CAP])
        gu_ps = [ps(f"gu_ps{i}", [P, 2, CAP]) for i in range(4)]
        d_ps = [ps(f"d_ps{i}", [P, CT, D]) for i in range(2)]

        numbers_ready = sem("numbers_ready")
        gathered = [sem(f"gathered{p}") for p in range(2)]
        xT_ready = sem("xgT_ready")
        x_high = sem("x_high")
        x_low = sem("x_low")
        w_high = sem("w_high")
        w_low = sem("w_low")
        gu_ready = sem("gu_ready")
        g_taken = sem("g_taken")
        h_ready = sem("h_ready")
        h_high = sem("h_high")
        h_low = sem("h_low")
        d_ready = sem("d_ready")
        out_ready = sem("out_ready")
        tick = sem("tick")
        added = sem("added")
        rows_out_free = sem("rows_out_free")
        back = [sem(f"rows_back{i}") for i in range(NB)]
        step = sem("n3_step")
        norm_step = sem("n3_norm_step")
        var_ready = sem("var_ready3")
        scale_ready = sem("scale_ready3")
        normed = sem("normed")
        stored = sem("stored")
        block = ctx.enter_context(nc.Block())
        rows = lambda ap: ap.rearrange("(t p) d -> p t d", p=P)

        def split_pieces(e, p, first, last, split):
            for n in range(first, last):
                name, c = WEIGHTS[n // W_PIECES], slice(n % W_PIECES * PIECE, (n % W_PIECES + 1) * PIECE)
                split(name, W_ALL * e + n, s.w_raw[name][:, c], w_parts[name][:, p, 0, c], w_parts[name][:, p, 1, c])

        @block.sync
        def _(sp):
            with sp.Fori(1, E) as e:
                for n, name in enumerate(WEIGHTS):
                    sp.wait_ge(w_low, W_ALL * (e - 1) + W_PIECES * (n + 1))
                    load_weight(sp, s, name, e)
            sp.wait_ge(added, 16 * CT * E)
            for n in range(NB):
                sp.dma_start(s.act[:, QT * n:QT * (n + 1), :], rows(s.acc)[:, QT * n:QT * (n + 1), :]).then_inc(back[n], 16)
            for n in range(NB):
                sp.wait_ge(normed, QT * (n + 1))
                sp.dma_start(rows(s.out)[:, QT * n:QT * (n + 1), :], s.act[:, QT * n:QT * (n + 1), :]).then_inc(stored, 16)
            sp.wait_ge(stored, 16 * NB)

        @block.gpsimd
        def _(pool):
            def numbers(e, out):
                pool.tensor_copy(out, s.token[:, :, ds(e, 1)].rearrange("p c o -> p (c o)")).then_inc(numbers_ready, 1)

            def gather(e, p, copies):
                numbers(e, load_numbers[:, p, :])
                pool.wait_ge(numbers_ready, copies + 1)
                pool.sem_inc(tick, 1)
                for c in range(CT):
                    pool.indirect_dma_start(out=xg[:, p, c, :], out_offset=None, in_=s.x2,
                                            in_offset=bass.IndirectOffsetOnAxis(ap=load_numbers[:, p, c:c + 1], axis=0)).then_inc(gathered[p], 16)

            def scatter(e, p, copies, first=False):
                pool.wait_ge(out_ready, e + 3)
                if not first:
                    pool.wait_ge(added, 16 * CT * e)
                pool.sem_inc(rows_out_free, 1)
                numbers(e, store_numbers[:, :])
                pool.wait_ge(numbers_ready, copies + 1)
                pool.sem_inc(tick, 1)
                for c in range(CT):
                    pool.indirect_dma_start(out=s.acc, out_offset=bass.IndirectOffsetOnAxis(ap=store_numbers[:, c:c + 1], axis=0),
                                            in_=rows_out[:, p, c, :], in_offset=None, compute_op=ALU.add).then_inc(added, 16)

            def expert(pair, p, first=False):
                e = 2 * pair + p
                pool.wait_ge(gathered[p], 16 * CT * pair)
                pool.wait_ge(xT_ready, e - 1)
                pool.wait_ge(out_ready, e + 1)
                gather(e, p, 2 * e - 2)
                scatter(e - 2, p, 2 * e - 1, first)

            pool.sem_inc(rows_out_free, 1)
            gather(0, 0, 0)
            gather(1, 1, 1)
            expert(1, 0, first=True)
            expert(1, 1)
            with pool.Fori(2, E // 2) as pair:
                for p in range(2):
                    expert(pair, p)
            scatter(E - 2, 0, 2 * E - 2)
            scatter(E - 1, 1, 2 * E - 1)
            link = chain(pool, norm_step)
            for n in range(NB):
                part = slice(QT * n, QT * (n + 1))
                pool.wait_ge(var_ready, n + 1)
                norm_scale(pool, link, norm_consts(s, QT), mvs[:, part, 1], scale[:, 0, part], scale[:, 1, part]).then_inc(scale_ready, 1)

        @block.tensor
        def _(pe):
            def turn_rows(pair, p):
                e = 2 * pair + p
                pe.wait_ge(gathered[p], 16 * CT * (pair + 1))
                pe.wait_ge(x_low, e + 1)
                for c in range(CT):
                    for k in range(KD):
                        mm = pe.transpose(x_ps[:, k, c * P:(c + 1) * P], xg[:, p, c, k * P:(k + 1) * P], s.ident[:, :])
                mm.then_inc(xT_ready, 1)

            def gate_up(pair, p):
                e = 2 * pair + p
                pe.wait_ge(x_low, e + 2)
                pe.wait_ge(w_low, W_ALL * e + 2 * W_PIECES)
                for i in range(FT):
                    pe.wait_ge(h_ready, FT * e + i + 1)
                    for a, name in enumerate(("gate", "up")):
                        for k in range(KD):
                            at = k * FI + i * P
                            mm = products(pe, gu_ps[i % 4][:, a, :], both(lambda c: w_parts[name][:, p, c, at:at + P]),
                                          both(lambda c: xgT[:, p, c, k, :]), start=(k == 0), stop=(k == KD - 1))
                    mm.then_inc(gu_ready, 1)

            def down(pair, p):
                e = 2 * pair + p
                pe.wait_ge(w_low, W_ALL * (e + 1))
                pe.wait_ge(out_ready, e + 1)
                for c in range(CT):
                    for i in range(FT):
                        if c == 0:
                            pe.wait_ge(h_low, FT * e + i + 3)
                        mm = products(pe, d_ps[p][:, c, :], both(lambda a: hidden[:, a, i, c * P:(c + 1) * P]),
                                      both(lambda a: w_parts["down"][:, p, a, i * D:(i + 1) * D]),
                                      start=(i == 0), stop=(i == FT - 1))
                mm.then_inc(d_ready, 1)

            def expert(pair, p, last=False):
                gate_up(pair, p)
                if not last:
                    turn_rows(pair + p, 1 - p)
                down(pair, p)

            pe.sem_inc(d_ready, 1)
            turn_rows(0, 0)
            with pe.Fori(0, E // 2 - 1) as pair:
                for p in range(2):
                    expert(pair, p)
            expert(E // 2 - 1, 0)
            expert(E // 2 - 1, 1, last=True)

        @block.scalar
        def _(act):
            def split_rows(e, p):
                act.wait_ge(xT_ready, e + 1)
                act.copy(xgT[:, p, 0, :, :], x_ps[:, :, :]).then_inc(x_high, 1)

            def split(name, n, raw, high, low):
                act.copy(high, raw).then_inc(w_high, 1)

            def split_weights(e, p, first, last):
                for n in range(first, last):
                    if n % W_PIECES == 0:
                        act.wait_ge(s.w_loaded[WEIGHTS[n // W_PIECES]], 16 * (e + 1))
                    if n == 2 * W_PIECES:
                        act.wait_ge(d_ready, e)
                    split_pieces(e, p, n, n + 1, split)

            def high(e, i):
                act.wait_ge(h_ready, FT * e + i + 5)
                act.copy(hidden[:, 0, i, :], product[:, i % 2, :]).then_inc(h_high, 1)

            def expert(pair, p, last=False):
                e = 2 * pair + p
                n = 0
                for i in range(FT):
                    act.wait_ge(gu_ready, FT * e + i + 1)
                    act.wait_ge(h_ready, FT * e + i + 3)
                    act.activation(gelu[:, i % 2, :], gu_ps[i % 4][:, 0, :], ACT.Gelu).then_inc(g_taken, 1)
                    if i:
                        high(e, i - 1)
                    if not last:
                        split_weights(e + 1, 1 - p, n, n + WITH_TILE[i])
                        n += WITH_TILE[i]
                high(e, FT - 1)
                if not last:
                    split_rows(e + 1, 1 - p)
                    split_weights(e + 1, 1 - p, n, W_ALL)

            for n in range(W_ALL):
                if n % W_PIECES == 0:
                    act.wait_ge(s.w_loaded[WEIGHTS[n // W_PIECES]], 16)
                split_pieces(0, 0, n, n + 1, split)
                if n == W_PIECES:
                    split_rows(0, 0)
            with act.Fori(0, E // 2 - 1) as pair:
                for p in range(2):
                    expert(pair, p)
            expert(E // 2 - 1, 0)
            expert(E // 2 - 1, 1, last=True)

        @block.vector
        def _(dve):
            dve.sem_inc(h_ready, 4)
            dve.sem_inc(out_ready, 2)
            dve.sem_inc(x_low, 1)
            dve.sem_inc(h_low, 2)

            def split_rows(e, p):
                dve.wait_ge(x_high, e + 1)
                dve.tensor_tensor(xgT[:, p, 1, :, :], x_ps[:, :, :], xgT[:, p, 0, :, :].bitcast(F32),
                                  ALU.subtract).then_inc(x_low, 1)

            def split(name, n, raw, high, low):
                dve.wait_ge(w_high, n + 1)
                dve.tensor_tensor(low, raw, high.bitcast(F32), ALU.subtract).then_inc(w_low, 1)

            def low(e, i):
                dve.wait_ge(h_high, FT * e + i + 1)
                dve.tensor_tensor(hidden[:, 1, i, :], product[:, i % 2, :], hidden[:, 0, i, :].bitcast(F32),
                                  ALU.subtract).then_inc(h_low, 1)

            def scale_rows(pair, p):
                e = 2 * pair + p
                dve.wait_ge(rows_out_free, e + 1)
                dve.wait_ge(d_ready, e + 2)
                for c in range(CT):
                    ins = dve.tensor_scalar(rows_out[:, p, c, :], d_ps[p][:, c, :],
                                            xg[:, p, c, ds(e + D, 1)], None, ALU.mult)
                ins.then_inc(out_ready, 1)

            def expert(pair, p, last=False):
                e = 2 * pair + p
                n = 0
                for i in range(FT):
                    dve.wait_ge(g_taken, FT * e + i + 1)
                    dve.wait_ge(h_low, FT * e + i + 1)
                    dve.tensor_tensor(product[:, i % 2, :], gelu[:, i % 2, :], gu_ps[i % 4][:, 1, :],
                                      ALU.mult).then_inc(h_ready, 1)
                    if i:
                        low(e, i - 1)
                    if not last:
                        split_pieces(e + 1, 1 - p, n, n + WITH_TILE[i], split)
                        n += WITH_TILE[i]
                low(e, FT - 1)
                if not last:
                    split_rows(e + 1, 1 - p)
                    split_pieces(e + 1, 1 - p, n, W_ALL, split)
                scale_rows(pair, p)

            for n in range(W_ALL):
                split_pieces(0, 0, n, n + 1, split)
                if n == W_PIECES:
                    split_rows(0, 0)
            with dve.Fori(0, E // 2 - 1) as pair:
                for p in range(2):
                    expert(pair, p)
            expert(E // 2 - 1, 0)
            expert(E // 2 - 1, 1, last=True)

            def norm(n):
                dve.wait_ge(scale_ready, n + 1)
                for t in range(QT * n, QT * (n + 1)):
                    dve.tensor_scalar(s.act[:, t, :], s.act[:, t, :], mvs[:, t, 0:1], scale[:, 1, t:t + 1],
                                      ALU.subtract, ALU.mult).then_inc(normed, 1)

            link = chain(dve, step)
            for n in range(NB):
                tiles = range(QT * n, QT * (n + 1))
                dve.wait_ge(back[n], 16)
                for t in tiles:
                    last = dve.bn_stats(all_stats[:, t, :], s.act[:, t, :])
                link(last)
                for t in tiles:
                    last = dve.bn_aggr(mvs[:, t, :], all_stats[:, t, :])
                last.then_inc(var_ready, 1)
                if n:
                    norm(n - 1)
            norm(NB - 1)


def program(nc, arg):
    s = Shared()
    s.xT, s.ctxT, s.x, s.mask = arg["xT"], arg["ctxT"], arg["x"], arg["mask"]
    s.w_q, s.w_k, s.w_v, s.w_o = arg["wq"], arg["wk"], arg["wv"], arg["wo"]
    s.w_cq, s.w_ck, s.w_cv, s.w_co = arg["cwq"], arg["cwk"], arg["cwv"], arg["cwo"]
    s.b = {"q": arg["bq"], "k": arg["bk"], "v": arg["bv"], "o": arg["bo"],
           "cq": arg["cbq"], "ck": arg["cbk"], "cv": arg["cbv"], "co": arg["cbo"]}
    s.gate_w, s.out = arg["gate"], arg["out"]
    s.w_dram = {"gate": arg["wg"], "up": arg["wu"], "down": arg["wd"]}
    s.s_gate, s.s_up, s.s_down = arg["sg"], arg["su"], arg["sd"]

    def dram(name, shape, dt=F32):
        return nc.dram_tensor(name, shape, dt, kind="Internal").ap()

    s.k_parts = dram("k_parts", (3, D, S2), BF16)
    s.q_parts = dram("q_parts", (3, D, T), BF16)
    s.mask_parts = dram("mask_parts", (6, S2), BF16)
    s.x2 = dram("x2_rows", (T, D + E))
    s.acc = dram("acc_rows", (T, D))
    with ExitStack() as ctx:
        def sb(name, shape, dt=F32):
            return ctx.enter_context(nc.sbuf_tensor(name, shape, dt))

        s.consts = ctx.enter_context(nc.semaphore("consts"))
        s.ident = sb("ident", [P, P])
        s.norm_consts = sb("norm_consts", [P, 3, QT])
        s.ident_b = sb("ident_b", [P, P], BF16)
        s.act = sb("activations", [P, NT, D])
        s.actT = sb("activationsT", [P, KD, T])
        s.qT = s.actT
        s.w_out = sb("w_out", [P, KD, D])
        s.b_co_row = sb("b_co_row", [P, D])
        with ExitStack() as attention:
            s.cv = attention.enter_context(nc.sbuf_tensor("cv", [P, NKT, H, VW], F32))
            s.k_stack_space = [attention.enter_context(nc.sbuf_tensor("k_stack0", [P, H // 2 * S2], BF16))]
            s.w_cq_sb = attention.enter_context(nc.sbuf_tensor("w_cq", [P, KD, D], F32))
            s.b_cq_sb = attention.enter_context(nc.sbuf_tensor("b_cq", [P, KD], F32))
            s.k_stack = [s.k_stack_space[0][:, :].rearrange("p (h n) -> p h n", n=S2), None]
            with ExitStack() as first:
                s.kT = first.enter_context(nc.sbuf_tensor("kT", [P, 2, KD, T], F32R))
                s.v = first.enter_context(nc.sbuf_tensor("v", [P, 2, NT, D], F32R))
                project_inputs(nc, s)
                self_attention(nc, s)
            cross_attention(nc, s)
        s.w_raw = {n: sb(f"w_raw_{n}", [P, KD * FI]) for n in WEIGHTS}
        s.gate_sb = sb("gate", [P, KD, E])
        s.sg_sb, s.su_sb = sb("s_gate", [P, KD, FS]), sb("s_up_w", [P, KD, FS])
        s.sd_sb = sb("s_down_w", [P, ST, D])
        s.token = sb("token", [P, CT, E], U32)
        s.w_loaded = {n: ctx.enter_context(nc.semaphore(f"w_{n}")) for n in WEIGHTS}
        s.r_loaded = ctx.enter_context(nc.semaphore("r_loaded"))
        cross_output(nc, s)
        route(nc, s)
        experts(nc, s)


def kernel(**inputs):
    import numpy as np
    import concourse.bacc as bacc
    from concourse.bass_utils import run_bass_kernel_spmd

    arrays = layout(np, inputs)
    nc = bacc.Bacc("TRN2", target_bir_lowering=False, num_devices=1)
    arg = {n: nc.dram_tensor(f"in_{n}", a.shape, mybir.dt.from_np(a.dtype), kind="ExternalInput").ap()
           for n, a in arrays.items()}
    arg["out"] = nc.dram_tensor("out_0", (T, D), F32, kind="ExternalOutput").ap()
    program(nc, arg)
    r = run_bass_kernel_spmd(nc, [{f"in_{n}": a for n, a in arrays.items()}], core_ids=[0])
    return r.results[0]["out_0"].reshape(1, T, D)


def layout(np, inputs):
    a = {n: np.asarray(v) for n, v in inputs.items()}

    def cut(m):
        m = m.reshape(*m.shape[:-2], m.shape[-2] // P, P, m.shape[-1])
        return np.ascontiguousarray(np.swapaxes(m, -3, -2))

    def turned(m):
        return cut(np.swapaxes(m, -1, -2))

    def column(v):
        return np.ascontiguousarray(v.reshape(KD, P).T)

    out = {"x": cut(a["x"][0]), "xT": turned(a["x"][0]), "ctxT": turned(a["ctx_1024"][0]),
           "mask": np.ascontiguousarray(a["mask_BxS2_if1"][0])}
    for n, k in (("q", "q"), ("k", "k"), ("v", "v"), ("o", "o")):
        out["w" + n] = turned(a[f"L0_attn_W{k}"])
        out["cw" + n] = turned(a[f"L0_xattn_W_{k}"])
        out["b" + n] = a[f"L0_attn_b{k}"]
        out["cb" + n] = a[f"L0_xattn_b_{k}"]
        if n in "qkv":
            out["b" + n] = column(out["b" + n])
        if n in "qk":
            out["cb" + n] = column(out["cb" + n])
    out["gate"] = turned(a["L0_ffn_gate_w"])
    for n, k in (("wg", "Wg"), ("wu", "Wu"), ("wd", "Wd"), ("sg", "Sg"), ("su", "Su"), ("sd", "Sd")):
        out[n] = turned(a[f"L0_ffn_{k}"])
    return out
```
